# Optimizing a Trainium2 kernel written in Bass

```python
import numpy as np
import jax
import jax.numpy as jnp

def _softmax(x, axis=-1):
    return jax.nn.softmax(x, axis=axis)

def _gelu(x):
    return jax.nn.gelu(x, approximate=True)

def _silu(x):
    return jax.nn.silu(x)

def _sigmoid(x):
    return jax.nn.sigmoid(x)

def _layernorm(x, axis=-1, eps=1e-05):
    m = jnp.mean(x, axis=axis, keepdims=True)
    v = jnp.var(x, axis=axis, keepdims=True)
    return (x - m) / jnp.sqrt(v + eps)

def _scatter_add(tgt, idx, src, axis=0):
    return tgt.at[idx].add(src)

def _segment_sum(src, seg, n):
    return jax.ops.segment_sum(src, seg, n)
kernel_name = 'mk_lm_tower_d1_tok_ids768_r4_5d4cfe'

def setup_inputs(seed: int=0):
    np.random.seed(seed)
    _w = jnp.asarray

    def _rec_inputs():
        import jax
        import jax.numpy as jnp
        _rk = jax.random.key(seed)
        x = jax.random.randint(jax.random.fold_in(_rk, 1), (16, 128), 0, 30522, jnp.int32)
        mask_BS_i1_0 = jnp.where(jnp.ones((16, 128), dtype=bool), 1, 0).astype(jnp.int32)
        pos_BS = jnp.broadcast_to(jnp.arange(128, dtype=jnp.int32), (16, 128))
        return (x, mask_BS_i1_0, pos_BS)
    x, mask_BS_i1_0, pos_BS = _rec_inputs()

    def _L0_tok_setup():
        import jax, jax.numpy as jnp
        import numpy as np
        VOCAB = 30522
        MAX_POS = 128
        TYPE_VOCAB = 2
        HIDDEN = 192
        EPS = 1e-12
        key = jax.random.key(seed)
        k1, k2, k3, k4, k5, k6, k7 = jax.random.split(key, 7)
        B, S = (64, 128)
        input_ids = jax.random.randint(k1, (B, S), 0, VOCAB, dtype=jnp.int32)
        token_type_ids = jax.random.randint(k2, (B, S), 0, TYPE_VOCAB, dtype=jnp.int32)
        position_ids = jnp.broadcast_to(jnp.arange(S, dtype=jnp.int32), (B, S))
        word_emb = jax.random.normal(k3, (VOCAB, HIDDEN), dtype=jnp.float32) * 0.02
        pos_emb = jax.random.normal(k4, (MAX_POS, HIDDEN), dtype=jnp.float32) * 0.02
        type_emb = jax.random.normal(k5, (TYPE_VOCAB, HIDDEN), dtype=jnp.float32) * 0.02
        gamma = jnp.ones((HIDDEN,), dtype=jnp.float32) + 0.01 * jax.random.normal(k6, (HIDDEN,), dtype=jnp.float32)
        beta = 0.01 * jax.random.normal(k7, (HIDDEN,), dtype=jnp.float32)
        return {'input_ids': input_ids, 'token_type_ids': token_type_ids, 'position_ids': position_ids, 'word_emb': word_emb, 'pos_emb': pos_emb, 'type_emb': type_emb, 'gamma': gamma, 'beta': beta}
    _L0_tok_all = _L0_tok_setup()
    _L0_tok_in = {k: v for k, v in _L0_tok_all.items() if k in ('word_emb', 'pos_emb', 'type_emb', 'gamma', 'beta')}
    del _L0_tok_all

    def _L0_attn_setup():
        import jax, jax.numpy as jnp
        import numpy as np
        import math
        H = 12
        LOGIT_SCALE_MAX = math.log(1.0 / 0.01)

        def _normalize(t, eps=1e-12):
            n = jnp.linalg.norm(t, axis=-1, keepdims=True)
            return t / jnp.maximum(n, eps)
        key = jax.random.key(seed)
        ks = jax.random.split(key, 4)
        L, N, C = (256, 8, 192)
        scale = (C // H) ** (-0.5)
        return {'x': jax.random.normal(ks[0], (L, N, C), jnp.float32), 'in_proj_weight': jax.random.normal(ks[1], (3 * C, C), jnp.float32) * scale, 'in_proj_bias': jnp.zeros((3 * C,), jnp.float32), 'logit_scale': jnp.full((H, 1, 1), jnp.log(10.0), jnp.float32), 'head_scale': jnp.ones((H, 1, 1), jnp.float32), 'out_w': jax.random.normal(ks[2], (C, C), jnp.float32) * scale, 'out_b': jnp.zeros((C,), jnp.float32)}
    _L0_attn_all = _L0_attn_setup()
    _L0_attn_in = {k: v for k, v in _L0_attn_all.items() if k in ('in_proj_weight', 'in_proj_bias', 'logit_scale', 'head_scale', 'out_w', 'out_b')}
    del _L0_attn_all

    def _L0_ffn_setup():
        import jax, jax.numpy as jnp
        import numpy as np
        import math
        B, T, C = (8, 512, 192)
        E = 3
        HD = C // E
        TOPK = 2
        NGLOB = 4

        def _masked_softmax(att, mask):
            att = jnp.where(mask, -jnp.inf, att)
            return jax.nn.softmax(att, axis=-1)
        key = jax.random.key(seed)
        ks = jax.random.split(key, 16)
        s = 0.02
        return {'x': jax.random.normal(ks[0], (B, T, C), jnp.float32), 'Wqk': jax.random.normal(ks[1], (C, 2 * C), jnp.float32) * s, 'bqk': jnp.zeros((2 * C,), jnp.float32), 'Wv': jax.random.normal(ks[2], (E, C, HD), jnp.float32) * s, 'bv': jnp.zeros((E, HD), jnp.float32), 'conv_w': jax.random.normal(ks[3], (HD, 1, 3), jnp.float32) * s, 'conv_b': jnp.zeros((HD,), jnp.float32), 'glob': jax.random.normal(ks[4], (NGLOB, HD), jnp.float32) * 0.02, 'pos_bias': jnp.zeros((64, 64), jnp.float32), 'Wg1': jax.random.normal(ks[5], (C, 32), jnp.float32) * s, 'bg1': jnp.zeros((32,), jnp.float32), 'Wg2': jax.random.normal(ks[6], (32, E), jnp.float32) * s, 'bg2': jnp.zeros((E,), jnp.float32), 'Wp': jax.random.normal(ks[7], (C, C), jnp.float32) * s, 'bp': jnp.zeros((C,), jnp.float32)}
    _L0_ffn_all = _L0_ffn_setup()
    _L0_ffn_in = {k: v for k, v in _L0_ffn_all.items() if k in ('Wqk', 'bqk', 'Wv', 'bv', 'conv_w', 'conv_b', 'glob', 'pos_bias', 'Wg1', 'bg1', 'Wg2', 'bg2', 'Wp', 'bp')}
    del _L0_ffn_all
    return {'x': x, 'mask_BS_i1_0': mask_BS_i1_0, 'pos_BS': pos_BS, 'L0_tok_word_emb': _L0_tok_in['word_emb'], 'L0_tok_pos_emb': _L0_tok_in['pos_emb'], 'L0_tok_type_emb': _L0_tok_in['type_emb'], 'L0_tok_gamma': _L0_tok_in['gamma'], 'L0_tok_beta': _L0_tok_in['beta'], 'L0_attn_in_proj_weight': _L0_attn_in['in_proj_weight'], 'L0_attn_in_proj_bias': _L0_attn_in['in_proj_bias'], 'L0_attn_logit_scale': _L0_attn_in['logit_scale'], 'L0_attn_head_scale': _L0_attn_in['head_scale'], 'L0_attn_out_w': _L0_attn_in['out_w'], 'L0_attn_out_b': _L0_attn_in['out_b'], 'L0_ffn_Wqk': _L0_ffn_in['Wqk'], 'L0_ffn_bqk': _L0_ffn_in['bqk'], 'L0_ffn_Wv': _L0_ffn_in['Wv'], 'L0_ffn_bv': _L0_ffn_in['bv'], 'L0_ffn_conv_w': _L0_ffn_in['conv_w'], 'L0_ffn_conv_b': _L0_ffn_in['conv_b'], 'L0_ffn_glob': _L0_ffn_in['glob'], 'L0_ffn_pos_bias': _L0_ffn_in['pos_bias'], 'L0_ffn_Wg1': _L0_ffn_in['Wg1'], 'L0_ffn_bg1': _L0_ffn_in['bg1'], 'L0_ffn_Wg2': _L0_ffn_in['Wg2'], 'L0_ffn_bg2': _L0_ffn_in['bg2'], 'L0_ffn_Wp': _L0_ffn_in['Wp'], 'L0_ffn_bp': _L0_ffn_in['bp']}

def reference(x, mask_BS_i1_0, pos_BS, L0_tok_word_emb, L0_tok_pos_emb, L0_tok_type_emb, L0_tok_gamma, L0_tok_beta, L0_attn_in_proj_weight, L0_attn_in_proj_bias, L0_attn_logit_scale, L0_attn_head_scale, L0_attn_out_w, L0_attn_out_b, L0_ffn_Wqk, L0_ffn_bqk, L0_ffn_Wv, L0_ffn_bv, L0_ffn_conv_w, L0_ffn_conv_b, L0_ffn_glob, L0_ffn_pos_bias, L0_ffn_Wg1, L0_ffn_bg1, L0_ffn_Wg2, L0_ffn_bg2, L0_ffn_Wp, L0_ffn_bp):
    import jax
    import jax.numpy as jnp

    def _L0_tok_ref(input_ids, token_type_ids, position_ids, word_emb, pos_emb, type_emb, gamma, beta):
        import jax, jax.numpy as jnp
        import numpy as np
        VOCAB = 30522
        MAX_POS = 128
        TYPE_VOCAB = 2
        HIDDEN = 192
        EPS = 1e-12
        x = word_emb[input_ids] + type_emb[token_type_ids] + pos_emb[position_ids]
        mean = jnp.mean(x, axis=-1, keepdims=True)
        var = jnp.mean(jnp.square(x - mean), axis=-1, keepdims=True)
        y = (x - mean) * jax.lax.rsqrt(var + EPS)
        return y * gamma + beta

    def _L0_attn_ref(x, in_proj_weight, in_proj_bias, logit_scale, head_scale, out_w, out_b):
        import jax, jax.numpy as jnp
        import numpy as np
        import math
        H = 12
        LOGIT_SCALE_MAX = math.log(1.0 / 0.01)

        def _normalize(t, eps=1e-12):
            n = jnp.linalg.norm(t, axis=-1, keepdims=True)
            return t / jnp.maximum(n, eps)
        L, N, C = x.shape
        D = C // H
        qkv = x @ in_proj_weight.T + in_proj_bias
        q, k, v = jnp.split(qkv, 3, axis=-1)

        def to_heads(t):
            return t.reshape(L, N, H, D).transpose(1, 2, 0, 3)
        q, k, v = (to_heads(q), to_heads(k), to_heads(v))
        attn = jnp.einsum('nhld,nhmd->nhlm', _normalize(q), _normalize(k))
        ls = jnp.exp(jnp.minimum(logit_scale, LOGIT_SCALE_MAX))
        attn = attn * ls[None]
        attn = jax.nn.softmax(attn, axis=-1)
        o = jnp.einsum('nhlm,nhmd->nhld', attn, v)
        o = o * head_scale[None]
        o = o.transpose(2, 0, 1, 3).reshape(L, N, C)
        return o @ out_w.T + out_b

    def _L0_ffn_ref(x, Wqk, bqk, Wv, bv, conv_w, conv_b, glob, pos_bias, Wg1, bg1, Wg2, bg2, Wp, bp):
        import jax, jax.numpy as jnp
        import numpy as np
        import math
        B, T, C = (8, 512, 192)
        E = 3
        HD = C // E
        TOPK = 2
        NGLOB = 4

        def _masked_softmax(att, mask):
            att = jnp.where(mask, -jnp.inf, att)
            return jax.nn.softmax(att, axis=-1)
        Bx, Tx, Cx = x.shape
        scale = 1.0 / math.sqrt(HD)
        gate = jax.nn.softmax(jax.nn.relu(x @ Wg1 + bg1) @ Wg2 + bg2, axis=-1)
        top_w, top_i = jax.lax.top_k(gate, TOPK)
        top_w = jax.nn.softmax(top_w, axis=-1)
        qk = x @ Wqk + bqk
        q, k = (qk[..., :Cx], qk[..., Cx:])
        q = q.reshape(Bx, Tx, E, HD)
        k = k.reshape(Bx, Tx, E, HD)
        rows = jnp.arange(Tx)[:, None]
        ys = []
        for e in range(E):
            qe = q[:, :, e]
            ke = k[:, :, e]
            ve = x @ Wv[e] + bv[e]
            if e == 0:
                qc = jnp.transpose(qe, (0, 2, 1))
                qc = jax.lax.conv_general_dilated(qc, conv_w, window_strides=(1,), padding=((1, 1),), feature_group_count=HD, dimension_numbers=('NCH', 'OIH', 'NCH'))
                qe = jnp.transpose(qc + conv_b[None, :, None], (0, 2, 1))
            elif e == 1:
                gb = jnp.broadcast_to(glob[None], (Bx, NGLOB, HD))
                ke = jnp.concatenate([ke, gb], axis=1)
                ve = jnp.concatenate([ve, gb], axis=1)
            att = jnp.einsum('btd,bsd->bts', qe, ke) * scale
            if e == 2 and Tx <= 64:
                att = att + pos_bias[:Tx, :Tx][None]
            S = att.shape[-1]
            mask = jnp.arange(S)[None, :] > rows
            att = _masked_softmax(att, mask[None])
            ys.append(jnp.einsum('bts,bsd->btd', att, ve))
        ys = jnp.stack(ys, axis=2)
        w_e = jnp.sum(jax.nn.one_hot(top_i, E, dtype=x.dtype) * top_w[..., None], axis=-2)
        combined = (ys * w_e[..., None]).reshape(Bx, Tx, Cx)
        return combined @ Wp + bp
    h = _L0_tok_ref(x, mask_BS_i1_0, pos_BS, L0_tok_word_emb, L0_tok_pos_emb, L0_tok_type_emb, L0_tok_gamma, L0_tok_beta)
    h = h + _L0_attn_ref(_layernorm(h, axis=-1), L0_attn_in_proj_weight, L0_attn_in_proj_bias, L0_attn_logit_scale, L0_attn_head_scale, L0_attn_out_w, L0_attn_out_b)
    h = h + _L0_ffn_ref(_layernorm(h, axis=-1), L0_ffn_Wqk, L0_ffn_bqk, L0_ffn_Wv, L0_ffn_bv, L0_ffn_conv_w, L0_ffn_conv_b, L0_ffn_glob, L0_ffn_pos_bias, L0_ffn_Wg1, L0_ffn_bg1, L0_ffn_Wg2, L0_ffn_bg2, L0_ffn_Wp, L0_ffn_bp)
    return h

_drawn_inputs = setup_inputs


def setup_inputs(seed=0):
    import zlib

    import numpy as np

    out = dict(_drawn_inputs(seed))
    spreads = {'L0_attn_in_proj_bias': (0.0, 0.1),
     'L0_attn_logit_scale': (2.3025851249694824, 0.2),
     'L0_attn_head_scale': (1.0, 0.2),
     'L0_attn_out_b': (0.0, 0.8),
     'L0_ffn_bqk': (0.0, 0.8),
     'L0_ffn_bv': (0.0, 0.8),
     'L0_ffn_conv_b': (0.0, 0.8),
     'L0_ffn_pos_bias': (0.0, 0.1),
     'L0_ffn_bg1': (0.0, 0.8),
     'L0_ffn_bg2': (0.0, 0.8),
     'L0_ffn_bp': (0.0, 0.787)}
    factors = {'L0_tok_gamma': 4.691,
     'L0_tok_beta': 3.835,
     'L0_ffn_Wqk': 8.0,
     'L0_ffn_Wv': 8.0,
     'L0_ffn_conv_w': 8.0,
     'L0_ffn_Wg1': 8.0,
     'L0_ffn_Wg2': 8.0,
     'L0_ffn_Wp': 8.0}
    for name, (base, spread) in spreads.items():
        noise = np.random.default_rng([zlib.crc32(name.encode()), seed]).standard_normal(out[name].shape)
        drawn = base * np.exp(spread * noise) if base else spread * noise
        out[name] = jnp.asarray(drawn.astype(out[name].dtype))
    for name, factor in factors.items():
        out[name] = (out[name] * factor).astype(out[name].dtype)
    return out
```

```python
from contextlib import ExitStack

import concourse.bass as bass
from concourse import mybir

ALU = mybir.AluOpType
ACT = mybir.ActivationFunctionType
AX = mybir.AxisListType
F32 = mybir.dt.float32
F32R = mybir.dt.float32r
F16 = mybir.dt.float16
BF16 = mybir.dt.bfloat16
I32 = mybir.dt.int32
U32 = mybir.dt.uint32

P = 128
LOG_SCALE_MAX = 4.605170185988092
MASK_Q, MASK_K = 128.0, 64.0
KEY_SCALE = 16.0
CAUSAL_OFF = -1.0e30


def block_kernel(nc, word_ids, type_ids, pos_ids, word_emb, pos_emb, type_emb, gamma, beta,
                 w_in, b_in, logit_scale, head_scale, w_out, b_out,
                 w_qk, b_qk, w_v, b_v, conv_w, conv_b, w_g1, b_g1, w_g2, b_g2, w_p, b_p,
                 h_scratch, out):
    C = word_emb.shape[1]
    T = word_ids.shape[1]
    H = logit_scale.shape[0]
    D = C // H
    L = out.shape[0]
    NPOS = P // L
    E = b_g2.shape[0]
    HD = C // E
    G1 = b_g1.shape[0]
    CB = C - P
    NG = 3
    J = H // 2
    U = L // 2
    NQKV = 3 * C
    NW2 = 3 * C + G1
    DA = D + 1

    ctx = ExitStack()
    with ctx:
        def sb(name, shape, dt=F32):
            return ctx.enter_context(nc.sbuf_tensor(name, shape, dt))

        def pb(name, shape, dt=F32):
            return ctx.enter_context(nc.psum_tensor(name, shape, dt))

        def sem(name):
            return ctx.enter_context(nc.semaphore(name))

        def two(name, shape, dt=F32):
            return [sb(f"{name}{i}", shape, dt) for i in range(2)]

        ids_w = sb("ids_w", [P, T], I32)
        ids_t = sb("ids_t", [P, T], I32)
        type_f = sb("type_f", [P, T])
        pos_row_i = sb("pos_row_i", [P, T * P], I32)
        pos_row = sb("pos_row", [P, T * P])
        iota_p = sb("iota_p", [P, 1])
        pos_tab = sb("pos_tab", [P, C])
        type_tab = sb("type_tab", [P, 2, C])
        type_diff = sb("type_diff", [P, C])
        pos_tab0 = sb("pos_tab0", [P, C])
        gamma_b = sb("gamma_b", [P, C])
        beta_b = sb("beta_b", [P, C])
        ident = sb("ident", [P, P])
        ident_h = sb("ident_h", [P, P], F16)
        ident_b = sb("ident_b", [P, P], BF16)
        minus_half = sb("minus_half", [P, 2 * H])
        eps = sb("eps", [P, 3])
        own_pos = sb("own_pos", [P, NPOS], F16)
        lscale = sb("lscale", [P, H])
        lscale_min = sb("lscale_min", [P, H])
        qk_scale = sb("qk_scale", [P, 2 * H])
        wi_f = sb("wi_f", [P, 2, NQKV])
        wi_hi = sb("wi_hi", [P, 2, NQKV], F32R)
        wi_lo = sb("wi_lo", [P, 2, NQKV], F32R)
        w2_f = sb("w2_f", [P, 2, NW2])
        w2_hi = sb("w2_hi", [P, 2, NW2], F32R)
        w2_lo = sb("w2_lo", [P, 2, NW2], F32R)
        wo_f = sb("wo_f", [P, 2, C])
        wo_s = sb("wo_s", [P, 2, C])
        hs_col = sb("hs_col", [P, 2])
        wp_f = sb("wp_f", [P, 2, C])
        mm_own = sb("mm_own", [P, 2, P], F16)
        mm_sum = sb("mm_sum", [P, P], F16)
        mm_sel = sb("mm_sel", [P, J, P], F16)
        mm_lhs = sb("mm_lhs", [P, J, P], F16)
        causal = sb("causal", [P, 4, P], BF16)
        conv_c = sb("conv_c", [HD, 4])
        wg2_b = sb("wg2_b", [P, E, G1])
        bg2_b = sb("bg2_b", [P, E])

        word = sb("word", [P, T, C])
        h0 = sb("h0", [P, T, C])
        onehot = two("onehot", [P, P])
        emb_a = two("emb_a", [P, C])
        emb_b = two("emb_b", [P, C])
        st1 = two("st1", [P, 6])
        mv1 = two("mv1", [P, 2])
        ve1 = two("ve1", [P, 1])
        rs1 = two("rs1", [P, 1])
        nrm = two("nrm", [P, C])
        nrg = two("nrg", [P, C])
        st2 = two("st2", [P, 6])
        mv2 = two("mv2", [P, 2])
        ve2 = two("ve2", [P, 1])
        rs2 = two("rs2", [P, 1])
        xn = two("xn", [P, 2 * P])
        xt_hi = two("xt_hi", [P, 2, P], F32R)
        xt_lo = two("xt_lo", [P, 2, P], F32R)
        sq = two("sq", [P, 2 * C])
        ssq = two("ssq", [P, 2 * H])
        ssc = two("ssc", [P, 2 * H])
        rno = two("rno", [P, 2 * H])
        rnk = two("rnk", [P, 2 * H])
        unit = two("unit", [P, 2 * C])
        qks = two("qks", [P, 2 * H, 4 * D], F16)
        qkt = two("qkt", [P, NG, 4, P], F16)
        nmx = two("nmx", [P, P], F16)
        nmt = two("nmt", [P, P], F16)
        vaug = two("vaug", [P, H, DA])
        et = two("et", [P, J, 2, P])
        rsum = two("rsum", [P, H])
        oa = two("oa", [P, 2 * P])
        ot = two("ot", [P, 2, P])
        h1t = two("h1t", [P, C])

        psA = pb("psA", [P, 512])
        psB = pb("psB", [P, 512])
        psC = pb("psC", [P, 512])
        psD = pb("psD", [P, 512])
        psS = pb("psS", [P, 2, 512])
        psT = pb("psT", [P, 2, 512])

        s_ids = sem("ids_loaded")
        s_tabs = sem("tables_loaded")
        s_zero = sem("weights_zeroed")
        s_win = sem("w_in_loaded")
        s_w2 = sem("w2_loaded")
        s_wop = sem("w_out_loaded")
        s_misc = sem("misc_loaded")
        s_pc = sem("pool_constants")
        s_cs = sem("setup_act")
        s_cd = sem("setup_dve")
        s_word = [sem(f"word_rows_{i}") for i in range(4)]
        s_oh = sem("onehot_built")
        s_pos = sem("pos_rows_out")
        s_e1 = sem("embed_dve")
        s_ln1 = sem("rstd1_done")
        s_aff = sem("affine_done")
        s_ln2 = sem("rstd2_done")
        s_xn = sem("xn_done")
        s_nd = sem("norm_dve")
        s_xT = sem("x_transposed")
        s_hi = sem("x_hi_copied")
        s_lo = sem("x_lo_made")
        s_qkv = sem("qkv_done")
        s_sq = sem("squares_done")
        s_ss = sem("square_sums")
        s_rn = sem("rnorm_done")
        s_unit = sem("unit_done")
        s_uh = sem("unit_hi")
        s_ul = sem("unit_lo")
        s_v = sem("v_copied")
        s_tr = sem("qk_transposed")
        s_qkt = sem("qkt_copied")
        s_sc = sem("scores_done")
        s_mx = sem("max_done")
        s_mT = sem("max_transposed")
        s_nmt = sem("max_copied")
        s_st = sem("scores_t_done")
        s_ex = sem("exp_done")
        s_pv = sem("pv_done")
        s_rc = sem("recip_done")
        s_oa = sem("attn_out_done")
        s_oT = sem("attn_transposed")
        s_ot = sem("attn_t_copied")
        s_pr = sem("proj_done")
        s_h1 = sem("h1_done")
        s_st1 = [sem(f"h1_stored_{i}") for i in range(2)]

        hb = word
        p_st = two("p_st", [P, 2, 6])
        p_mv = two("p_mv", [P, 2, 2])
        p_ve = two("p_ve", [P, 2])
        p_rs = two("p_rs", [P, 2])
        p_xn = two("p_xn", [P, 2, 2 * P])
        p_xh = two("p_xh", [P, 2, 2 * P], F32R)
        p_xl = two("p_xl", [P, 2, 2 * P], F32R)
        p_qk = two("p_qk", [P, 4, 2 * P])
        p_cv = two("p_cv", [HD, 2, P])
        p_v = two("p_v", [P, 2 * E, HD + 1])
        p_rl = two("p_rl", [P, 2, G1])
        p_rw = two("p_rw", [P, 2, E, G1])
        p_lg = two("p_lg", [P, 2 * E])
        p_lb = two("p_lb", [P, 2 * E])
        p_gm = two("p_gm", [P, 2])
        p_gd = two("p_gd", [P, 2 * E])
        p_ge = two("p_ge", [P, 2 * E])
        p_gs = two("p_gs", [P, 2])
        p_gr = two("p_gr", [P, 2])
        p_g = two("p_g", [P, 2 * E])
        p_mn = two("p_mn", [P, 2, 2])
        p_kp = two("p_kp", [P, 2, E])
        p_ks = two("p_ks", [P, 2])
        p_eg = two("p_eg", [P, 2 * E])
        p_ek = two("p_ek", [P, 2 * E])
        p_es = two("p_es", [P, 2])
        p_er = two("p_er", [P, 2])
        p_w = two("p_w", [P, 2 * E])
        p_nm = two("p_nm", [P, 2 * E])
        p_sh = two("p_sh", [P, 2 * E, P])
        p_ex = two("p_ex", [P, 2 * E, P])
        p_pt = two("p_pt", [P, 2 * E, P])
        p_ri = two("p_ri", [P, 2 * E])
        p_fc = two("p_fc", [P, 2 * E])
        p_y = two("p_y", [P, 2, 2 * P])
        p_yt = two("p_yt", [P, 2, 2 * P])
        p_o = two("p_o", [P, 2, C])

        q_h = [sem(f"p_rows_loaded_{i}") for i in range(4)]
        q_st = sem("p_stats")
        q_rs = sem("p_rstd")
        q_xn = sem("p_xn_done")
        q_xT = sem("p_x_transposed")
        q_hi = sem("p_x_hi")
        q_lo = sem("p_x_lo")
        q_qk = sem("p_qk_done")
        q_vg = sem("p_vg_done")
        q_qe = sem("p_qk_copied")
        q_cv = sem("p_conv")
        q_rl = sem("p_relu")
        q_vc = sem("p_v_copied")
        q_gp = sem("p_gate_pool")
        q_gd = sem("p_gate_dve")
        q_ga = sem("p_gate_act")
        q_gc = sem("p_gate_chain")
        q_ge = sem("p_gate_sums")
        q_kp = sem("p_gate_keep")
        q_sc = sem("p_scores")
        q_nm = sem("p_max")
        q_sh = sem("p_shifted")
        q_ex = sem("p_exp")
        q_pT = sem("p_p_transposed")
        q_pt = sem("p_pt_copied")
        q_pv = sem("p_pv")
        q_fc = sem("p_factor")
        q_y = sem("p_y_done")
        q_yT = sem("p_y_transposed")
        q_yt = sem("p_yt_copied")
        q_pr = sem("p_proj")
        q_o = sem("p_out_made")
        s_out = [sem(f"out_stored_{i}") for i in range(2)]

        pX = psA
        pQ = psT
        pV = psB
        pS = psS
        pP = [psC, psD]

        block = ctx.enter_context(nc.Block())

        def wait(eng, s, value):
            if not isinstance(value, int) or value > 0:
                eng.wait_ge(s, value)

        def steps(eng, stages, n, last):
            lo = last + 2
            hi = lo + (n - lo) // 2 * 2

            def one(s):
                stages(s, s % 2, lambda off: 0 <= s - off < n)

            for s in range(lo):
                one(s)
            with eng.Fori(lo, hi - 1, 2) as s:
                for k in range(2):
                    stages(s + k, (lo + k) % 2, lambda off: True)
            for s in range(hi, n + last):
                one(s)

        qk3 = psC[:, 0:2 * C].rearrange("p (h d) -> p h d", d=D)
        trb = psB[:, 256:512].bitcast(F16)
        mtb = psA[:, 256:320].bitcast(F16)
        pvo = psD[:, 256:256 + H * DA].rearrange("p (h d) -> p h d", d=DA)

        @block.sync
        def _(sp):
            sp.dma_start(ids_w[:], word_ids).then_inc(s_ids, 16)
            sp.dma_start(pos_row_i[:], pos_ids.partition_broadcast(P)).then_inc(s_tabs, 16)
            sp.dma_start(pos_tab[:], pos_emb).then_inc(s_tabs, 16)
            sp.dma_start(type_tab[:].rearrange("p a c -> p (a c)"),
                         type_emb.rearrange("a c -> (a c)").partition_broadcast(P)).then_inc(s_tabs, 16)
            sp.dma_start(ids_t[:], type_ids).then_inc(s_tabs, 16)
            sp.dma_start(wi_f[:, 0, :], w_in[0:P, :]).then_inc(s_win, 16)
            sp.wait_ge(s_zero, 1)
            sp.dma_start(wi_f[0:CB, 1, :], w_in[P:C, :]).then_inc(s_win, 16)
            sp.dma_start(wi_f[CB:CB + 1, 1, :], b_in.unsqueeze(0)).then_inc(s_win, 16)
            sp.wait_ge(s_zero, 3)
            sp.dma_start(wo_f[:, 0, :], w_out[0:P, :]).then_inc(s_wop, 16)
            sp.dma_start(wo_f[0:CB, 1, :], w_out[P:C, :]).then_inc(s_wop, 16)
            sp.dma_start(wo_f[CB:CB + 1, 1, :], b_out.unsqueeze(0)).then_inc(s_wop, 16)
            hs16 = head_scale.rearrange("h a b -> h (a b)")
            sp.dma_start(hs_col[:, 0:1], hs16[0:P // D, :].unsqueeze(1).broadcast_to([P // D, D, 1])).then_inc(s_wop, 16)
            sp.dma_start(hs_col[0:CB, 1:2], hs16[P // D:H, :].unsqueeze(1).broadcast_to([H - P // D, D, 1])).then_inc(s_wop, 16)
            sp.dma_start(wp_f[:, 0, :], w_p[0:P, :]).then_inc(s_wop, 16)
            sp.dma_start(wp_f[0:CB, 1, :], w_p[P:C, :]).then_inc(s_wop, 16)
            sp.dma_start(wp_f[CB:CB + 1, 1, :], b_p.unsqueeze(0)).then_inc(s_wop, 16)

            def store_h1(t, b):
                wait(sp, s_h1, t + 1)
                sp.dma_start(h_scratch[bass.ts(t, P), :], h1t[b][:]).then_inc(s_st1[b], 16)

            def stages(s, b, on):
                if on(3):
                    store_h1(s - 3, 1 - b)

            steps(sp, stages, T, 3)
            for b in range(2):
                sp.wait_ge(s_st1[b], 16 * (T // 2))
            src = h_scratch.rearrange("(n l) c -> n l c", l=L)
            for i in range(4):
                sp.dma_start(hb[:, 4 * i:4 * i + 4, :], src[:, 4 * i:4 * i + 4, :]).then_inc(q_h[i], 16)

            def store_out(u, b):
                wait(sp, q_o, u + 1)
                sp.dma_start(out[bass.ts(u, 2), :, :].rearrange("l n c -> n l c"), p_o[b][:]).then_inc(s_out[b], 16)

            def stages2(s, b, on):
                if on(1):
                    store_out(s - 1, 1 - b)

            steps(sp, stages2, U, 1)
            for b in range(2):
                sp.wait_ge(s_out[b], 16 * (U // 2))

        @block.gpsimd
        def _(pool):
            pool.iota(iota_p[:], pattern=[[0, 1]], base=0, channel_multiplier=1,
                      allow_small_or_imprecise_dtypes=True).then_inc(s_pc, 1)
            pool.memset(minus_half[:], -0.5).then_inc(s_pc, 1)
            pool.memset(ident[:], 0.0).then_inc(s_pc, 1)
            pool.wait_ge(s_pc, 3)
            pool.affine_select(out=ident[:], in_=ident[:], compare_op=ALU.not_equal, fill=1.0, base=0,
                               pattern=[[-1, P]], channel_multiplier=1).then_inc(s_pc, 1)
            pool.wait_ge(s_ids, 16)

            def gather(t):
                pool.indirect_dma_start(
                    word[:, t, :], None, word_emb,
                    bass.IndirectOffsetOnAxis(ids_w[:, t:t + 1].bitcast(U32), 0)).then_inc(s_word[min(t, 3)], 16)

            gather(0)
            gather(1)
            pool.wait_ge(s_pc, 4)
            pool.tensor_copy(ident_h[:], ident[:]).then_inc(s_pc, 1)
            pool.tensor_copy(ident_b[:], ident[:]).then_inc(s_pc, 1)
            pool.memset(own_pos[:], 1.0).then_inc(s_pc, 1)
            pool.wait_ge(s_pc, 7)
            pool.affine_select(out=own_pos[:], in_=own_pos[:], compare_op=ALU.is_ge, fill=0.0, base=0,
                               pattern=[[-L, NPOS]], channel_multiplier=1).then_inc(s_pc, 1)
            pool.wait_ge(s_pc, 8)
            pool.affine_select(out=own_pos[:], in_=own_pos[:], compare_op=ALU.is_ge, fill=0.0, base=L - 1,
                               pattern=[[L, NPOS]], channel_multiplier=-1).then_inc(s_pc, 1)
            for b in range(2):
                pool.memset(qks[b][:], 0.0).then_inc(s_pc, 1)
                pool.memset(nmx[b][:], 0.0).then_inc(s_pc, 1)
            pool.wait_ge(s_pc, 13)
            for b in range(2):
                for h0_, f in ((0, MASK_Q), (H, MASK_K)):
                    pool.tensor_scalar(qks[b][:, h0_:h0_ + H, 3 * D:3 * D + NPOS],
                                       own_pos[:].unsqueeze(1).broadcast_to([P, H, NPOS]), f, None, ALU.mult).then_inc(s_pc, 1)
                pool.memset(qks[b][:, 0:H, 3 * D + NPOS:3 * D + NPOS + 1], -MASK_Q).then_inc(s_pc, 1)
                pool.memset(qks[b][:, H:2 * H, 3 * D + NPOS:3 * D + NPOS + 1], MASK_K).then_inc(s_pc, 1)
                for p in range(2):
                    o = 64 * p + J
                    pool.tensor_scalar(nmx[b][:, o:o + NPOS], own_pos[:], MASK_Q, None, ALU.mult).then_inc(s_pc, 1)
                    pool.memset(nmx[b][:, o + NPOS:o + NPOS + 1], -MASK_Q).then_inc(s_pc, 1)
            gather(2)
            for t in range(3, T):
                gather(t)
            pool.memset(mm_own[:], MASK_K).then_inc(s_pc, 1)
            pool.memset(mm_sel[:], 0.0).then_inc(s_pc, 1)
            c0 = 13 + 2 * 8
            assert c0 == 29
            for p in range(2):
                r0 = 64 * p + J
                pool.wait_ge(s_pc, c0 + 2 + 4 * p)
                pool.affine_select(out=mm_own[:, p, :], in_=mm_own[:, p, :], compare_op=ALU.is_ge, fill=0.0,
                                   base=L * r0, pattern=[[1, P]], channel_multiplier=-L).then_inc(s_pc, 1)
                pool.affine_select(out=mm_sel[:], in_=mm_sel[:], compare_op=ALU.not_equal, fill=1.0,
                                   base=-64 * p, pattern=[[-1, J], [0, P]], channel_multiplier=1).then_inc(s_pc, 1)
                pool.wait_ge(s_pc, c0 + 4 + 4 * p)
                pool.affine_select(out=mm_own[:, p, :], in_=mm_own[:, p, :], compare_op=ALU.is_ge, fill=0.0,
                                   base=L - 1 - L * r0, pattern=[[-1, P]], channel_multiplier=L).then_inc(s_pc, 1)
                pool.wait_ge(s_pc, c0 + 5 + 4 * p)
                pool.affine_select(out=mm_own[:, p, :], in_=mm_own[:, p, :], compare_op=ALU.not_equal, fill=MASK_K,
                                   base=-(r0 + NPOS), pattern=[[0, P]], channel_multiplier=1).then_inc(s_pc, 1)
            pool.wait_ge(s_pc, c0 + 10)
            pool.tensor_tensor(mm_sum[:], mm_own[:, 0, :], mm_own[:, 1, :], ALU.add).then_inc(s_pc, 1)
            pool.wait_ge(s_pc, c0 + 11)
            pool.tensor_tensor(mm_lhs[:], mm_sel[:], mm_sum[:].unsqueeze(1).broadcast_to([P, J, P]), ALU.add).then_inc(s_pc, 1)
            pool.memset(causal[:], 0.0).then_inc(s_pc, 1)
            pool.wait_ge(s_pc, c0 + 13)
            pool.affine_select(out=causal[:], in_=causal[:], compare_op=ALU.is_ge, fill=CAUSAL_OFF, base=0,
                               pattern=[[0, 4], [-1, P]], channel_multiplier=1).then_inc(s_pc, 1)

            def rstd(ve, rs, mv, eps, s_in, v_in, s_own, t):
                wait(pool, s_in, v_in)
                pool.tensor_tensor(ve[:], mv[:, 1:2], eps, ALU.add).then_inc(s_own, 1)
                wait(pool, s_own, 2 * t + 1)
                pool.tensor_tensor(rs[:], ve[:], minus_half[:, 0:1], ALU.pow).then_inc(s_own, 1)

            def affine(t, b):
                wait(pool, s_nd, 3 * t + 1)
                pool.tensor_tensor(nrg[b][:], nrm[b][:], gamma_b[:], ALU.mult).then_inc(s_aff, 1)
                wait(pool, s_aff, 2 * t + 1)
                pool.tensor_tensor(h0[:, bass.ds(t, 1), :].rearrange("p a c -> p (a c)"), nrg[b][:], beta_b[:], ALU.add).then_inc(s_aff, 1)

            def rnorm(t, b):
                wait(pool, s_ss, 2 * t + 2)
                pool.tensor_tensor(rno[b][:], ssc[b][:], minus_half[:], ALU.pow).then_inc(s_rn, 1)
                wait(pool, s_rn, 2 * t + 1)
                wait(pool, s_unit, t - 1)
                pool.tensor_tensor(rnk[b][:], rno[b][:], qk_scale[:], ALU.mult).then_inc(s_rn, 1)

            def unit_lo(t, b):
                wait(pool, s_uh, 2 * t + 2)
                u = unit[b][:].rearrange("p (h d) -> p h d", d=D)
                pool.tensor_tensor(qks[b][:, 0:H, D:2 * D], u[:, 0:H, :], qks[b][:, 0:H, 0:D], ALU.subtract).then_inc(s_ul, 1)
                pool.tensor_tensor(qks[b][:, H:2 * H, 2 * D:3 * D], u[:, H:2 * H, :], qks[b][:, H:2 * H, 0:D], ALU.subtract).then_inc(s_ul, 1)

            pool.wait_ge(s_misc, 16 * 7)
            pool.wait_ge(s_cd, 5)

            def stages(s, b, on):
                if on(0):
                    rstd(ve1[b], rs1[b], mv1[b], eps[:, 2:3], s_e1, 4 * s + 4, s_ln1, s)
                if on(2):
                    unit_lo(s - 2, b)
                if on(0):
                    affine(s, b)
                    rstd(ve2[b], rs2[b], mv2[b], eps[:, 0:1], s_nd, 3 * s + 3, s_ln2, s)
                if on(1):
                    rnorm(s - 1, 1 - b)

            steps(pool, stages, T, 3)

            def gate(u, b):
                wait(pool, q_rl, u + 1)
                pool.tensor_tensor(p_rw[b][:], p_rl[b][:].unsqueeze(2).broadcast_to([P, 2, E, G1]),
                                   wg2_b[:].unsqueeze(1).broadcast_to([P, 2, E, G1]), ALU.mult).then_inc(q_gp, 1)

            def rstd2(u, b):
                wait(pool, q_st, 4 * u + 4)
                pool.tensor_tensor(p_ve[b][:], p_mv[b][:, :, 1:2].rearrange("p a o -> p (a o)"), eps[:, 0:2], ALU.add).then_inc(q_rs, 1)
                wait(pool, q_rs, 2 * u + 1)
                pool.tensor_tensor(p_rs[b][:], p_ve[b][:], minus_half[:, 0:2], ALU.pow).then_inc(q_rs, 1)

            def stages2(s, b, on):
                if on(0):
                    rstd2(s, b)
                    gate(s, b)

            steps(pool, stages2, U, 1)

        @block.scalar
        def _(act):
            act.dma_start(gamma_b[:], gamma.partition_broadcast(P)).then_inc(s_misc, 16)
            act.dma_start(beta_b[:], beta.partition_broadcast(P)).then_inc(s_misc, 16)
            act.dma_start(lscale[:], logit_scale.rearrange("h a b -> (h a b)").partition_broadcast(P)).then_inc(s_misc, 16)
            act.dma_start(conv_c[:, 0:3], conv_w.rearrange("c a k -> c (a k)")).then_inc(s_misc, 16)
            act.dma_start(conv_c[:, 3:4], conv_b.unsqueeze(1)).then_inc(s_misc, 16)
            act.dma_start(wg2_b[:].rearrange("p e g -> p (e g)"), w_g2.rearrange("e g -> (e g)").partition_broadcast(P)).then_inc(s_misc, 16)
            act.dma_start(bg2_b[:], b_g2.partition_broadcast(P)).then_inc(s_misc, 16)
            act.wait_ge(s_zero, 2)
            for dst, src in ((slice(0, 2 * C), w_qk), (slice(3 * C, NW2), w_g1)):
                act.dma_start(w2_f[:, 0, dst], src[0:P, :]).then_inc(s_w2, 16)
                act.dma_start(w2_f[0:CB, 1, dst], src[P:C, :]).then_inc(s_w2, 16)
            for e in range(E):
                dst = slice(2 * C + e * HD, 2 * C + (e + 1) * HD)
                act.dma_start(w2_f[:, 0, dst], w_v[e, 0:P, :]).then_inc(s_w2, 16)
                act.dma_start(w2_f[0:CB, 1, dst], w_v[e, P:C, :]).then_inc(s_w2, 16)
            act.dma_start(w2_f[CB:CB + 1, 1, 0:2 * C], b_qk.unsqueeze(0)).then_inc(s_w2, 16)
            act.dma_start(w2_f[CB:CB + 1, 1, 2 * C:3 * C], b_v.rearrange("e d -> (e d)").unsqueeze(0)).then_inc(s_w2, 16)
            act.dma_start(w2_f[CB:CB + 1, 1, 3 * C:NW2], b_g1.unsqueeze(0)).then_inc(s_w2, 16)
            act.wait_ge(s_tabs, 64)
            act.activation(pos_row[:], pos_row_i[:], ACT.Copy).then_inc(s_cs, 1)
            act.wait_ge(s_cd, 1)
            act.activation(qk_scale[:, 0:H], lscale_min[:], ACT.Exp).then_inc(s_cs, 1)
            act.wait_ge(s_win, 48)
            act.activation(wi_hi[:], wi_f[:], ACT.Copy).then_inc(s_cs, 1)
            act.wait_ge(s_w2, 16 * 13)
            act.activation(w2_hi[:], w2_f[:], ACT.Copy).then_inc(s_cs, 1)

            def x_hi(t, b):
                wait(act, s_xT, t + 1)
                wait(act, s_qkv, t - 1)
                act.activation(xt_hi[b][:].rearrange("p a n -> p (a n)"), psB[:, 0:2 * P], ACT.Copy).then_inc(s_hi, 1)

            def squares(t, b):
                wait(act, s_qkv, t + 1)
                wait(act, s_ss, 2 * (t - 1) - 1)
                act.activation(sq[b][:], psC[:, 0:2 * C], ACT.Square).then_inc(s_sq, 1)
                wait(act, s_pv, 3 * (t - 1))
                act.activation(vaug[b][:, :, 0:D], psD[:, 0:C].rearrange("p (h d) -> p h d", d=D), ACT.Copy).then_inc(s_v, 1)

            def unit_hi(t, b):
                wait(act, s_unit, t + 1)
                wait(act, s_tr, 3 * (t - 1))
                u = unit[b][:].rearrange("p (h d) -> p h d", d=D)
                q = qks[b][:, 0:H, :].rearrange("p h (a x) -> p h a x", x=2 * D)[:, :, :, 0:D]
                k = qks[b][:, H:2 * H, 0:2 * D].rearrange("p h (a x) -> p h a x", x=D)
                act.activation(qks[b][:, 0:H, 0:D], u[:, 0:H, :], ACT.Copy)
                act.activation(qks[b][:, 0:H, 2 * D:3 * D], u[:, 0:H, :], ACT.Copy).then_inc(s_uh, 1)
                act.activation(k, u[:, H:2 * H, :].unsqueeze(2).broadcast_to([P, H, 2, D]), ACT.Copy).then_inc(s_uh, 1)

            def copy_qkt(t, b, g):
                wait(act, s_tr, 3 * t + g + 1)
                wait(act, s_st, 3 * (t - 2) + g + 1)
                act.activation(qkt[b][:, g, :, :].rearrange("p a n -> p (a n)"), trb, ACT.Copy).then_inc(s_qkt, 1)

            def copy_max(t, b):
                wait(act, s_mT, t + 1)
                wait(act, s_st, 3 * (t - 1))
                act.activation(nmt[b][:], mtb, ACT.Copy).then_inc(s_nmt, 1)

            def exps(t, b, g):
                wait(act, s_st, 3 * t + g + 1)
                wait(act, s_pv, 3 * (t - 2) + g + 1)
                act.activation(et[b][:, 2 * g:2 * g + 2, :, :].rearrange("q j p c -> q p j c"),
                               psT[:, :, 0:2 * P].rearrange("q p (j c) -> q p j c", j=2),
                               ACT.Exp, scale=1.0 / KEY_SCALE).then_inc(s_ex, 1)

            def copy_ot(t, b):
                wait(act, s_oT, t + 1)
                wait(act, s_pr, t - 1)
                act.activation(ot[b][:].rearrange("p a n -> p (a n)"), psB[:, 0:2 * P], ACT.Copy).then_inc(s_ot, 1)

            def stages(s, b, on):
                if on(3):
                    exps(s - 3, 1 - b, 0)
                if on(2):
                    unit_hi(s - 2, b)
                if on(1):
                    x_hi(s - 1, 1 - b)
                if on(3):
                    exps(s - 3, 1 - b, 1)
                    exps(s - 3, 1 - b, 2)
                if on(1):
                    squares(s - 1, 1 - b)
                if on(2):
                    for g in range(NG):
                        copy_qkt(s - 2, b, g)
                if on(3):
                    copy_ot(s - 3, 1 - b)
                if on(2):
                    copy_max(s - 2, b)

            steps(act, stages, T, 3)

            def p_hi(u, b):
                wait(act, q_xT, u + 1)
                wait(act, q_vg, u - 1)
                act.activation(p_xh[b][:].rearrange("p a n -> p (a n)"), pX[:], ACT.Copy).then_inc(q_hi, 1)

            def p_qkcopy(u, b):
                wait(act, q_qk, u + 1)
                wait(act, q_sc, u - 1)
                act.activation(p_qk[b][:, 0:2, :], pQ[:, 0, :].rearrange("p (a n) -> p a n", a=2), ACT.Copy).then_inc(q_qe, 1)
                act.activation(p_qk[b][0:HD, 2, :], pQ[0:HD, 1, 0:2 * P], ACT.Copy).then_inc(q_qe, 1)
                act.activation(p_qk[b][0:HD, 3, :], pQ[HD:P, 1, 0:2 * P], ACT.Copy).then_inc(q_qe, 1)

            def p_relu(u, b):
                wait(act, q_vg, u + 1)
                wait(act, q_gp, u - 1)
                vg = pV[:, 0:2 * (C + G1)].rearrange("p (a n) -> p a n", a=2)
                act.activation(p_rl[b][:], vg[:, :, C:C + G1], ACT.Relu).then_inc(q_rl, 1)

            def p_gate(u, b):
                wait(act, q_gd, 7 * u + 3)
                act.activation(p_ge[b][:], p_gd[b][:], ACT.Exp).then_inc(q_ga, 1)
                wait(act, q_gd, 7 * u + 6)
                act.activation(p_eg[b][:], p_g[b][:], ACT.Exp).then_inc(q_ga, 1)

            def p_exp(u, b):
                wait(act, q_sh, u + 1)
                wait(act, q_pT, u - 1)
                act.activation(p_ex[b][:], p_sh[b][:], ACT.Exp, scale=float(HD) ** -0.5).then_inc(q_ex, 1)

            def p_ptcopy(u, b):
                wait(act, q_pT, u + 1)
                wait(act, q_pv, u - 1)
                for i in range(2):
                    act.activation(p_pt[b][:, 3 * i:3 * i + 3, :].rearrange("p a n -> p (a n)"), pP[i][:, 0:3 * P], ACT.Copy).then_inc(q_pt, 1)

            def p_ytcopy(u, b):
                wait(act, q_yT, u + 1)
                wait(act, q_pr, u - 1)
                act.activation(p_yt[b][:].rearrange("p a n -> p (a n)"), pX[:], ACT.Copy).then_inc(q_yt, 1)

            def stages2(s, b, on):
                if on(0):
                    p_hi(s, b)
                if on(1):
                    p_exp(s - 1, 1 - b)
                    p_ptcopy(s - 1, 1 - b)
                if on(0):
                    p_qkcopy(s, b)
                    p_relu(s, b)
                    p_gate(s, b)
                if on(1):
                    p_ytcopy(s - 1, 1 - b)

            steps(act, stages2, U, 1)

        @block.vector
        def _(dve):
            dve.memset(eps[:, 0:2], 1e-5)
            dve.memset(eps[:, 2:3], 1e-12)
            dve.memset(wi_f[:, 1, :], 0.0).then_inc(s_zero, 1)
            dve.memset(w2_f[:, 1, :], 0.0).then_inc(s_zero, 1)
            dve.memset(wo_f[:, 1, :], 0.0)
            dve.memset(wp_f[:, 1, :], 0.0)
            dve.memset(hs_col[:], 1.0).then_inc(s_zero, 1)
            dve.wait_ge(s_misc, 16 * 7)
            dve.tensor_scalar(lscale_min[:], lscale[:], LOG_SCALE_MAX, None, ALU.min).then_inc(s_cd, 1)
            dve.memset(qk_scale[:, H:2 * H], KEY_SCALE).then_inc(s_cd, 1)
            dve.wait_ge(s_tabs, 64)
            dve.tensor_tensor(type_diff[:], type_tab[:, 1, :], type_tab[:, 0, :], ALU.subtract).then_inc(s_cd, 1)
            dve.tensor_tensor(pos_tab0[:], pos_tab[:], type_tab[:, 0, :], ALU.add).then_inc(s_cd, 1)
            dve.tensor_copy(type_f[:], ids_t[:]).then_inc(s_cd, 1)
            for b in range(2):
                for tile in (xn[b], oa[b]):
                    dve.memset(tile[:, C:C + 1], 1.0)
                    dve.memset(tile[:, C + 1:2 * P], 0.0)
                for tile in (p_xn[b], p_y[b]):
                    dve.memset(tile[:, :, C:C + 1], 1.0)
                    dve.memset(tile[:, :, C + 1:2 * P], 0.0)
                dve.memset(vaug[b][:, :, D:DA], 1.0)
                dve.memset(p_v[b][:, :, HD:HD + 1], 1.0).then_inc(s_cd, 1)
            dve.wait_ge(s_cs, 3)
            dve.tensor_tensor(wi_lo[:], wi_f[:], wi_hi[:].bitcast(F32), ALU.subtract).then_inc(s_cd, 1)
            dve.wait_ge(s_wop, 16 * 8)
            for c in range(2):
                dve.tensor_scalar(wo_s[:, c, :], wo_f[:, c, :], hs_col[:, c:c + 1], None, ALU.mult).then_inc(s_cd, 1)
            dve.wait_ge(s_cs, 4)
            dve.tensor_tensor(w2_lo[:], w2_f[:], w2_hi[:].bitcast(F32), ALU.subtract).then_inc(s_cd, 1)

            def build_onehot(t, b):
                wait(dve, s_pos, t - 1)
                dve.tensor_scalar(onehot[b][:], pos_row[:, bass.ts(t, P)], iota_p[:, 0:1], None, ALU.is_equal).then_inc(s_oh, 1)

            def embed(t, b):
                if isinstance(t, int) and t < 3:
                    dve.wait_ge(s_word[t], 16)
                elif isinstance(t, int) and t == 3:
                    dve.wait_ge(s_word[3], 16 * (T - 3))
                dve.scalar_tensor_tensor(emb_a[b][:], type_diff[:], type_f[:, bass.ds(t, 1)],
                                         word[:, bass.ds(t, 1), :].rearrange("p a c -> p (a c)"), ALU.mult, ALU.add).then_inc(s_e1, 1)
                wait(dve, s_e1, 4 * t + 1)
                wait(dve, s_pos, t + 1)
                dve.tensor_tensor(emb_b[b][:], emb_a[b][:], psA[:, 0:C], ALU.add).then_inc(s_e1, 1)
                wait(dve, s_e1, 4 * t + 2)
                dve.bn_stats(st1[b][:], emb_b[b][:]).then_inc(s_e1, 1)
                wait(dve, s_e1, 4 * t + 3)
                if not isinstance(t, int) or t + 1 < T:
                    build_onehot(t + 1, 1 - b)
                dve.bn_aggr(mv1[b][:], st1[b][:]).then_inc(s_e1, 1)

            def normalise(t, b):
                wait(dve, s_ln1, 2 * t + 2)
                wait(dve, s_aff, 2 * (t - 2) + 1)
                dve.tensor_scalar(nrm[b][:], emb_b[b][:], mv1[b][:, 0:1], rs1[b][:, 0:1], ALU.subtract, ALU.mult).then_inc(s_nd, 1)

            def stats2(t, b):
                wait(dve, s_aff, 2 * t + 2)
                dve.bn_stats(st2[b][:], h0[:, bass.ds(t, 1), :].rearrange("p a c -> p (a c)")).then_inc(s_nd, 1)

            def stats2_end(t, b):
                if isinstance(t, int):
                    wait(dve, s_nd, 3 * t + 2)
                dve.bn_aggr(mv2[b][:], st2[b][:]).then_inc(s_nd, 1)

            def normalise2(t, b):
                wait(dve, s_ln2, 2 * t + 2)
                wait(dve, s_xT, t - 1)
                dve.tensor_scalar(xn[b][:, 0:C], h0[:, bass.ds(t, 1), :].rearrange("p a c -> p (a c)"), mv2[b][:, 0:1], rs2[b][:, 0:1],
                                  ALU.subtract, ALU.mult).then_inc(s_xn, 1)

            def x_lo(t, b):
                wait(dve, s_hi, t + 1)
                dve.tensor_tensor(xt_lo[b][:].rearrange("p a n -> p (a n)"), psB[:, 0:2 * P],
                                  xt_hi[b][:].bitcast(F32).rearrange("p a n -> p (a n)"), ALU.subtract).then_inc(s_lo, 1)

            def square_sums(t, b):
                wait(dve, s_sq, t + 1)
                dve.tensor_reduce(ssq[b][:], sq[b][:].rearrange("p (h d) -> p h d", d=D), AX.X, ALU.add).then_inc(s_ss, 1)
                wait(dve, s_ss, 2 * t + 1)
                dve.tensor_scalar(ssc[b][:], ssq[b][:], 1e-24, None, ALU.max).then_inc(s_ss, 1)

            def units(t, b):
                wait(dve, s_rn, 2 * t + 2)
                wait(dve, s_ul, 2 * (t - 1))
                dve.tensor_tensor(unit[b][:].rearrange("p (h d) -> p h d", d=D), qk3,
                                  rnk[b][:].unsqueeze(2).broadcast_to([P, 2 * H, D]), ALU.mult).then_inc(s_unit, 1)

            def maxima(t, b, g):
                wait(dve, s_sc, 3 * t + g + 1)
                wait(dve, s_mT, t - 1)
                dst = nmx[b][:].rearrange("q (p x) -> q p x", p=2)[:, :, 2 * g:2 * g + 2]
                dve.tensor_reduce(dst, psS[:, :, 0:2 * P].rearrange("q p (j c) -> q p j c", j=2), AX.X, ALU.max,
                                  negate=True).then_inc(s_mx, 1)

            def attn_out(t, b):
                wait(dve, s_pv, 3 * t + 3)
                dve.reciprocal(rsum[b][:].unsqueeze(2), pvo[:, :, D:DA]).then_inc(s_rc, 1)
                wait(dve, s_rc, t + 1)
                wait(dve, s_oT, t - 1)
                dve.tensor_tensor(oa[b][:, 0:C].rearrange("p (h d) -> p h d", d=D), pvo[:, :, 0:D],
                                  rsum[b][:].unsqueeze(2).broadcast_to([P, H, D]), ALU.mult).then_inc(s_oa, 1)

            def residual(t, b):
                wait(dve, s_pr, t + 1)
                if not isinstance(t, int) or t >= 2:
                    wait(dve, s_st1[b], (t - b) * 8)
                dve.tensor_tensor(h1t[b][:], psA[:, 0:C], h0[:, bass.ds(t, 1), :].rearrange("p a c -> p (a c)"), ALU.add).then_inc(s_h1, 1)

            dve.wait_ge(s_pc, 29)
            dve.wait_ge(s_cs, 2)
            dve.wait_ge(s_cd, 11)
            build_onehot(0, 0)

            def stages(s, b, on):
                if on(2):
                    units(s - 2, b)
                if on(0):
                    embed(s, b)
                if on(1):
                    x_lo(s - 1, 1 - b)
                if on(3):
                    attn_out(s - 3, 1 - b)
                if on(0):
                    normalise(s, b)
                if on(1):
                    square_sums(s - 1, 1 - b)
                if on(2):
                    maxima(s - 2, b, 0)
                if on(0):
                    stats2(s, b)
                if on(2):
                    if on(0):
                        wait(dve, s_nd, 3 * s + 2)
                    maxima(s - 2, b, 1)
                if on(0):
                    stats2_end(s, b)
                    normalise2(s, b)
                if on(2):
                    maxima(s - 2, b, 2)
                if on(3):
                    residual(s - 3, 1 - b)

            steps(dve, stages, T, 3)

            def p_stats(u, b):
                if isinstance(u, int):
                    dve.wait_ge(q_h[u // 2], 16)
                for a in range(2):
                    dve.bn_stats(p_st[b][:, a, :], hb[:, bass.ds(2 * u + a, 1), :].rearrange("p a c -> p (a c)")).then_inc(q_st, 1)

            def p_stats_end(u, b):
                for a in range(2):
                    if isinstance(u, int):
                        wait(dve, q_st, 4 * u + 1 + a)
                    dve.bn_aggr(p_mv[b][:, a, :], p_st[b][:, a, :]).then_inc(q_st, 1)

            def p_norm(u, b):
                wait(dve, q_rs, 2 * u + 2)
                wait(dve, q_xT, u - 1)
                for a in range(2):
                    dve.tensor_scalar(p_xn[b][:, a, 0:C], hb[:, bass.ds(2 * u + a, 1), :].rearrange("p a c -> p (a c)"), p_mv[b][:, a, 0:1],
                                      p_rs[b][:, a:a + 1], ALU.subtract, ALU.mult).then_inc(q_xn, 1)

            def p_lo(u, b):
                wait(dve, q_hi, u + 1)
                dve.tensor_tensor(p_xl[b][:].rearrange("p a n -> p (a n)"), pX[:],
                                  p_xh[b][:].bitcast(F32).rearrange("p a n -> p (a n)"), ALU.subtract).then_inc(q_lo, 1)

            def p_vcopy(u, b):
                wait(dve, q_rl, u + 1)
                wait(dve, q_pv, u - 1)
                vg = pV[:, 0:2 * (C + G1)].rearrange("p (a n) -> p a n", a=2)
                dve.tensor_copy(p_v[b][:, :, 0:HD].rearrange("p (a e) d -> p a e d", a=2),
                                vg[:, :, 0:C].rearrange("p a (e d) -> p a e d", e=E)).then_inc(q_vc, 1)

            def p_conv(u, b):
                wait(dve, q_qe, 3 * u + 1)
                q0 = p_qk[b][0:HD, 0, :].rearrange("p (a n) -> p a n", a=2)
                c = p_cv[b]
                wait(dve, q_sc, u - 1)
                dve.tensor_scalar(c[:], q0, conv_c[:, 1:2], conv_c[:, 3:4], ALU.mult, ALU.add).then_inc(q_cv, 1)
                wait(dve, q_cv, 3 * u + 1)
                dve.scalar_tensor_tensor(c[:, :, 1:P], q0[:, :, 0:P - 1], conv_c[:, 0:1], c[:, :, 1:P], ALU.mult, ALU.add).then_inc(q_cv, 1)
                wait(dve, q_cv, 3 * u + 2)
                dve.scalar_tensor_tensor(c[:, :, 0:P - 1], q0[:, :, 1:P], conv_c[:, 2:3], c[:, :, 0:P - 1], ALU.mult, ALU.add).then_inc(q_cv, 1)

            def bc(x):
                return x.unsqueeze(2).broadcast_to([P, 2, E])

            def three(x):
                return x.rearrange("p (a e) -> p a e", e=E)

            def p_gate(u, b):
                n = 7 * u
                wait(dve, q_gp, u + 1)
                dve.tensor_reduce(p_lg[b][:], p_rw[b][:].rearrange("p a e g -> p (a e) g"), AX.X, ALU.add).then_inc(q_gd, 1)
                wait(dve, q_gd, n + 1)
                dve.tensor_tensor(three(p_lb[b][:]), three(p_lg[b][:]), bg2_b[:].unsqueeze(1).broadcast_to([P, 2, E]), ALU.add).then_inc(q_gc, 1)
                wait(dve, q_gc, 3 * u + 1)
                dve.tensor_reduce(p_gm[b][:], three(p_lb[b][:]), AX.X, ALU.max, negate=True).then_inc(q_gd, 1)
                wait(dve, q_gd, n + 2)
                dve.tensor_tensor(three(p_gd[b][:]), three(p_lb[b][:]), bc(p_gm[b][:]), ALU.add).then_inc(q_gd, 1)

            def p_gate2(u, b):
                n = 7 * u
                wait(dve, q_ga, 2 * u + 1)
                dve.tensor_reduce(p_gs[b][:], three(p_ge[b][:]), AX.X, ALU.add).then_inc(q_gd, 1)
                wait(dve, q_gd, n + 4)
                dve.reciprocal(p_gr[b][:], p_gs[b][:]).then_inc(q_gd, 1)
                wait(dve, q_gd, n + 5)
                dve.tensor_tensor(three(p_g[b][:]), three(p_ge[b][:]), bc(p_gr[b][:]), ALU.mult).then_inc(q_gd, 1)

            def p_gate3(u, b):
                g3 = three(p_g[b][:])
                wait(dve, q_gd, 7 * u + 6)
                dve.tensor_tensor(p_mn[b][:], g3[:, :, 1:3], g3[:, :, 0:2], ALU.min).then_inc(q_kp, 1)
                wait(dve, q_kp, 4 * u + 1)
                dve.tensor_tensor(p_kp[b][:, :, 0:1], g3[:, :, 0:1], p_mn[b][:, :, 1:2], ALU.is_ge).then_inc(q_kp, 1)
                dve.tensor_tensor(p_kp[b][:, :, 2:3], g3[:, :, 2:3], p_mn[b][:, :, 0:1], ALU.is_gt).then_inc(q_kp, 1)
                wait(dve, q_kp, 4 * u + 3)
                dve.tensor_tensor(p_ks[b][:].unsqueeze(2), p_kp[b][:, :, 0:1], p_kp[b][:, :, 2:3], ALU.add).then_inc(q_kp, 1)
                wait(dve, q_kp, 4 * u + 4)
                dve.tensor_scalar(p_kp[b][:, :, 1:2], p_ks[b][:].unsqueeze(2), -1.0, 2.0, ALU.mult, ALU.add).then_inc(q_gc, 1)
                wait(dve, q_gc, 3 * u + 2)
                wait(dve, q_ga, 2 * u + 2)
                dve.tensor_tensor(three(p_ek[b][:]), three(p_eg[b][:]), p_kp[b][:], ALU.mult).then_inc(q_gc, 1)
                wait(dve, q_gc, 3 * u + 3)
                dve.tensor_reduce(p_es[b][:], three(p_ek[b][:]), AX.X, ALU.add).then_inc(q_ge, 1)
                wait(dve, q_ge, 2 * u + 1)
                dve.reciprocal(p_er[b][:], p_es[b][:]).then_inc(q_ge, 1)
                wait(dve, q_ge, 2 * u + 2)
                dve.tensor_tensor(three(p_w[b][:]), three(p_ek[b][:]), bc(p_er[b][:]), ALU.mult).then_inc(q_gd, 1)

            def p_shift(u, b):
                wait(dve, q_sc, u + 1)
                s4 = pS[:, 0, :].rearrange("p (i n) -> p i n", n=P)
                s2 = pS[:, 1, 0:2 * P].rearrange("p (i n) -> p i n", n=P)
                dve.tensor_reduce(p_nm[b][:, 0:4], s4, AX.X, ALU.max, negate=True).then_inc(q_nm, 1)
                dve.tensor_reduce(p_nm[b][:, 4:6], s2, AX.X, ALU.max, negate=True).then_inc(q_nm, 1)
                wait(dve, q_nm, 2 * u + 2)
                wait(dve, q_ex, u - 1)
                dve.tensor_tensor(p_sh[b][:, 0:4, :], s4, p_nm[b][:, 0:4].unsqueeze(2).broadcast_to([P, 4, P]), ALU.add)
                dve.tensor_tensor(p_sh[b][:, 4:6, :], s2, p_nm[b][:, 4:6].unsqueeze(2).broadcast_to([P, 2, P]), ALU.add).then_inc(q_sh, 1)

            def p_outs(u, b):
                pv = pQ[:, 0, 0:2 * E * (HD + 1)].rearrange("p (i d) -> p i d", d=HD + 1)
                wait(dve, q_pv, u + 1)
                dve.reciprocal(p_ri[b][:].unsqueeze(2), pv[:, :, HD:HD + 1]).then_inc(q_fc, 1)
                wait(dve, q_fc, 2 * u + 1)
                dve.tensor_tensor(p_fc[b][:], p_ri[b][:], p_w[b][:], ALU.mult).then_inc(q_fc, 1)
                wait(dve, q_fc, 2 * u + 2)
                wait(dve, q_yT, u - 1)
                dve.tensor_tensor(p_y[b][:, :, 0:C].rearrange("p a (e d) -> p a e d", e=E),
                                  pv[:, :, 0:HD].rearrange("p (a e) d -> p a e d", a=2),
                                  p_fc[b][:].rearrange("p (a e) -> p a e", a=2).unsqueeze(3).broadcast_to([P, 2, E, HD]), ALU.mult).then_inc(q_y, 1)

            def p_residual(u, b):
                wait(dve, q_pr, u + 1)
                if not isinstance(u, int) or u >= 2:
                    wait(dve, s_out[b], (u - b) * 8)
                dve.tensor_tensor(p_o[b][:], pV[:, 0:2 * C].rearrange("p (a n) -> p a n", a=2), hb[:, bass.ds(2 * u, 2), :], ALU.add).then_inc(q_o, 1)

            def stages2(s, b, on):
                if on(0):
                    p_stats(s, b)
                if on(1):
                    if on(0):
                        wait(dve, q_st, 4 * s + 2)
                    p_shift(s - 1, 1 - b)
                if on(0):
                    p_stats_end(s, b)
                    p_norm(s, b)
                    p_lo(s, b)
                    p_conv(s, b)
                    p_vcopy(s, b)
                    p_gate(s, b)
                if on(1):
                    p_outs(s - 1, 1 - b)
                if on(0):
                    p_gate2(s, b)
                    p_gate3(s, b)
                if on(1):
                    p_residual(s - 1, 1 - b)

            for i in range(4):
                dve.wait_ge(q_h[i], 16)
            steps(dve, stages2, U, 1)

        @block.tensor
        def _(pe):
            pe.wait_ge(s_pc, 4)
            pe.wait_ge(s_cd, 4)

            def pos_rows(t, b):
                wait(pe, s_oh, t + 1)
                wait(pe, s_nmt, t - 2)
                wait(pe, s_h1, t - 3)
                pe.matmul(psA[:, 0:C], onehot[b][:], pos_tab0[:], start=True, stop=True).then_inc(s_pos, 1)

            def x_transpose(t, b):
                wait(pe, s_xn, t + 1)
                wait(pe, s_ot, t - 2)
                for c in range(2):
                    m = pe.transpose(psB[:, c * P:(c + 1) * P], xn[b][:, c * P:(c + 1) * P], ident[:])
                m.then_inc(s_xT, 1)

            def qkv(t, b):
                wait(pe, s_lo, t + 1)
                wait(pe, s_unit, t)
                wait(pe, s_v, t)
                if isinstance(t, int) and t == 0:
                    pe.wait_ge(s_cd, 8)
                wait(pe, s_oa, t - 1)
                parts = [(xt_hi[b], wi_hi), (xt_hi[b], wi_lo), (xt_lo[b], wi_hi)]
                for k, (x, w) in enumerate(parts):
                    for c in range(2):
                        first, last = k + c == 0, k == 2 and c == 1
                        pe.matmul(psC[:, 0:2 * C], x[:, c, :], w[:, c, 0:2 * C], start=first, stop=last)
                        m = pe.matmul(psD[:, 0:C], x[:, c, :], w[:, c, 2 * C:3 * C], start=first, stop=last)
                m.then_inc(s_qkv, 1)

            def transposes(t, b, g):
                wait(pe, s_ul, 2 * t + 2)
                wait(pe, s_qkt, 3 * t + g)
                if g == 0:
                    wait(pe, s_lo, t + 2 if not isinstance(t, int) else min(t + 2, T))
                for i in range(4):
                    h0_ = (i // 2) * H + 4 * g + 2 * (i % 2)
                    m = pe.transpose(trb[:, i * P:(i + 1) * P], qks[b][:, h0_:h0_ + 2, :].rearrange("p h x -> p (h x)"), ident_h[:])
                m.then_inc(s_tr, 1)

            def scores(t, b, g):
                wait(pe, s_qkt, 3 * t + g + 1)
                wait(pe, s_mx, 3 * t + g)
                for j in range(2):
                    for p in range(2):
                        r = slice(64 * p, 64 * p + 64)
                        m = pe.matmul(psS[:, p, j * P:(j + 1) * P], qkt[b][r, g, j, :], qkt[b][r, g, 2 + j, :], start=True, stop=True)
                m.then_inc(s_sc, 1)

            def max_transpose(t, b):
                wait(pe, s_mx, 3 * t + 3)
                wait(pe, s_h1, t - 1)
                wait(pe, s_e1, 4 * (t + 2) + 2 if not isinstance(t, int) else 4 * min(t + 2, T - 1) + 2)
                pe.transpose(mtb, nmx[b][:], ident_h[:]).then_inc(s_mT, 1)

            def scores_t(t, b, g):
                wait(pe, s_nmt, t + 1)
                wait(pe, s_ex, 3 * t + g)
                for j in range(2):
                    for p in range(2):
                        r = slice(64 * p, 64 * p + 64)
                        rs = slice(64 * p, 64 * p + 3 * D)
                        o = psT[:, p, j * P:(j + 1) * P]
                        pe.matmul(o, mm_lhs[r, 2 * g + j, :], nmt[b][r, :], start=True, stop=False)
                        m = pe.matmul(o, qkt[b][rs, g, 2 + j, :], qkt[b][rs, g, j, :], start=False, stop=True)
                m.then_inc(s_st, 1)

            def weighted(t, b, g):
                wait(pe, s_ex, 3 * t + g + 1)
                if g == 0:
                    wait(pe, s_v, t + 2 if not isinstance(t, int) else min(t + 2, T))
                for j in range(2):
                    for p in range(2):
                        h = 4 * g + 2 * j + p
                        m = pe.matmul(pvo[:, h, :], et[b][:, 2 * g + j, p, :], vaug[b][:, h, :], start=True, stop=True)
                m.then_inc(s_pv, 1)

            def out_transpose(t, b):
                wait(pe, s_oa, t + 1)
                for c in range(2):
                    m = pe.transpose(psB[:, c * P:(c + 1) * P], oa[b][:, c * P:(c + 1) * P], ident[:])
                m.then_inc(s_oT, 1)

            def project(t, b):
                wait(pe, s_ot, t + 1)
                for c in range(2):
                    m = pe.matmul(psA[:, 0:C], ot[b][:, c, :], wo_s[:, c, :], start=(c == 0), stop=(c == 1))
                m.then_inc(s_pr, 1)

            def stages(s, b, on):
                if on(3):
                    scores_t(s - 3, 1 - b, 0)
                if on(0):
                    pos_rows(s, b)
                if on(1):
                    x_transpose(s - 1, 1 - b)
                if on(3):
                    scores_t(s - 3, 1 - b, 1)
                    weighted(s - 3, 1 - b, 0)
                    scores_t(s - 3, 1 - b, 2)
                    weighted(s - 3, 1 - b, 1)
                    weighted(s - 3, 1 - b, 2)
                if on(1):
                    qkv(s - 1, 1 - b)
                if on(2):
                    transposes(s - 2, b, 0)
                for g in range(NG):
                    if on(2):
                        scores(s - 2, b, g)
                        if g + 1 < NG:
                            transposes(s - 2, b, g + 1)
                if on(3):
                    wait(pe, s_qkt, 3 * (s - 3) + 6 if not isinstance(s, int) else 3 * min(s - 1, T))
                    out_transpose(s - 3, 1 - b)
                if on(2):
                    max_transpose(s - 2, b)
                if on(3):
                    wait(pe, s_nmt, s - 1 if not isinstance(s, int) else min(s - 1, T))
                    project(s - 3, 1 - b)

            pe.wait_ge(s_pc, 43)
            steps(pe, stages, T, 3)

            def p_xT(u, b):
                wait(pe, q_xn, 2 * u + 2)
                if isinstance(u, int) and u == 0:
                    pe.wait_ge(s_h1, T)
                    pe.wait_ge(s_cd, 11)
                wait(pe, q_yt, u - 1)
                for c in range(2):
                    for a in range(2):
                        o = 256 * c + P * a
                        m = pe.transpose(pX[:, o:o + P], p_xn[b][:, a, c * P:(c + 1) * P], ident[:])
                m.then_inc(q_xT, 1)

            def p_qkv(u, b):
                wait(pe, q_lo, u + 1)
                wait(pe, q_y, u - 1)
                wait(pe, q_o, u - 1)
                parts = [(p_xh[b], w2_hi), (p_xh[b], w2_lo), (p_xl[b], w2_hi)]
                n = len(parts) * 2
                for i in range(3):
                    o = pQ[:, i // 2, 256 * (i % 2):256 * (i % 2) + 256]
                    for k in range(n):
                        x, w = parts[k // 2]
                        m = pe.matmul(o, w[:, k % 2, i * P:(i + 1) * P], x[:, k % 2, :], start=(k == 0), stop=(k == n - 1))
                m.then_inc(q_qk, 1)
                for a in range(2):
                    o = pV[:, a * (C + G1):(a + 1) * (C + G1)]
                    for k in range(n):
                        x, w = parts[k // 2]
                        m = pe.matmul(o, x[:, k % 2, a * P:(a + 1) * P], w[:, k % 2, 2 * C:NW2], start=(k == 0), stop=(k == n - 1))
                m.then_inc(q_vg, 1)

            SLOTS = [(0, 0), (0, 2), (1, 0), (1, 2), (0, 1), (1, 1)]

            def p_scores(u, b):
                wait(pe, q_sh, u)
                wait(pe, q_cv, 3 * u + 3)
                wait(pe, q_qe, 3 * u + 3)
                pe.matmul(pS[:, 0, :], ident_b[:], causal[:].rearrange("p a n -> p (a n)"), start=True, stop=True, skip_group_check=True)
                pe.matmul(pS[:, 1, 0:2 * P], ident_b[:], causal[:, 0:2, :].rearrange("p a n -> p (a n)"), start=True, stop=True, skip_group_check=True)
                for i, (a, e) in enumerate(SLOTS):
                    col = slice(a * P, (a + 1) * P)
                    lhs = (p_cv[b][:, a, :], p_qk[b][HD:P, 0, col], p_qk[b][0:HD, 2, col])[e]
                    rhs = (p_qk[b][0:HD, 1, col], p_qk[b][HD:P, 1, col], p_qk[b][0:HD, 3, col])[e]
                    m = pe.matmul(pS[:, i // 4, (i % 4) * P:(i % 4 + 1) * P], lhs, rhs, start=False, stop=True, skip_group_check=True)
                m.then_inc(q_sc, 1)

            def p_pT(u, b):
                wait(pe, q_ex, u + 1)
                wait(pe, q_pt, 2 * u)
                for i in range(2 * E):
                    m = pe.transpose(pP[i // 3][:, (i % 3) * P:(i % 3 + 1) * P], p_ex[b][:, i, :], ident[:])
                m.then_inc(q_pT, 1)

            def p_pv(u, b):
                wait(pe, q_pt, 2 * u + 2)
                wait(pe, q_vc, u + 1)
                wait(pe, q_qe, 3 * (u + 2) if not isinstance(u, int) else 3 * min(u + 2, U))
                for i, (a, e) in enumerate(SLOTS):
                    k = a * E + e
                    m = pe.matmul(pQ[:, 0, k * (HD + 1):(k + 1) * (HD + 1)], p_pt[b][:, i, :], p_v[b][:, k, :], start=True, stop=True)
                m.then_inc(q_pv, 1)

            def p_yT(u, b):
                wait(pe, q_y, u + 1)
                wait(pe, q_lo, u + 2 if not isinstance(u, int) else min(u + 2, U))
                for c in range(2):
                    for a in range(2):
                        o = 256 * c + P * a
                        m = pe.transpose(pX[:, o:o + P], p_y[b][:, a, c * P:(c + 1) * P], ident[:])
                m.then_inc(q_yT, 1)

            def p_project(u, b):
                wait(pe, q_yt, u + 1)
                nxt = u + 2 if not isinstance(u, int) else min(u + 2, U)
                wait(pe, q_vc, nxt)
                wait(pe, q_rl, nxt)
                for a in range(2):
                    for c in range(2):
                        m = pe.matmul(pV[:, a * C:(a + 1) * C], p_yt[b][:, c, a * P:(a + 1) * P], wp_f[:, c, :], start=(c == 0), stop=(c == 1))
                m.then_inc(q_pr, 1)

            def stages2(s, b, on):
                if on(1):
                    p_scores(s - 1, 1 - b)
                if on(0):
                    p_xT(s, b)
                    p_qkv(s, b)
                if on(1):
                    p_pT(s - 1, 1 - b)
                    p_pv(s - 1, 1 - b)
                    p_yT(s - 1, 1 - b)
                    p_project(s - 1, 1 - b)

            steps(pe, stages2, U, 1)


_INS = ['word_ids', 'type_ids', 'pos_ids', 'word_emb', 'pos_emb', 'type_emb', 'gamma', 'beta',
        'w_in', 'b_in', 'logit_scale', 'head_scale', 'w_out', 'b_out', 'w_qk', 'b_qk', 'w_v', 'b_v',
        'conv_w', 'conv_b', 'w_g1', 'b_g1', 'w_g2', 'b_g2', 'w_p', 'b_p']


def kernel(**inputs):
    import numpy as _np
    import concourse.bacc as _bacc
    from concourse import mybir as _mybir
    from concourse.bass_utils import run_bass_kernel_spmd as _run

    a = {k: _np.asarray(v) for k, v in inputs.items()}
    seqs, positions = a['x'].shape
    near = 128 // seqs

    def by_tile(ids):
        return ids.reshape(seqs, positions // near, near).transpose(1, 2, 0)

    laid = {
        'word_ids': by_tile(a['x']).reshape(-1, 128).T,
        'type_ids': by_tile(a['mask_BS_i1_0']).reshape(-1, 128).T,
        'pos_ids': by_tile(a['pos_BS']).reshape(-1),
        'word_emb': a['L0_tok_word_emb'], 'pos_emb': a['L0_tok_pos_emb'], 'type_emb': a['L0_tok_type_emb'],
        'gamma': a['L0_tok_gamma'], 'beta': a['L0_tok_beta'],
        'w_in': a['L0_attn_in_proj_weight'].T, 'b_in': a['L0_attn_in_proj_bias'],
        'logit_scale': a['L0_attn_logit_scale'], 'head_scale': a['L0_attn_head_scale'],
        'w_out': a['L0_attn_out_w'].T, 'b_out': a['L0_attn_out_b'],
    }
    hd = a['L0_ffn_Wqk'].shape[1] // 6
    order = _np.concatenate([_np.arange(hd) + hd * e for e in (0, 1, 3, 4, 2, 5)])
    laid['w_qk'] = a['L0_ffn_Wqk'][:, order]
    laid['b_qk'] = a['L0_ffn_bqk'][order]
    laid['w_g2'] = a['L0_ffn_Wg2'].T
    for name, key in (('w_v', 'Wv'), ('b_v', 'bv'), ('conv_w', 'conv_w'), ('conv_b', 'conv_b'), ('w_g1', 'Wg1'),
                      ('b_g1', 'bg1'), ('b_g2', 'bg2'), ('w_p', 'Wp'), ('b_p', 'bp')):
        laid[name] = a['L0_ffn_' + key]

    nc = _bacc.Bacc("TRN2", target_bir_lowering=False, num_devices=1)
    arrays, args = {}, []
    for name in _INS:
        x = _np.ascontiguousarray(laid[name])
        arrays[f"in_{name}"] = x
        args.append(nc.dram_tensor(f"in_{name}", x.shape, _mybir.dt.from_np(x.dtype), kind="ExternalInput").ap())
    width = a['L0_tok_word_emb'].shape[1]
    args.append(nc.dram_tensor("h_scratch", (seqs * positions, width), _mybir.dt.float32, kind="Internal").ap())
    args.append(nc.dram_tensor("out_0", (seqs, positions, width), _mybir.dt.float32, kind="ExternalOutput").ap())
    block_kernel(nc, *args)
    r = _run(nc, [arrays], core_ids=[0])
    return r.results[0]["out_0"]
```

```python
from contextlib import ExitStack

import concourse.bass as bass
from concourse import mybir

ALU = mybir.AluOpType
ACT = mybir.ActivationFunctionType
AX = mybir.AxisListType
F32 = mybir.dt.float32
F32R = mybir.dt.float32r
F16 = mybir.dt.float16
BF16 = mybir.dt.bfloat16
I32 = mybir.dt.int32
U32 = mybir.dt.uint32

P = 128
LOG_SCALE_MAX = 4.605170185988092
MASK_Q, MASK_K = 128.0, 64.0
KEY_SCALE = 16.0
CAUSAL_OFF = -1.0e30


def block_kernel(nc, word_ids, type_ids, pos_ids, word_emb, pos_emb, type_emb, gamma, beta,
                 w_in, b_in, logit_scale, head_scale, w_out, b_out,
                 w_qk, b_qk, w_v, b_v, conv_w, conv_b, w_g1, b_g1, w_g2, b_g2, w_p, b_p,
                 h_scratch, out):
    C = word_emb.shape[1]
    T = word_ids.shape[1]
    H = logit_scale.shape[0]
    D = C // H
    L = out.shape[0]
    NPOS = P // L
    E = b_g2.shape[0]
    HD = C // E
    G1 = b_g1.shape[0]
    CB = C - P
    NG = 3
    J = H // 2
    U = L // 2
    NQKV = 3 * C
    NW2 = 3 * C + G1
    DA = D + 1

    ctx = ExitStack()
    with ctx:
        def sb(name, shape, dt=F32):
            return ctx.enter_context(nc.sbuf_tensor(name, shape, dt))

        def pb(name, shape, dt=F32):
            return ctx.enter_context(nc.psum_tensor(name, shape, dt))

        def sem(name):
            return ctx.enter_context(nc.semaphore(name))

        def two(name, shape, dt=F32):
            return [sb(f"{name}{i}", shape, dt) for i in range(2)]

        ids_w = sb("ids_w", [P, T], I32)
        ids_t = sb("ids_t", [P, T], I32)
        type_f = sb("type_f", [P, T])
        pos_row_i = sb("pos_row_i", [P, T * P], I32)
        pos_row = sb("pos_row", [P, T * P])
        iota_p = sb("iota_p", [P, 1])
        pos_tab = sb("pos_tab", [P, C])
        type_tab = sb("type_tab", [P, 2, C])
        type_diff = sb("type_diff", [P, C])
        pos_tab0 = sb("pos_tab0", [P, C])
        pos_parts = sb("pos_parts", [P, 3, C], BF16)
        pos_rest = sb("pos_rest", [P, 1, C])
        gamma_b = sb("gamma_b", [P, C])
        beta_b = sb("beta_b", [P, C])
        ident = sb("ident", [P, P])
        ident_h = sb("ident_h", [P, P], F16)
        ident_b = sb("ident_b", [P, P], BF16)
        minus_half = sb("minus_half", [P, 2 * H])
        eps = sb("eps", [P, 3])
        own_pos = sb("own_pos", [P, NPOS], F16)
        lscale = sb("lscale", [P, H])
        lscale_min = sb("lscale_min", [P, H])
        qk_scale = sb("qk_scale", [P, 2 * H])
        wi_f = sb("wi_f", [P, 2, NQKV])
        wi_hi = sb("wi_hi", [P, 2, NQKV], F32R)
        wi_lo = sb("wi_lo", [P, 2, NQKV], F32R)
        w2_f = sb("w2_f", [P, 2, NW2])
        w2_hi = sb("w2_hi", [P, 2, NW2], F32R)
        w2_lo = sb("w2_lo", [P, 2, NW2], F32R)
        wo_f = sb("wo_f", [P, 2, C])
        wo_s = sb("wo_s", [P, 2, C])
        hs_col = sb("hs_col", [P, 2])
        wp_f = sb("wp_f", [P, 2, C])
        mm_own = sb("mm_own", [P, 2, P], F16)
        mm_sum = sb("mm_sum", [P, P], F16)
        mm_sel = sb("mm_sel", [P, J, P], F16)
        mm_lhs = sb("mm_lhs", [P, J, P], F16)
        causal = sb("causal", [P, 4, P], BF16)
        conv_c = sb("conv_c", [HD, 4])
        wg2_b = sb("wg2_b", [P, E, G1])
        bg2_b = sb("bg2_b", [P, E])

        word = sb("word", [P, T, C])
        h0 = sb("h0", [P, T, C])
        onehot = two("onehot", [P, P], BF16)
        emb_a = two("emb_a", [P, C])
        emb_b = two("emb_b", [P, C])
        st1 = two("st1", [P, 6])
        mv1 = two("mv1", [P, 2])
        ve1 = two("ve1", [P, 1])
        rs1 = two("rs1", [P, 1])
        nrm = two("nrm", [P, C])
        nrg = two("nrg", [P, C])
        st2 = two("st2", [P, 6])
        mv2 = two("mv2", [P, 2])
        ve2 = two("ve2", [P, 1])
        rs2 = two("rs2", [P, 1])
        xn = two("xn", [P, 2 * P])
        xt_hi = two("xt_hi", [P, 2, P], F32R)
        xt_lo = two("xt_lo", [P, 2, P], F32R)
        sq = two("sq", [P, 2 * C])
        ssq = two("ssq", [P, 2 * H])
        ssc = two("ssc", [P, 2 * H])
        rno = two("rno", [P, 2 * H])
        rnk = two("rnk", [P, 2 * H])
        unit = two("unit", [P, 2 * C])
        qks = two("qks", [P, 2 * H, 4 * D], F16)
        qkt = two("qkt", [P, NG, 4, P], F16)
        nmx = two("nmx", [P, P], F16)
        nmt = two("nmt", [P, P], F16)
        vnew = two("vnew", [P, C])
        vaug = two("vaug", [P, H, DA])
        et = two("et", [P, J, 2, P])
        rsum = two("rsum", [P, H])
        oa = two("oa", [P, 2 * P])
        ot = two("ot", [P, 2, P])
        h1t = two("h1t", [P, C])

        psA = pb("psA", [P, 512])
        psB = pb("psB", [P, 512])
        psC = pb("psC", [P, 512])
        psD = pb("psD", [P, 512])
        psS = pb("psS", [P, 2, 512])
        psT = pb("psT", [P, 2, 512])

        LAST = 4
        LO = LAST + 2
        s_ids = sem("ids_loaded")
        s_tabs = sem("tables_loaded")
        s_zero = sem("weights_zeroed")
        s_win = sem("w_in_loaded")
        s_w2 = sem("w2_loaded")
        s_wop = sem("w_out_loaded")
        s_misc = sem("misc_loaded")
        s_pc = sem("pool_constants")
        s_cs = sem("setup_act")
        s_cd = sem("setup_dve")
        s_word = [sem(f"word_rows_{i}") for i in range(LO + 1)]
        s_oh = sem("onehot_built")
        s_pos = sem("pos_rows_out")
        s_e1 = sem("embed_dve")
        s_ln1 = sem("rstd1_done")
        s_aff = sem("affine_done")
        s_ln2 = sem("rstd2_done")
        s_xn = sem("xn_done")
        s_nd = sem("stats2_dve")
        s_nrm = sem("embedding_normalised")
        s_xT = sem("x_transposed")
        s_hi = sem("x_hi_copied")
        s_lo = sem("x_lo_made")
        s_qkv = sem("qkv_done")
        s_sq = sem("squares_done")
        s_ss = sem("square_sums")
        s_rn = sem("rnorm_done")
        s_unit = sem("unit_done")
        s_uh = sem("unit_hi")
        s_ul = sem("unit_lo")
        s_v = sem("v_copied")
        s_va = sem("v_augmented")
        s_tr = sem("qk_transposed")
        s_qkt = sem("qkt_copied")
        s_sc = sem("scores_done")
        s_mx = sem("max_done")
        s_mT = sem("max_transposed")
        s_nmt = sem("max_copied")
        s_st = sem("scores_t_done")
        s_ex = sem("exp_done")
        s_pv = sem("pv_done")
        s_rc = sem("recip_done")
        s_oa = sem("attn_out_done")
        s_oT = sem("attn_transposed")
        s_ot = sem("attn_t_copied")
        s_pr = sem("proj_done")
        s_h1 = sem("h1_done")
        s_st1 = [sem(f"h1_stored_{i}") for i in range(2)]

        hb = word
        p_st = two("p_st", [P, 2, 6])
        p_mv = two("p_mv", [P, 2, 2])
        p_ve = two("p_ve", [P, 2])
        p_rs = two("p_rs", [P, 2])
        p_xn = two("p_xn", [P, 2, 2 * P])
        p_xh = two("p_xh", [P, 2, 2 * P], F32R)
        p_xl = two("p_xl", [P, 2, 2 * P], F32R)
        p_qk = two("p_qk", [P, 4, 2 * P])
        p_cv = two("p_cv", [HD, 2, P])
        p_v = two("p_v", [P, 2 * E, HD + 1])
        p_rl = two("p_rl", [P, 2, G1])
        p_rw = two("p_rw", [P, 2, E, G1])
        p_lg = two("p_lg", [P, 2 * E])
        p_lb = two("p_lb", [P, 2 * E])
        p_gm = two("p_gm", [P, 2])
        p_gd = two("p_gd", [P, 2 * E])
        p_ge = two("p_ge", [P, 2 * E])
        p_gs = two("p_gs", [P, 2])
        p_gr = two("p_gr", [P, 2])
        p_g = two("p_g", [P, 2 * E])
        p_mn = two("p_mn", [P, 2, 2])
        p_kp = two("p_kp", [P, 2, E])
        p_ks = two("p_ks", [P, 2])
        p_eg = two("p_eg", [P, 2 * E])
        p_ek = two("p_ek", [P, 2 * E])
        p_es = two("p_es", [P, 2])
        p_er = two("p_er", [P, 2])
        p_w = two("p_w", [P, 2 * E])
        p_nm = two("p_nm", [P, 2 * E])
        p_sh = two("p_sh", [P, 2 * E, P])
        p_ex = two("p_ex", [P, 2 * E, P])
        p_pt = two("p_pt", [P, 2 * E, P])
        p_ri = two("p_ri", [P, 2 * E])
        p_fc = two("p_fc", [P, 2 * E])
        p_y = two("p_y", [P, 2, 2 * P])
        p_yt = two("p_yt", [P, 2, 2 * P])
        p_o = two("p_o", [P, 2, C])

        q_h = [sem(f"p_rows_loaded_{i}") for i in range(4)]
        q_st = sem("p_stats")
        q_rs = sem("p_rstd")
        q_xn = sem("p_xn_done")
        q_xT = sem("p_x_transposed")
        q_hi = sem("p_x_hi")
        q_lo = sem("p_x_lo")
        q_qk = sem("p_qk_done")
        q_vg = sem("p_vg_done")
        q_qe = sem("p_qk_copied")
        q_cv = sem("p_conv")
        q_rl = sem("p_relu")
        q_vc = sem("p_v_copied")
        q_gp = sem("p_gate_pool")
        q_gd = sem("p_gate_dve")
        q_ga = sem("p_gate_act")
        q_gc = sem("p_gate_chain")
        q_ge = sem("p_gate_sums")
        q_kp = sem("p_gate_keep")
        q_sc = sem("p_scores")
        q_nm = sem("p_max")
        q_sh = sem("p_shifted")
        q_ex = sem("p_exp")
        q_pT = sem("p_p_transposed")
        q_pt = sem("p_pt_copied")
        q_pv = sem("p_pv")
        q_fc = sem("p_factor")
        q_y = sem("p_y_done")
        q_yT = sem("p_y_transposed")
        q_yt = sem("p_yt_copied")
        q_pr = sem("p_proj")
        q_o = sem("p_out_made")
        s_out = [sem(f"out_stored_{i}") for i in range(2)]

        pX = psA
        pQ = psT
        pV = psB
        pS = psS
        pP = [psC, psD]

        block = ctx.enter_context(nc.Block())

        def wait(eng, s, value):
            if not isinstance(value, int) or value > 0:
                eng.wait_ge(s, value)

        def steps(eng, stages, n, last, enter=None):
            lo = last + 2
            hi = lo + (n - lo) // 2 * 2

            def one(s):
                stages(s, s % 2, lambda off: 0 <= s - off < n)

            for s in range(lo):
                one(s)
            if enter:
                enter()
            with eng.Fori(lo, hi - 1, 2) as s:
                for k in range(2):
                    stages(s + k, (lo + k) % 2, lambda off: True)
            for s in range(hi, n + last):
                one(s)

        qk3 = psC[:, 0:2 * C].rearrange("p (h d) -> p h d", d=D)
        trb = psB[:, 256:512].bitcast(F16)
        mtb = psA[:, 256:320].bitcast(F16)
        pvo = psD[:, 256:256 + H * DA].rearrange("p (h d) -> p h d", d=DA)

        @block.sync
        def _(sp):
            sp.dma_start(ids_w[:], word_ids).then_inc(s_ids, 16)
            sp.dma_start(pos_row_i[:], pos_ids.partition_broadcast(P)).then_inc(s_tabs, 16)
            sp.dma_start(pos_tab[:], pos_emb).then_inc(s_tabs, 16)
            sp.dma_start(type_tab[:].rearrange("p a c -> p (a c)"),
                         type_emb.rearrange("a c -> (a c)").partition_broadcast(P)).then_inc(s_tabs, 16)
            sp.dma_start(ids_t[:], type_ids).then_inc(s_tabs, 16)
            sp.dma_start(wi_f[:, 0, :], w_in[0:P, :]).then_inc(s_win, 16)
            sp.wait_ge(s_zero, 1)
            sp.dma_start(wi_f[0:CB, 1, :], w_in[P:C, :]).then_inc(s_win, 16)
            sp.dma_start(wi_f[CB:CB + 1, 1, :], b_in.unsqueeze(0)).then_inc(s_win, 16)
            sp.wait_ge(s_zero, 3)
            sp.dma_start(wo_f[:, 0, :], w_out[0:P, :]).then_inc(s_wop, 16)
            sp.dma_start(wo_f[0:CB, 1, :], w_out[P:C, :]).then_inc(s_wop, 16)
            sp.dma_start(wo_f[CB:CB + 1, 1, :], b_out.unsqueeze(0)).then_inc(s_wop, 16)
            hs16 = head_scale.rearrange("h a b -> h (a b)")
            sp.dma_start(hs_col[:, 0:1], hs16[0:P // D, :].unsqueeze(1).broadcast_to([P // D, D, 1])).then_inc(s_wop, 16)
            sp.dma_start(hs_col[0:CB, 1:2], hs16[P // D:H, :].unsqueeze(1).broadcast_to([H - P // D, D, 1])).then_inc(s_wop, 16)
            sp.dma_start(wp_f[:, 0, :], w_p[0:P, :]).then_inc(s_wop, 16)
            sp.dma_start(wp_f[0:CB, 1, :], w_p[P:C, :]).then_inc(s_wop, 16)
            sp.dma_start(wp_f[CB:CB + 1, 1, :], b_p.unsqueeze(0)).then_inc(s_wop, 16)

            def store_h1(t, b):
                wait(sp, s_h1, t + 1)
                sp.dma_start(h_scratch[bass.ts(t, P), :], h1t[b][:]).then_inc(s_st1[b], 16)

            def stages(s, b, on):
                if on(4):
                    store_h1(s - 4, b)

            steps(sp, stages, T, LAST)
            for b in range(2):
                sp.wait_ge(s_st1[b], 16 * (T // 2))
            src = h_scratch.rearrange("(n l) c -> n l c", l=L)
            for i in range(4):
                sp.dma_start(hb[:, 4 * i:4 * i + 4, :], src[:, 4 * i:4 * i + 4, :]).then_inc(q_h[i], 16)

            def store_out(u, b):
                wait(sp, q_o, u + 1)
                sp.dma_start(out[bass.ts(u, 2), :, :].rearrange("l n c -> n l c"), p_o[b][:]).then_inc(s_out[b], 16)

            def stages2(s, b, on):
                if on(1):
                    store_out(s - 1, 1 - b)

            steps(sp, stages2, U, 1)
            for b in range(2):
                sp.wait_ge(s_out[b], 16 * (U // 2))

        @block.gpsimd
        def _(pool):
            pool.iota(iota_p[:], pattern=[[0, 1]], base=0, channel_multiplier=1,
                      allow_small_or_imprecise_dtypes=True).then_inc(s_pc, 1)
            pool.memset(ident[:], 0.0).then_inc(s_pc, 1)
            pool.wait_ge(s_pc, 2)
            pool.affine_select(out=ident[:], in_=ident[:], compare_op=ALU.not_equal, fill=1.0, base=0,
                               pattern=[[-1, P]], channel_multiplier=1).then_inc(s_pc, 1)
            pool.wait_ge(s_ids, 16)

            def gather(t):
                pool.indirect_dma_start(
                    word[:, t, :], None, word_emb,
                    bass.IndirectOffsetOnAxis(ids_w[:, t:t + 1].bitcast(U32), 0)).then_inc(s_word[min(t, LO)], 16)

            for t in range(3):
                gather(t)
            pool.wait_ge(s_pc, 3)
            pool.tensor_copy(ident_h[:], ident[:]).then_inc(s_pc, 1)
            pool.tensor_copy(ident_b[:], ident[:]).then_inc(s_pc, 1)
            pool.memset(own_pos[:], 1.0).then_inc(s_pc, 1)
            pool.wait_ge(s_pc, 6)
            pool.affine_select(out=own_pos[:], in_=own_pos[:], compare_op=ALU.is_ge, fill=0.0, base=0,
                               pattern=[[-L, NPOS]], channel_multiplier=1).then_inc(s_pc, 1)
            pool.wait_ge(s_pc, 7)
            pool.affine_select(out=own_pos[:], in_=own_pos[:], compare_op=ALU.is_ge, fill=0.0, base=L - 1,
                               pattern=[[L, NPOS]], channel_multiplier=-1).then_inc(s_pc, 1)
            pool.wait_ge(s_pc, 8)
            pool.wait_ge(s_zero, 4)
            for b in range(2):
                for h0_, f in ((0, MASK_Q), (H, MASK_K)):
                    pool.tensor_scalar(qks[b][:, h0_:h0_ + H, 3 * D:3 * D + NPOS],
                                       own_pos[:].unsqueeze(1).broadcast_to([P, H, NPOS]), f, None, ALU.mult).then_inc(s_pc, 1)
                pool.memset(qks[b][:, 0:H, 3 * D + NPOS:3 * D + NPOS + 1], -MASK_Q).then_inc(s_pc, 1)
                pool.memset(qks[b][:, H:2 * H, 3 * D + NPOS:3 * D + NPOS + 1], MASK_K).then_inc(s_pc, 1)
                for p in range(2):
                    o = 64 * p + J
                    pool.tensor_scalar(nmx[b][:, o:o + NPOS], own_pos[:], MASK_Q, None, ALU.mult).then_inc(s_pc, 1)
                    pool.memset(nmx[b][:, o + NPOS:o + NPOS + 1], -MASK_Q).then_inc(s_pc, 1)
            def late_constants():
                pool.memset(mm_own[:], MASK_K).then_inc(s_pc, 1)
                pool.memset(mm_sel[:], 0.0).then_inc(s_pc, 1)
                c0 = 8 + 2 * 8
                for p in range(2):
                    r0 = 64 * p + J
                    pool.wait_ge(s_pc, c0 + 2 + 4 * p)
                    pool.affine_select(out=mm_own[:, p, :], in_=mm_own[:, p, :], compare_op=ALU.is_ge, fill=0.0,
                                       base=L * r0, pattern=[[1, P]], channel_multiplier=-L).then_inc(s_pc, 1)
                    pool.affine_select(out=mm_sel[:], in_=mm_sel[:], compare_op=ALU.not_equal, fill=1.0,
                                       base=-64 * p, pattern=[[-1, J], [0, P]], channel_multiplier=1).then_inc(s_pc, 1)
                    pool.wait_ge(s_pc, c0 + 4 + 4 * p)
                    pool.affine_select(out=mm_own[:, p, :], in_=mm_own[:, p, :], compare_op=ALU.is_ge, fill=0.0,
                                       base=L - 1 - L * r0, pattern=[[-1, P]], channel_multiplier=L).then_inc(s_pc, 1)
                    pool.wait_ge(s_pc, c0 + 5 + 4 * p)
                    pool.affine_select(out=mm_own[:, p, :], in_=mm_own[:, p, :], compare_op=ALU.not_equal, fill=MASK_K,
                                       base=-(r0 + NPOS), pattern=[[0, P]], channel_multiplier=1).then_inc(s_pc, 1)
                pool.wait_ge(s_pc, c0 + 10)
                pool.tensor_tensor(mm_sum[:], mm_own[:, 0, :], mm_own[:, 1, :], ALU.add).then_inc(s_pc, 1)
                pool.wait_ge(s_pc, c0 + 11)
                pool.tensor_tensor(mm_lhs[:], mm_sel[:], mm_sum[:].unsqueeze(1).broadcast_to([P, J, P]), ALU.add).then_inc(s_pc, 1)
                pool.memset(causal[:], 0.0).then_inc(s_pc, 1)
                pool.wait_ge(s_pc, c0 + 13)
                pool.affine_select(out=causal[:], in_=causal[:], compare_op=ALU.is_ge, fill=CAUSAL_OFF, base=0,
                                   pattern=[[0, 4], [-1, P]], channel_multiplier=1).then_inc(s_pc, 1)

            def rstd(ve, rs, mv, eps, s_own, t):
                pool.tensor_tensor(ve[:], mv[:, 1:2], eps, ALU.add).then_inc(s_own, 1)
                wait(pool, s_own, 2 * t + 1)
                pool.tensor_tensor(rs[:], ve[:], minus_half[:, 0:1], ALU.pow).then_inc(s_own, 1)

            def affine(t, b):
                wait(pool, s_nrm, t + 1)
                pool.tensor_tensor(nrg[b][:], nrm[b][:], gamma_b[:], ALU.mult).then_inc(s_aff, 1)
                wait(pool, s_aff, 2 * t + 1)
                pool.tensor_tensor(h0[:, bass.ds(t, 1), :].rearrange("p a c -> p (a c)"), nrg[b][:], beta_b[:], ALU.add).then_inc(s_aff, 1)

            def rnorm(t, b):
                wait(pool, s_ss, 2 * t + 2)
                pool.tensor_tensor(rno[b][:], ssc[b][:], minus_half[:], ALU.pow).then_inc(s_rn, 1)
                wait(pool, s_rn, 2 * t + 1)
                wait(pool, s_unit, t - 1)
                pool.tensor_tensor(rnk[b][:], rno[b][:], qk_scale[:], ALU.mult).then_inc(s_rn, 1)

            def unit_lo(t, b):
                wait(pool, s_uh, 2 * t + 2)
                u = unit[b][:].rearrange("p (h d) -> p h d", d=D)
                pool.tensor_tensor(qks[b][:, 0:H, D:2 * D], u[:, 0:H, :], qks[b][:, 0:H, 0:D], ALU.subtract).then_inc(s_ul, 1)
                pool.tensor_tensor(qks[b][:, H:2 * H, 2 * D:3 * D], u[:, H:2 * H, :], qks[b][:, H:2 * H, 0:D], ALU.subtract).then_inc(s_ul, 1)

            pool.wait_ge(s_misc, 16 * 7)
            pool.wait_ge(s_cd, 5)

            def stages(s, b, on):
                if on(1):
                    wait(pool, s_nd, 2 * s)
                    rstd(ve2[1 - b], rs2[1 - b], mv2[1 - b], eps[:, 0:1], s_ln2, s - 1)
                if on(2):
                    rnorm(s - 2, b)
                if on(0):
                    wait(pool, s_e1, 4 * s + 4)
                    rstd(ve1[b], rs1[b], mv1[b], eps[:, 2:3], s_ln1, s)
                if on(2):
                    unit_lo(s - 2, b)
                if on(0):
                    affine(s, b)
                if isinstance(s, int) and s < LO:
                    for t in range(3 + 3 * s, min(6 + 3 * s, T)):
                        gather(t)
                    if s == 0:
                        late_constants()

            steps(pool, stages, T, LAST)

            def gate(u, b):
                wait(pool, q_rl, u + 1)
                pool.tensor_tensor(p_rw[b][:], p_rl[b][:].unsqueeze(2).broadcast_to([P, 2, E, G1]),
                                   wg2_b[:].unsqueeze(1).broadcast_to([P, 2, E, G1]), ALU.mult).then_inc(q_gp, 1)

            def rstd2(u, b):
                wait(pool, q_st, 4 * u + 4)
                pool.tensor_tensor(p_ve[b][:], p_mv[b][:, :, 1:2].rearrange("p a o -> p (a o)"), eps[:, 0:2], ALU.add).then_inc(q_rs, 1)
                wait(pool, q_rs, 2 * u + 1)
                pool.tensor_tensor(p_rs[b][:], p_ve[b][:], minus_half[:, 0:2], ALU.pow).then_inc(q_rs, 1)

            def stages2(s, b, on):
                if on(0):
                    rstd2(s, b)
                    gate(s, b)

            steps(pool, stages2, U, 1)

        @block.scalar
        def _(act):
            act.dma_start(gamma_b[:], gamma.partition_broadcast(P)).then_inc(s_misc, 16)
            act.dma_start(beta_b[:], beta.partition_broadcast(P)).then_inc(s_misc, 16)
            act.dma_start(lscale[:], logit_scale.rearrange("h a b -> (h a b)").partition_broadcast(P)).then_inc(s_misc, 16)
            act.dma_start(conv_c[:, 0:3], conv_w.rearrange("c a k -> c (a k)")).then_inc(s_misc, 16)
            act.dma_start(conv_c[:, 3:4], conv_b.unsqueeze(1)).then_inc(s_misc, 16)
            act.dma_start(wg2_b[:].rearrange("p e g -> p (e g)"), w_g2.rearrange("e g -> (e g)").partition_broadcast(P)).then_inc(s_misc, 16)
            act.dma_start(bg2_b[:], b_g2.partition_broadcast(P)).then_inc(s_misc, 16)
            act.wait_ge(s_zero, 2)
            for dst, src in ((slice(0, 2 * C), w_qk), (slice(3 * C, NW2), w_g1)):
                act.dma_start(w2_f[:, 0, dst], src[0:P, :]).then_inc(s_w2, 16)
                act.dma_start(w2_f[0:CB, 1, dst], src[P:C, :]).then_inc(s_w2, 16)
            for e in range(E):
                dst = slice(2 * C + e * HD, 2 * C + (e + 1) * HD)
                act.dma_start(w2_f[:, 0, dst], w_v[e, 0:P, :]).then_inc(s_w2, 16)
                act.dma_start(w2_f[0:CB, 1, dst], w_v[e, P:C, :]).then_inc(s_w2, 16)
            act.dma_start(w2_f[CB:CB + 1, 1, 0:2 * C], b_qk.unsqueeze(0)).then_inc(s_w2, 16)
            act.dma_start(w2_f[CB:CB + 1, 1, 2 * C:3 * C], b_v.rearrange("e d -> (e d)").unsqueeze(0)).then_inc(s_w2, 16)
            act.dma_start(w2_f[CB:CB + 1, 1, 3 * C:NW2], b_g1.unsqueeze(0)).then_inc(s_w2, 16)
            act.wait_ge(s_tabs, 64)
            act.activation(pos_row[:], pos_row_i[:], ACT.Copy).then_inc(s_cs, 1)
            act.wait_ge(s_cd, 1)
            act.activation(qk_scale[:, 0:H], lscale_min[:], ACT.Exp).then_inc(s_cs, 1)
            act.wait_ge(s_win, 48)
            act.activation(wi_hi[:], wi_f[:], ACT.Copy).then_inc(s_cs, 1)

            def late_setup():
                act.wait_ge(s_w2, 16 * 13)
                act.activation(w2_hi[:], w2_f[:], ACT.Copy).then_inc(s_cs, 1)

            def x_hi(t, b):
                wait(act, s_xT, t + 1)
                wait(act, s_qkv, t - 1)
                act.activation(xt_hi[b][:].rearrange("p a n -> p (a n)"), psB[:, 0:2 * P], ACT.Copy).then_inc(s_hi, 1)

            def squares(t, b):
                wait(act, s_qkv, t + 1)
                wait(act, s_ss, 2 * (t - 1) - 1)
                act.activation(sq[b][:], psC[:, 0:2 * C], ACT.Square).then_inc(s_sq, 1)
                wait(act, s_va, t - 1)
                act.activation(vnew[b][:], psD[:, 0:C], ACT.Copy).then_inc(s_v, 1)

            def unit_hi(t, b):
                wait(act, s_unit, t + 1)
                wait(act, s_tr, 3 * (t - 1))
                u = unit[b][:].rearrange("p (h d) -> p h d", d=D)
                q = qks[b][:, 0:H, :].rearrange("p h (a x) -> p h a x", x=2 * D)[:, :, :, 0:D]
                k = qks[b][:, H:2 * H, 0:2 * D].rearrange("p h (a x) -> p h a x", x=D)
                if isinstance(t, int) and t == 0:
                    act.wait_ge(s_pc, 24)
                act.activation(qks[b][:, 0:H, 0:D], u[:, 0:H, :], ACT.Copy)
                act.activation(qks[b][:, 0:H, 2 * D:3 * D], u[:, 0:H, :], ACT.Copy).then_inc(s_uh, 1)
                act.activation(k, u[:, H:2 * H, :].unsqueeze(2).broadcast_to([P, H, 2, D]), ACT.Copy).then_inc(s_uh, 1)

            def copy_qkt(t, b, g):
                wait(act, s_tr, 3 * t + g + 1)
                wait(act, s_st, 3 * (t - 2) + g + 1)
                act.activation(qkt[b][:, g, :, :].rearrange("p a n -> p (a n)"), trb, ACT.Copy).then_inc(s_qkt, 1)

            def copy_max(t, b):
                wait(act, s_mT, t + 1)
                wait(act, s_st, 3 * (t - 1))
                act.activation(nmt[b][:], mtb, ACT.Copy).then_inc(s_nmt, 1)

            def exps(t, b, g):
                wait(act, s_st, 3 * t + g + 1)
                wait(act, s_pv, 3 * (t - 2) + g + 1)
                act.activation(et[b][:, 2 * g:2 * g + 2, :, :].rearrange("q j p c -> q p j c"),
                               psT[:, :, 0:2 * P].rearrange("q p (j c) -> q p j c", j=2),
                               ACT.Exp, scale=1.0 / KEY_SCALE).then_inc(s_ex, 1)

            def copy_ot(t, b):
                wait(act, s_oT, t + 1)
                wait(act, s_pr, t - 1)
                act.activation(ot[b][:].rearrange("p a n -> p (a n)"), psB[:, 0:2 * P], ACT.Copy).then_inc(s_ot, 1)

            def stages(s, b, on):
                for g in range(NG):
                    if on(4):
                        exps(s - 4, b, g)
                    if on(3):
                        copy_qkt(s - 3, 1 - b, g)
                if on(1):
                    x_hi(s - 1, 1 - b)
                if on(2):
                    unit_hi(s - 2, b)
                if on(1):
                    squares(s - 1, 1 - b)
                if on(3):
                    copy_max(s - 3, 1 - b)
                if on(4):
                    copy_ot(s - 4, b)
                if isinstance(s, int) and s == 1:
                    late_setup()

            steps(act, stages, T, LAST)

            def p_hi(u, b):
                wait(act, q_xT, u + 1)
                wait(act, q_vg, u - 1)
                act.activation(p_xh[b][:].rearrange("p a n -> p (a n)"), pX[:], ACT.Copy).then_inc(q_hi, 1)

            def p_qkcopy(u, b):
                wait(act, q_qk, u + 1)
                wait(act, q_sc, u - 1)
                act.activation(p_qk[b][:, 0:2, :], pQ[:, 0, :].rearrange("p (a n) -> p a n", a=2), ACT.Copy).then_inc(q_qe, 1)
                act.activation(p_qk[b][0:HD, 2, :], pQ[0:HD, 1, 0:2 * P], ACT.Copy).then_inc(q_qe, 1)
                act.activation(p_qk[b][0:HD, 3, :], pQ[HD:P, 1, 0:2 * P], ACT.Copy).then_inc(q_qe, 1)

            def p_relu(u, b):
                wait(act, q_vg, u + 1)
                wait(act, q_gp, u - 1)
                vg = pV[:, 0:2 * (C + G1)].rearrange("p (a n) -> p a n", a=2)
                act.activation(p_rl[b][:], vg[:, :, C:C + G1], ACT.Relu).then_inc(q_rl, 1)

            def p_gate(u, b):
                wait(act, q_gd, 7 * u + 3)
                act.activation(p_ge[b][:], p_gd[b][:], ACT.Exp).then_inc(q_ga, 1)
                wait(act, q_gd, 7 * u + 6)
                act.activation(p_eg[b][:], p_g[b][:], ACT.Exp).then_inc(q_ga, 1)

            def p_exp(u, b):
                wait(act, q_sh, u + 1)
                wait(act, q_pT, u - 1)
                act.activation(p_ex[b][:], p_sh[b][:], ACT.Exp, scale=float(HD) ** -0.5).then_inc(q_ex, 1)

            def p_ptcopy(u, b):
                wait(act, q_pT, u + 1)
                wait(act, q_pv, u - 1)
                for i in range(2):
                    act.activation(p_pt[b][:, 3 * i:3 * i + 3, :].rearrange("p a n -> p (a n)"), pP[i][:, 0:3 * P], ACT.Copy).then_inc(q_pt, 1)

            def p_ytcopy(u, b):
                wait(act, q_yT, u + 1)
                wait(act, q_pr, u - 1)
                act.activation(p_yt[b][:].rearrange("p a n -> p (a n)"), pX[:], ACT.Copy).then_inc(q_yt, 1)

            def stages2(s, b, on):
                if on(0):
                    p_hi(s, b)
                if on(1):
                    p_exp(s - 1, 1 - b)
                    p_ptcopy(s - 1, 1 - b)
                if on(0):
                    p_qkcopy(s, b)
                    p_relu(s, b)
                    p_gate(s, b)
                if on(1):
                    p_ytcopy(s - 1, 1 - b)

            steps(act, stages2, U, 1)

        @block.vector
        def _(dve):
            for b in range(2):
                dve.memset(qks[b][:].rearrange("p h x -> p (h x)").bitcast(U32), 0)
                dve.memset(nmx[b][:].bitcast(U32), 0)
            dve.memset(eps[:, 0:2], 1e-5)
            dve.memset(eps[:, 2:3], 1e-12)
            dve.memset(wi_f[:, 1, :], 0.0).then_inc(s_zero, 1)
            dve.memset(w2_f[:, 1, :], 0.0).then_inc(s_zero, 1)
            dve.memset(wo_f[:, 1, :], 0.0)
            dve.memset(wp_f[:, 1, :], 0.0)
            dve.memset(hs_col[:], 1.0).then_inc(s_zero, 1)
            dve.memset(minus_half[:], -0.5).then_inc(s_zero, 1)
            dve.wait_ge(s_misc, 16 * 7)
            dve.tensor_scalar(lscale_min[:], lscale[:], LOG_SCALE_MAX, None, ALU.min).then_inc(s_cd, 1)
            dve.memset(qk_scale[:, H:2 * H], KEY_SCALE).then_inc(s_cd, 1)
            dve.wait_ge(s_tabs, 64)
            dve.tensor_tensor(type_diff[:], type_tab[:, 1, :], type_tab[:, 0, :], ALU.subtract).then_inc(s_cd, 1)
            dve.tensor_tensor(pos_tab0[:], pos_tab[:], type_tab[:, 0, :], ALU.add).then_inc(s_cd, 1)
            dve.tensor_copy(type_f[:], ids_t[:]).then_inc(s_cd, 1)
            dve.wait_ge(s_cd, 4)
            dve.tensor_copy(pos_parts[:, 0, :], pos_tab0[:]).then_inc(s_cd, 1)
            dve.wait_ge(s_cd, 6)
            dve.tensor_tensor(pos_rest[:, 0, :], pos_tab0[:], pos_parts[:, 0, :], ALU.subtract).then_inc(s_cd, 1)
            dve.wait_ge(s_cd, 7)
            dve.tensor_copy(pos_parts[:, 1, :], pos_rest[:, 0, :]).then_inc(s_cd, 1)
            dve.wait_ge(s_cd, 8)
            dve.tensor_tensor(pos_parts[:, 2, :], pos_rest[:, 0, :], pos_parts[:, 1, :], ALU.subtract).then_inc(s_cd, 1)
            for b in range(2):
                for tile in (xn[b], oa[b]):
                    dve.memset(tile[:, C:C + 1], 1.0)
                    dve.memset(tile[:, C + 1:2 * P], 0.0)
                for tile in (p_xn[b], p_y[b]):
                    dve.memset(tile[:, :, C:C + 1], 1.0)
                    dve.memset(tile[:, :, C + 1:2 * P], 0.0)
                dve.memset(vaug[b][:, :, D:DA], 1.0)
                dve.memset(p_v[b][:, :, HD:HD + 1], 1.0).then_inc(s_cd, 1)
            dve.wait_ge(s_cs, 3)
            dve.tensor_tensor(wi_lo[:], wi_f[:], wi_hi[:].bitcast(F32), ALU.subtract).then_inc(s_cd, 1)

            def late_setup():
                dve.wait_ge(s_wop, 16 * 8)
                for c in range(2):
                    dve.tensor_scalar(wo_s[:, c, :], wo_f[:, c, :], hs_col[:, c:c + 1], None, ALU.mult).then_inc(s_cd, 1)
                dve.wait_ge(s_cs, 4)
                dve.tensor_tensor(w2_lo[:], w2_f[:], w2_hi[:].bitcast(F32), ALU.subtract).then_inc(s_cd, 1)

            def build_onehot(t, b):
                wait(dve, s_pos, t - 1)
                dve.tensor_scalar(onehot[b][:], pos_row[:, bass.ts(t, P)], iota_p[:, 0:1], None, ALU.is_equal).then_inc(s_oh, 1)

            def embed(t, b):
                if isinstance(t, int) and t < LO:
                    dve.wait_ge(s_word[t], 16)
                if not isinstance(t, int) or t >= 1:
                    wait(dve, s_nd, 2 * (t - 1) + 1)
                dve.scalar_tensor_tensor(emb_a[b][:], type_diff[:], type_f[:, bass.ds(t, 1)],
                                         word[:, bass.ds(t, 1), :].rearrange("p a c -> p (a c)"), ALU.mult, ALU.add).then_inc(s_e1, 1)
                if not isinstance(t, int) or t >= 1:
                    stats2_end(t - 1, 1 - b)
                wait(dve, s_e1, 4 * t + 1)
                wait(dve, s_pos, t + 1)
                dve.tensor_tensor(emb_b[b][:], emb_a[b][:], psA[:, 0:C], ALU.add).then_inc(s_e1, 1)
                wait(dve, s_e1, 4 * t + 2)
                dve.bn_stats(st1[b][:], emb_b[b][:]).then_inc(s_e1, 1)

            def embed_end(t, b):
                if isinstance(t, int):
                    wait(dve, s_e1, 4 * t + 3)
                dve.bn_aggr(mv1[b][:], st1[b][:]).then_inc(s_e1, 1)

            def normalise(t, b):
                wait(dve, s_ln1, 2 * t + 2)
                wait(dve, s_aff, 2 * (t - 2) + 1)
                dve.tensor_scalar(nrm[b][:], emb_b[b][:], mv1[b][:, 0:1], rs1[b][:, 0:1], ALU.subtract, ALU.mult).then_inc(s_nrm, 1)

            def stats2(t, b):
                wait(dve, s_aff, 2 * t + 2)
                wait(dve, s_ln2, 2 * t - 2)
                dve.bn_stats(st2[b][:], h0[:, bass.ds(t, 1), :].rearrange("p a c -> p (a c)")).then_inc(s_nd, 1)

            def stats2_end(t, b):
                if isinstance(t, int):
                    wait(dve, s_nd, 2 * t + 1)
                dve.bn_aggr(mv2[b][:], st2[b][:]).then_inc(s_nd, 1)

            def normalise2(t, b, more=None):
                if more:
                    more()
                wait(dve, s_ln2, 2 * t + 2)
                wait(dve, s_xT, t - 1)
                dve.tensor_scalar(xn[b][:, 0:C], h0[:, bass.ds(t, 1), :].rearrange("p a c -> p (a c)"), mv2[b][:, 0:1], rs2[b][:, 0:1],
                                  ALU.subtract, ALU.mult).then_inc(s_xn, 1)

            def x_lo(t, b):
                wait(dve, s_hi, t + 1)
                dve.tensor_tensor(xt_lo[b][:].rearrange("p a n -> p (a n)"), psB[:, 0:2 * P],
                                  xt_hi[b][:].bitcast(F32).rearrange("p a n -> p (a n)"), ALU.subtract).then_inc(s_lo, 1)

            def square_sums(t, b):
                wait(dve, s_sq, t + 1)
                dve.tensor_reduce(ssq[b][:], sq[b][:].rearrange("p (h d) -> p h d", d=D), AX.X, ALU.add).then_inc(s_ss, 1)
                wait(dve, s_ss, 2 * t + 1)
                dve.tensor_scalar(ssc[b][:], ssq[b][:], 1e-24, None, ALU.max).then_inc(s_ss, 1)

            def units(t, b):
                wait(dve, s_rn, 2 * t + 2)
                wait(dve, s_ul, 2 * (t - 1))
                dve.tensor_tensor(unit[b][:].rearrange("p (h d) -> p h d", d=D), qk3,
                                  rnk[b][:].unsqueeze(2).broadcast_to([P, 2 * H, D]), ALU.mult).then_inc(s_unit, 1)

            def augment_v(t, b):
                wait(dve, s_v, t + 1)
                wait(dve, s_pv, 3 * (t - 1))
                dve.tensor_copy(vaug[b][:, :, 0:D], vnew[b][:].rearrange("p (h d) -> p h d", d=D)).then_inc(s_va, 1)

            def maxima(t, b, g):
                wait(dve, s_sc, 3 * t + g + 1)
                wait(dve, s_mT, t - 1)
                if isinstance(t, int) and t == 0:
                    dve.wait_ge(s_pc, 24)
                dst = nmx[b][:].rearrange("q (p x) -> q p x", p=2)[:, :, 2 * g:2 * g + 2]
                dve.tensor_reduce(dst, psS[:, :, 0:2 * P].rearrange("q p (j c) -> q p j c", j=2), AX.X, ALU.max,
                                  negate=True).then_inc(s_mx, 1)

            def attn_out(t, b):
                wait(dve, s_pv, 3 * t + 3)
                dve.reciprocal(rsum[b][:].unsqueeze(2), pvo[:, :, D:DA]).then_inc(s_rc, 1)
                wait(dve, s_rc, t + 1)
                wait(dve, s_oT, t - 1)
                dve.tensor_tensor(oa[b][:, 0:C].rearrange("p (h d) -> p h d", d=D), pvo[:, :, 0:D],
                                  rsum[b][:].unsqueeze(2).broadcast_to([P, H, D]), ALU.mult).then_inc(s_oa, 1)

            def residual(t, b):
                wait(dve, s_pr, t + 1)
                if not isinstance(t, int) or t >= 2:
                    wait(dve, s_st1[b], (t - b) * 8)
                dve.tensor_tensor(h1t[b][:], psA[:, 0:C], h0[:, bass.ds(t, 1), :].rearrange("p a c -> p (a c)"), ALU.add).then_inc(s_h1, 1)

            dve.wait_ge(s_pc, 1)
            dve.wait_ge(s_cs, 2)
            dve.wait_ge(s_cd, 12)

            def stages(s, b, on):
                if on(0):
                    build_onehot(s, b)
                if on(1):
                    stats2(s - 1, 1 - b)
                if on(0):
                    embed(s, b)
                elif on(1):
                    stats2_end(s - 1, 1 - b)
                if on(1):
                    normalise2(s - 1, 1 - b, (lambda: wait(dve, s_e1, 4 * s + 3)) if on(0) else None)
                if on(0):
                    embed_end(s, b)
                if on(3):
                    maxima(s - 3, 1 - b, 0)
                    augment_v(s - 3, 1 - b)
                    maxima(s - 3, 1 - b, 1)
                if on(4):
                    attn_out(s - 4, b)
                if on(1):
                    x_lo(s - 1, 1 - b)
                if on(3):
                    maxima(s - 3, 1 - b, 2)
                if on(2):
                    units(s - 2, b)
                if on(0):
                    normalise(s, b)
                if on(1):
                    square_sums(s - 1, 1 - b)
                if on(4):
                    residual(s - 4, b)
                if isinstance(s, int) and s == 1:
                    late_setup()

            steps(dve, stages, T, LAST, lambda: dve.wait_ge(s_word[LO], 16 * (T - LO)))

            def p_stats(u, b):
                if isinstance(u, int):
                    dve.wait_ge(q_h[u // 2], 16)
                for a in range(2):
                    dve.bn_stats(p_st[b][:, a, :], hb[:, bass.ds(2 * u + a, 1), :].rearrange("p a c -> p (a c)")).then_inc(q_st, 1)

            def p_stats_end(u, b):
                for a in range(2):
                    if isinstance(u, int):
                        wait(dve, q_st, 4 * u + 1 + a)
                    dve.bn_aggr(p_mv[b][:, a, :], p_st[b][:, a, :]).then_inc(q_st, 1)

            def p_norm(u, b):
                wait(dve, q_rs, 2 * u + 2)
                wait(dve, q_xT, u - 1)
                for a in range(2):
                    dve.tensor_scalar(p_xn[b][:, a, 0:C], hb[:, bass.ds(2 * u + a, 1), :].rearrange("p a c -> p (a c)"), p_mv[b][:, a, 0:1],
                                      p_rs[b][:, a:a + 1], ALU.subtract, ALU.mult).then_inc(q_xn, 1)

            def p_lo(u, b):
                wait(dve, q_hi, u + 1)
                dve.tensor_tensor(p_xl[b][:].rearrange("p a n -> p (a n)"), pX[:],
                                  p_xh[b][:].bitcast(F32).rearrange("p a n -> p (a n)"), ALU.subtract).then_inc(q_lo, 1)

            def p_vcopy(u, b):
                wait(dve, q_rl, u + 1)
                wait(dve, q_pv, u - 1)
                vg = pV[:, 0:2 * (C + G1)].rearrange("p (a n) -> p a n", a=2)
                dve.tensor_copy(p_v[b][:, :, 0:HD].rearrange("p (a e) d -> p a e d", a=2),
                                vg[:, :, 0:C].rearrange("p a (e d) -> p a e d", e=E)).then_inc(q_vc, 1)

            def p_conv(u, b):
                wait(dve, q_qe, 3 * u + 1)
                q0 = p_qk[b][0:HD, 0, :].rearrange("p (a n) -> p a n", a=2)
                c = p_cv[b]
                wait(dve, q_sc, u - 1)
                dve.tensor_scalar(c[:], q0, conv_c[:, 1:2], conv_c[:, 3:4], ALU.mult, ALU.add).then_inc(q_cv, 1)
                wait(dve, q_cv, 3 * u + 1)
                dve.scalar_tensor_tensor(c[:, :, 1:P], q0[:, :, 0:P - 1], conv_c[:, 0:1], c[:, :, 1:P], ALU.mult, ALU.add).then_inc(q_cv, 1)
                wait(dve, q_cv, 3 * u + 2)
                dve.scalar_tensor_tensor(c[:, :, 0:P - 1], q0[:, :, 1:P], conv_c[:, 2:3], c[:, :, 0:P - 1], ALU.mult, ALU.add).then_inc(q_cv, 1)

            def bc(x):
                return x.unsqueeze(2).broadcast_to([P, 2, E])

            def three(x):
                return x.rearrange("p (a e) -> p a e", e=E)

            def p_gate(u, b):
                n = 7 * u
                wait(dve, q_gp, u + 1)
                dve.tensor_reduce(p_lg[b][:], p_rw[b][:].rearrange("p a e g -> p (a e) g"), AX.X, ALU.add).then_inc(q_gd, 1)
                wait(dve, q_gd, n + 1)
                dve.tensor_tensor(three(p_lb[b][:]), three(p_lg[b][:]), bg2_b[:].unsqueeze(1).broadcast_to([P, 2, E]), ALU.add).then_inc(q_gc, 1)
                wait(dve, q_gc, 3 * u + 1)
                dve.tensor_reduce(p_gm[b][:], three(p_lb[b][:]), AX.X, ALU.max, negate=True).then_inc(q_gd, 1)
                wait(dve, q_gd, n + 2)
                dve.tensor_tensor(three(p_gd[b][:]), three(p_lb[b][:]), bc(p_gm[b][:]), ALU.add).then_inc(q_gd, 1)

            def p_gate2(u, b):
                n = 7 * u
                wait(dve, q_ga, 2 * u + 1)
                dve.tensor_reduce(p_gs[b][:], three(p_ge[b][:]), AX.X, ALU.add).then_inc(q_gd, 1)
                wait(dve, q_gd, n + 4)
                dve.reciprocal(p_gr[b][:], p_gs[b][:]).then_inc(q_gd, 1)
                wait(dve, q_gd, n + 5)
                dve.tensor_tensor(three(p_g[b][:]), three(p_ge[b][:]), bc(p_gr[b][:]), ALU.mult).then_inc(q_gd, 1)

            def p_gate3(u, b):
                g3 = three(p_g[b][:])
                wait(dve, q_gd, 7 * u + 6)
                dve.tensor_tensor(p_mn[b][:], g3[:, :, 1:3], g3[:, :, 0:2], ALU.min).then_inc(q_kp, 1)
                wait(dve, q_kp, 4 * u + 1)
                dve.tensor_tensor(p_kp[b][:, :, 0:1], g3[:, :, 0:1], p_mn[b][:, :, 1:2], ALU.is_ge).then_inc(q_kp, 1)
                dve.tensor_tensor(p_kp[b][:, :, 2:3], g3[:, :, 2:3], p_mn[b][:, :, 0:1], ALU.is_gt).then_inc(q_kp, 1)
                wait(dve, q_kp, 4 * u + 3)
                dve.tensor_tensor(p_ks[b][:].unsqueeze(2), p_kp[b][:, :, 0:1], p_kp[b][:, :, 2:3], ALU.add).then_inc(q_kp, 1)
                wait(dve, q_kp, 4 * u + 4)
                dve.tensor_scalar(p_kp[b][:, :, 1:2], p_ks[b][:].unsqueeze(2), -1.0, 2.0, ALU.mult, ALU.add).then_inc(q_gc, 1)
                wait(dve, q_gc, 3 * u + 2)
                wait(dve, q_ga, 2 * u + 2)
                dve.tensor_tensor(three(p_ek[b][:]), three(p_eg[b][:]), p_kp[b][:], ALU.mult).then_inc(q_gc, 1)
                wait(dve, q_gc, 3 * u + 3)
                dve.tensor_reduce(p_es[b][:], three(p_ek[b][:]), AX.X, ALU.add).then_inc(q_ge, 1)
                wait(dve, q_ge, 2 * u + 1)
                dve.reciprocal(p_er[b][:], p_es[b][:]).then_inc(q_ge, 1)
                wait(dve, q_ge, 2 * u + 2)
                dve.tensor_tensor(three(p_w[b][:]), three(p_ek[b][:]), bc(p_er[b][:]), ALU.mult).then_inc(q_gd, 1)

            def p_shift(u, b):
                wait(dve, q_sc, u + 1)
                s4 = pS[:, 0, :].rearrange("p (i n) -> p i n", n=P)
                s2 = pS[:, 1, 0:2 * P].rearrange("p (i n) -> p i n", n=P)
                dve.tensor_reduce(p_nm[b][:, 0:4], s4, AX.X, ALU.max, negate=True).then_inc(q_nm, 1)
                dve.tensor_reduce(p_nm[b][:, 4:6], s2, AX.X, ALU.max, negate=True).then_inc(q_nm, 1)
                wait(dve, q_nm, 2 * u + 2)
                wait(dve, q_ex, u - 1)
                dve.tensor_tensor(p_sh[b][:, 0:4, :], s4, p_nm[b][:, 0:4].unsqueeze(2).broadcast_to([P, 4, P]), ALU.add)
                dve.tensor_tensor(p_sh[b][:, 4:6, :], s2, p_nm[b][:, 4:6].unsqueeze(2).broadcast_to([P, 2, P]), ALU.add).then_inc(q_sh, 1)

            def p_outs(u, b):
                pv = pQ[:, 0, 0:2 * E * (HD + 1)].rearrange("p (i d) -> p i d", d=HD + 1)
                wait(dve, q_pv, u + 1)
                dve.reciprocal(p_ri[b][:].unsqueeze(2), pv[:, :, HD:HD + 1]).then_inc(q_fc, 1)
                wait(dve, q_fc, 2 * u + 1)
                dve.tensor_tensor(p_fc[b][:], p_ri[b][:], p_w[b][:], ALU.mult).then_inc(q_fc, 1)
                wait(dve, q_fc, 2 * u + 2)
                wait(dve, q_yT, u - 1)
                dve.tensor_tensor(p_y[b][:, :, 0:C].rearrange("p a (e d) -> p a e d", e=E),
                                  pv[:, :, 0:HD].rearrange("p (a e) d -> p a e d", a=2),
                                  p_fc[b][:].rearrange("p (a e) -> p a e", a=2).unsqueeze(3).broadcast_to([P, 2, E, HD]), ALU.mult).then_inc(q_y, 1)

            def p_residual(u, b):
                wait(dve, q_pr, u + 1)
                if not isinstance(u, int) or u >= 2:
                    wait(dve, s_out[b], (u - b) * 8)
                dve.tensor_tensor(p_o[b][:], pV[:, 0:2 * C].rearrange("p (a n) -> p a n", a=2), hb[:, bass.ds(2 * u, 2), :], ALU.add).then_inc(q_o, 1)

            def stages2(s, b, on):
                if on(0):
                    p_stats(s, b)
                if on(1):
                    if on(0):
                        wait(dve, q_st, 4 * s + 2)
                    p_shift(s - 1, 1 - b)
                if on(0):
                    p_stats_end(s, b)
                    p_norm(s, b)
                    p_lo(s, b)
                    p_conv(s, b)
                    p_vcopy(s, b)
                    p_gate(s, b)
                if on(1):
                    p_outs(s - 1, 1 - b)
                if on(0):
                    p_gate2(s, b)
                    p_gate3(s, b)
                if on(1):
                    p_residual(s - 1, 1 - b)

            for i in range(4):
                dve.wait_ge(q_h[i], 16)
            steps(dve, stages2, U, 1)

        @block.tensor
        def _(pe):
            pe.wait_ge(s_pc, 3)
            pe.wait_ge(s_cd, 9)

            def pos_rows(t, b):
                wait(pe, s_oh, t + 1)
                wait(pe, s_nmt, t - 3)
                wait(pe, s_h1, t - 4)
                for k in range(3):
                    m = pe.matmul(psA[:, 0:C], onehot[b][:], pos_parts[:, k, :], start=(k == 0), stop=(k == 2))
                m.then_inc(s_pos, 1)

            def x_transpose(t, b):
                wait(pe, s_xn, t + 1)
                wait(pe, s_ot, t - 4)
                wait(pe, s_qkt, 3 * (t - 1) if not isinstance(t, int) else 3 * min(t - 1, T))
                for c in range(2):
                    m = pe.transpose(psB[:, c * P:(c + 1) * P], xn[b][:, c * P:(c + 1) * P], ident[:])
                m.then_inc(s_xT, 1)

            def qkv(t, b):
                wait(pe, s_lo, t + 1)
                wait(pe, s_unit, t)
                wait(pe, s_v, t)
                if isinstance(t, int) and t == 0:
                    pe.wait_ge(s_cd, 12)
                wait(pe, s_oa, t - 2)
                parts = [(xt_hi[b], wi_hi), (xt_hi[b], wi_lo), (xt_lo[b], wi_hi)]
                for k, (x, w) in enumerate(parts):
                    for c in range(2):
                        first, last = k + c == 0, k == 2 and c == 1
                        pe.matmul(psC[:, 0:2 * C], x[:, c, :], w[:, c, 0:2 * C], start=first, stop=last)
                        m = pe.matmul(psD[:, 0:C], x[:, c, :], w[:, c, 2 * C:3 * C], start=first, stop=last)
                m.then_inc(s_qkv, 1)

            def transposes(t, b, g):
                wait(pe, s_ul, 2 * t + 2)
                wait(pe, s_qkt, 3 * t + g)
                if g == 0:
                    wait(pe, s_lo, t + 2 if not isinstance(t, int) else min(t + 2, T))
                    wait(pe, s_ot, t - 1)
                    if isinstance(t, int) and t == 0:
                        pe.wait_ge(s_pc, 24)
                for i in range(4):
                    h0_ = (i // 2) * H + 4 * g + 2 * (i % 2)
                    m = pe.transpose(trb[:, i * P:(i + 1) * P], qks[b][:, h0_:h0_ + 2, :].rearrange("p h x -> p (h x)"), ident_h[:])
                m.then_inc(s_tr, 1)

            def scores(t, b, g):
                wait(pe, s_qkt, 3 * t + g + 1)
                wait(pe, s_mx, 3 * t + g)
                for j in range(2):
                    for p in range(2):
                        r = slice(64 * p, 64 * p + 64)
                        m = pe.matmul(psS[:, p, j * P:(j + 1) * P], qkt[b][r, g, j, :], qkt[b][r, g, 2 + j, :], start=True, stop=True)
                m.then_inc(s_sc, 1)

            def max_transpose(t, b):
                wait(pe, s_mx, 3 * t + 3)
                wait(pe, s_h1, t - 1)
                wait(pe, s_e1, 4 * (t + 3) + 2 if not isinstance(t, int) else 4 * min(t + 3, T - 1) + 2)
                pe.transpose(mtb, nmx[b][:], ident_h[:]).then_inc(s_mT, 1)

            def scores_t(t, b, g):
                wait(pe, s_nmt, t + 1)
                wait(pe, s_ex, 3 * t + g)
                if isinstance(t, int) and t + g == 0:
                    pe.wait_ge(s_pc, 38)
                for j in range(2):
                    for p in range(2):
                        r = slice(64 * p, 64 * p + 64)
                        rs = slice(64 * p, 64 * p + 3 * D)
                        o = psT[:, p, j * P:(j + 1) * P]
                        pe.matmul(o, mm_lhs[r, 2 * g + j, :], nmt[b][r, :], start=True, stop=False)
                        m = pe.matmul(o, qkt[b][rs, g, 2 + j, :], qkt[b][rs, g, j, :], start=False, stop=True)
                m.then_inc(s_st, 1)

            def weighted(t, b, g):
                wait(pe, s_ex, 3 * t + g + 1)
                if g == 0:
                    wait(pe, s_v, t + 3 if not isinstance(t, int) else min(t + 3, T))
                    wait(pe, s_va, t + 1)
                for j in range(2):
                    for p in range(2):
                        h = 4 * g + 2 * j + p
                        m = pe.matmul(pvo[:, h, :], et[b][:, 2 * g + j, p, :], vaug[b][:, h, :], start=True, stop=True)
                m.then_inc(s_pv, 1)

            def out_transpose(t, b):
                wait(pe, s_oa, t + 1)
                for c in range(2):
                    m = pe.transpose(psB[:, c * P:(c + 1) * P], oa[b][:, c * P:(c + 1) * P], ident[:])
                m.then_inc(s_oT, 1)

            def project(t, b):
                wait(pe, s_ot, t + 1)
                for c in range(2):
                    m = pe.matmul(psA[:, 0:C], ot[b][:, c, :], wo_s[:, c, :], start=(c == 0), stop=(c == 1))
                m.then_inc(s_pr, 1)

            def stages(s, b, on):
                if on(4):
                    scores_t(s - 4, b, 0)
                if on(3):
                    transposes(s - 3, 1 - b, 0)
                if on(4):
                    scores_t(s - 4, b, 1)
                    weighted(s - 4, b, 0)
                if on(0):
                    pos_rows(s, b)
                if on(3):
                    scores(s - 3, 1 - b, 0)
                    transposes(s - 3, 1 - b, 1)
                if on(4):
                    scores_t(s - 4, b, 2)
                    weighted(s - 4, b, 1)
                if on(3):
                    scores(s - 3, 1 - b, 1)
                    transposes(s - 3, 1 - b, 2)
                if on(4):
                    weighted(s - 4, b, 2)
                if on(1):
                    x_transpose(s - 1, 1 - b)
                if on(3):
                    scores(s - 3, 1 - b, 2)
                if on(1):
                    qkv(s - 1, 1 - b)
                if on(3):
                    max_transpose(s - 3, 1 - b)
                if on(4):
                    if isinstance(s, int):
                        wait(pe, s_lo, min(s, T))
                    else:
                        wait(pe, s_lo, s)
                    out_transpose(s - 4, b)
                    wait(pe, s_nmt, s - 2 if not isinstance(s, int) else min(s - 2, T))
                    project(s - 4, b)

            steps(pe, stages, T, LAST)

            def p_xT(u, b):
                wait(pe, q_xn, 2 * u + 2)
                if isinstance(u, int) and u == 0:
                    pe.wait_ge(s_h1, T)
                    pe.wait_ge(s_cd, 15)
                wait(pe, q_yt, u - 1)
                for c in range(2):
                    for a in range(2):
                        o = 256 * c + P * a
                        m = pe.transpose(pX[:, o:o + P], p_xn[b][:, a, c * P:(c + 1) * P], ident[:])
                m.then_inc(q_xT, 1)

            def p_qkv(u, b):
                wait(pe, q_lo, u + 1)
                wait(pe, q_y, u - 1)
                wait(pe, q_o, u - 1)
                parts = [(p_xh[b], w2_hi), (p_xh[b], w2_lo), (p_xl[b], w2_hi)]
                n = len(parts) * 2
                for i in range(3):
                    o = pQ[:, i // 2, 256 * (i % 2):256 * (i % 2) + 256]
                    for k in range(n):
                        x, w = parts[k // 2]
                        m = pe.matmul(o, w[:, k % 2, i * P:(i + 1) * P], x[:, k % 2, :], start=(k == 0), stop=(k == n - 1))
                m.then_inc(q_qk, 1)
                for a in range(2):
                    o = pV[:, a * (C + G1):(a + 1) * (C + G1)]
                    for k in range(n):
                        x, w = parts[k // 2]
                        m = pe.matmul(o, x[:, k % 2, a * P:(a + 1) * P], w[:, k % 2, 2 * C:NW2], start=(k == 0), stop=(k == n - 1))
                m.then_inc(q_vg, 1)

            SLOTS = [(0, 0), (0, 2), (1, 0), (1, 2), (0, 1), (1, 1)]

            def p_scores(u, b):
                wait(pe, q_sh, u)
                wait(pe, q_cv, 3 * u + 3)
                wait(pe, q_qe, 3 * u + 3)
                pe.matmul(pS[:, 0, :], ident_b[:], causal[:].rearrange("p a n -> p (a n)"), start=True, stop=True, skip_group_check=True)
                pe.matmul(pS[:, 1, 0:2 * P], ident_b[:], causal[:, 0:2, :].rearrange("p a n -> p (a n)"), start=True, stop=True, skip_group_check=True)
                for i, (a, e) in enumerate(SLOTS):
                    col = slice(a * P, (a + 1) * P)
                    lhs = (p_cv[b][:, a, :], p_qk[b][HD:P, 0, col], p_qk[b][0:HD, 2, col])[e]
                    rhs = (p_qk[b][0:HD, 1, col], p_qk[b][HD:P, 1, col], p_qk[b][0:HD, 3, col])[e]
                    m = pe.matmul(pS[:, i // 4, (i % 4) * P:(i % 4 + 1) * P], lhs, rhs, start=False, stop=True, skip_group_check=True)
                m.then_inc(q_sc, 1)

            def p_pT(u, b):
                wait(pe, q_ex, u + 1)
                wait(pe, q_pt, 2 * u)
                for i in range(2 * E):
                    m = pe.transpose(pP[i // 3][:, (i % 3) * P:(i % 3 + 1) * P], p_ex[b][:, i, :], ident[:])
                m.then_inc(q_pT, 1)

            def p_pv(u, b):
                wait(pe, q_pt, 2 * u + 2)
                wait(pe, q_vc, u + 1)
                wait(pe, q_qe, 3 * (u + 2) if not isinstance(u, int) else 3 * min(u + 2, U))
                for i, (a, e) in enumerate(SLOTS):
                    k = a * E + e
                    m = pe.matmul(pQ[:, 0, k * (HD + 1):(k + 1) * (HD + 1)], p_pt[b][:, i, :], p_v[b][:, k, :], start=True, stop=True)
                m.then_inc(q_pv, 1)

            def p_yT(u, b):
                wait(pe, q_y, u + 1)
                wait(pe, q_lo, u + 2 if not isinstance(u, int) else min(u + 2, U))
                for c in range(2):
                    for a in range(2):
                        o = 256 * c + P * a
                        m = pe.transpose(pX[:, o:o + P], p_y[b][:, a, c * P:(c + 1) * P], ident[:])
                m.then_inc(q_yT, 1)

            def p_project(u, b):
                wait(pe, q_yt, u + 1)
                nxt = u + 2 if not isinstance(u, int) else min(u + 2, U)
                wait(pe, q_vc, nxt)
                wait(pe, q_rl, nxt)
                for a in range(2):
                    for c in range(2):
                        m = pe.matmul(pV[:, a * C:(a + 1) * C], p_yt[b][:, c, a * P:(a + 1) * P], wp_f[:, c, :], start=(c == 0), stop=(c == 1))
                m.then_inc(q_pr, 1)

            def stages2(s, b, on):
                if on(1):
                    p_scores(s - 1, 1 - b)
                if on(0):
                    p_xT(s, b)
                    p_qkv(s, b)
                if on(1):
                    p_pT(s - 1, 1 - b)
                    p_pv(s - 1, 1 - b)
                    p_yT(s - 1, 1 - b)
                    p_project(s - 1, 1 - b)

            steps(pe, stages2, U, 1)


_INS = ['word_ids', 'type_ids', 'pos_ids', 'word_emb', 'pos_emb', 'type_emb', 'gamma', 'beta',
        'w_in', 'b_in', 'logit_scale', 'head_scale', 'w_out', 'b_out', 'w_qk', 'b_qk', 'w_v', 'b_v',
        'conv_w', 'conv_b', 'w_g1', 'b_g1', 'w_g2', 'b_g2', 'w_p', 'b_p']


def kernel(**inputs):
    import numpy as _np
    import concourse.bacc as _bacc
    from concourse import mybir as _mybir
    from concourse.bass_utils import run_bass_kernel_spmd as _run

    a = {k: _np.asarray(v) for k, v in inputs.items()}
    seqs, positions = a['x'].shape
    near = 128 // seqs

    def by_tile(ids):
        return ids.reshape(seqs, positions // near, near).transpose(1, 2, 0)

    laid = {
        'word_ids': by_tile(a['x']).reshape(-1, 128).T,
        'type_ids': by_tile(a['mask_BS_i1_0']).reshape(-1, 128).T,
        'pos_ids': by_tile(a['pos_BS']).reshape(-1),
        'word_emb': a['L0_tok_word_emb'], 'pos_emb': a['L0_tok_pos_emb'], 'type_emb': a['L0_tok_type_emb'],
        'gamma': a['L0_tok_gamma'], 'beta': a['L0_tok_beta'],
        'w_in': a['L0_attn_in_proj_weight'].T, 'b_in': a['L0_attn_in_proj_bias'],
        'logit_scale': a['L0_attn_logit_scale'], 'head_scale': a['L0_attn_head_scale'],
        'w_out': a['L0_attn_out_w'].T, 'b_out': a['L0_attn_out_b'],
    }
    hd = a['L0_ffn_Wqk'].shape[1] // 6
    order = _np.concatenate([_np.arange(hd) + hd * e for e in (0, 1, 3, 4, 2, 5)])
    laid['w_qk'] = a['L0_ffn_Wqk'][:, order]
    laid['b_qk'] = a['L0_ffn_bqk'][order]
    laid['w_g2'] = a['L0_ffn_Wg2'].T
    for name, key in (('w_v', 'Wv'), ('b_v', 'bv'), ('conv_w', 'conv_w'), ('conv_b', 'conv_b'), ('w_g1', 'Wg1'),
                      ('b_g1', 'bg1'), ('b_g2', 'bg2'), ('w_p', 'Wp'), ('b_p', 'bp')):
        laid[name] = a['L0_ffn_' + key]

    nc = _bacc.Bacc("TRN2", target_bir_lowering=False, num_devices=1)
    arrays, args = {}, []
    for name in _INS:
        x = _np.ascontiguousarray(laid[name])
        arrays[f"in_{name}"] = x
        args.append(nc.dram_tensor(f"in_{name}", x.shape, _mybir.dt.from_np(x.dtype), kind="ExternalInput").ap())
    width = a['L0_tok_word_emb'].shape[1]
    args.append(nc.dram_tensor("h_scratch", (seqs * positions, width), _mybir.dt.float32, kind="Internal").ap())
    args.append(nc.dram_tensor("out_0", (seqs, positions, width), _mybir.dt.float32, kind="ExternalOutput").ap())
    block_kernel(nc, *args)
    r = _run(nc, [arrays], core_ids=[0])
    return r.results[0]["out_0"]
```

```python
from contextlib import ExitStack

import concourse.bass as bass
from concourse import mybir

ALU = mybir.AluOpType
ACT = mybir.ActivationFunctionType
AX = mybir.AxisListType
F32 = mybir.dt.float32
F32R = mybir.dt.float32r
F16 = mybir.dt.float16
BF16 = mybir.dt.bfloat16
I32 = mybir.dt.int32
U32 = mybir.dt.uint32

P = 128
LOG_SCALE_MAX = 4.605170185988092
MASK_Q, MASK_K = 128.0, 64.0
KEY_SCALE = 16.0
CAUSAL_OFF = -1.0e30


def block_kernel(nc, word_ids, type_ids, pos_ids, word_emb, pos_emb, type_emb, gamma, beta,
                 w_in, b_in, logit_scale, head_scale, w_out, b_out,
                 w_qk, b_qk, w_v, b_v, conv_w, conv_b, w_g1, b_g1, w_g2, b_g2, w_p, b_p,
                 h_scratch, out):
    C = word_emb.shape[1]
    T = word_ids.shape[1]
    H = logit_scale.shape[0]
    D = C // H
    L = out.shape[0]
    NPOS = P // L
    E = b_g2.shape[0]
    HD = C // E
    G1 = b_g1.shape[0]
    CB = C - P
    NG = 3
    J = H // 2
    U = L // 2
    NQKV = 3 * C
    NW2 = 3 * C + G1
    DA = D + 1
    WIDE = 3

    ctx = ExitStack()
    with ctx:
        def sb(name, shape, dt=F32):
            return ctx.enter_context(nc.sbuf_tensor(name, shape, dt))

        def pb(name, shape, dt=F32):
            return ctx.enter_context(nc.psum_tensor(name, shape, dt))

        def sem(name):
            return ctx.enter_context(nc.semaphore(name))

        def two(name, shape, dt=F32):
            return [sb(f"{name}{i}", shape, dt) for i in range(2)]

        ids_w = sb("ids_w", [P, T], I32)
        ids_t = sb("ids_t", [P, T], I32)
        type_f = sb("type_f", [P, T])
        pos_row_i = sb("pos_row_i", [P, T * P], I32)
        iota_p = sb("iota_p", [P, 1])
        pos_tab = sb("pos_tab", [P, C])
        type_tab = sb("type_tab", [P, 2, C])
        type_diff = sb("type_diff", [P, C])
        pos_tab0 = sb("pos_tab0", [P, C])
        pos_parts = sb("pos_parts", [P, 3, C], BF16)
        pos_rest = sb("pos_rest", [P, 1, C])
        gamma_b = sb("gamma_b", [P, C])
        beta_b = sb("beta_b", [P, C])
        ident = sb("ident", [P, P])
        ident_h = sb("ident_h", [P, P], F16)
        ident_b = sb("ident_b", [P, P], BF16)
        minus_half = sb("minus_half", [P, 2 * H])
        keep_in = sb("keep_in", [P, 4 * P], F16)
        eps = sb("eps", [P, 3])
        own_pos = sb("own_pos", [P, NPOS], F16)
        lscale = sb("lscale", [P, H])
        lscale_min = sb("lscale_min", [P, H])
        qk_scale = sb("qk_scale", [P, 2 * H])
        wi_f = sb("wi_f", [P, 2, NQKV])
        wi_hi = sb("wi_hi", [P, 2, NQKV], F32R)
        wi_lo = sb("wi_lo", [P, 2, NQKV], F32R)
        w2_f = sb("w2_f", [P, 2, NW2])
        w2_hi = sb("w2_hi", [P, 2, NW2], F32R)
        w2_lo = sb("w2_lo", [P, 2, NW2], F32R)
        wo_f = sb("wo_f", [P, 2, C])
        wo_s = sb("wo_s", [P, 2, C])
        hs_col = sb("hs_col", [P, 2])
        wp_f = sb("wp_f", [P, 2, C])
        mm_own = sb("mm_own", [P, 2, P], F16)
        mm_sum = sb("mm_sum", [P, P], F16)
        mm_sel = sb("mm_sel", [P, J, P], F16)
        mm_lhs = sb("mm_lhs", [P, J, P], F16)
        causal = sb("causal", [P, 2, P], BF16)
        conv_c = sb("conv_c", [HD, 4])
        wg2_b = sb("wg2_b", [P, E, G1])
        bg2_b = sb("bg2_b", [P, E])

        word = sb("word", [P, T, C])
        h0 = sb("h0", [P, T, C])
        onehot = two("onehot", [P, P], BF16)
        emb_a = two("emb_a", [P, C])
        emb_b = two("emb_b", [P, C])
        st1 = two("st1", [P, 6])
        mv1 = two("mv1", [P, 2])
        ve1 = two("ve1", [P, 1])
        rs1 = two("rs1", [P, 1])
        nrg = two("nrg", [P, C])
        st2 = two("st2", [P, 6])
        mv2 = two("mv2", [P, 2])
        ve2 = two("ve2", [P, 1])
        rs2 = two("rs2", [P, 1])
        xn = two("xn", [P, 2 * P])
        xt_hi = two("xt_hi", [P, 2, P], F32R)
        xt_lo = two("xt_lo", [P, 2, P], F32R)
        qkf = two("qkf", [P, 2 * C])
        sq = two("sq", [P, 2 * C])
        ssq = two("ssq", [P, 2 * H])
        ssc = two("ssc", [P, 2 * H])
        rno = two("rno", [P, 2 * H])
        rnk = two("rnk", [P, 2 * H])
        unit = two("unit", [P, 2 * C])
        qks = two("qks", [P, 2 * H, 4 * D], F16)
        qkt = two("qkt", [P, NG, 4, P], F16)
        nmx = two("nmx", [P, P], F16)
        nmt = two("nmt", [P, P], F16)
        vnew = two("vnew", [P, C])
        vaug = two("vaug", [P, H + WIDE - 1, DA])
        et = two("et", [P, J, 2, P])
        rsum = two("rsum", [P, H])
        oa = two("oa", [P, 2 * P])
        ot = two("ot", [P, 2, P])
        h1t = two("h1t", [P, C])

        psA = pb("psA", [P, 512])
        psB = pb("psB", [P, 512])
        psC = pb("psC", [P, 512])
        psD = pb("psD", [P, 512])
        psS = pb("psS", [P, 2, 512])
        psT = pb("psT", [P, 2, 512])

        LAST = 6
        LO = LAST + 2
        s_ids = sem("ids_loaded")
        s_tabs = sem("tables_loaded")
        s_zero = sem("weights_zeroed")
        s_win = sem("w_in_loaded")
        s_w2 = sem("w2_loaded")
        s_wop = sem("w_out_loaded")
        s_misc = sem("misc_loaded")
        s_pc = sem("pool_constants")
        s_id = sem("identities_copied")
        s_own = sem("own_positions_built")
        s_qm = sem("mask_columns_built")
        s_qsc = sem("logit_scales")
        s_tb = sem("tables_added")
        s_pp = sem("position_parts")
        s_one = sem("ones_columns")
        s_mm = sem("mask_rows_built")
        s_cz = sem("causal_built")
        s_wh = sem("w_in_high")
        s_wl = sem("w_in_low")
        s_ws = sem("w_out_scaled")
        s_w2h = sem("w2_high")
        s_w2l = sem("w2_low")
        s_word = [sem(f"word_rows_{i}") for i in range(LO + 1)]
        s_oh = sem("onehot_built")
        s_pos = sem("pos_rows_out")
        s_e1 = sem("embed_dve")
        s_ln1 = sem("rstd1_done")
        s_aff = sem("affine_done")
        s_ln2 = sem("rstd2_done")
        s_xn = sem("xn_done")
        s_nd = sem("stats2_dve")
        s_qc = sem("qk_copied")
        s_xT = sem("x_transposed")
        s_hi = sem("x_hi_copied")
        s_lo = sem("x_lo_made")
        s_qk = sem("qk_done")
        s_qkv = sem("qkv_done")
        s_sq = sem("squares_done")
        s_ss = sem("square_sums")
        s_rn = sem("rnorm_done")
        s_unit = sem("unit_done")
        s_uh = sem("unit_hi")
        s_ul = sem("unit_lo")
        s_v = sem("v_copied")
        s_va = sem("v_augmented")
        s_tr = sem("qk_transposed")
        s_qkt = sem("qkt_copied")
        s_sc = sem("scores_done")
        s_mx = sem("max_done")
        s_mT = sem("max_transposed")
        s_nmt = sem("max_copied")
        s_st = sem("scores_t_done")
        s_ex = sem("exp_done")
        s_pv = sem("pv_done")
        s_rc = sem("recip_done")
        s_oa = sem("attn_out_done")
        s_oT = sem("attn_transposed")
        s_ot = sem("attn_t_copied")
        s_pr = sem("proj_done")
        s_h1 = sem("h1_done")
        s_st1 = [sem(f"h1_stored_{i}") for i in range(2)]

        hb = word
        p_st = two("p_st", [P, 2, 6])
        p_mv = two("p_mv", [P, 2, 2])
        p_ve = two("p_ve", [P, 2])
        p_rs = two("p_rs", [P, 2])
        p_xn = two("p_xn", [P, 2, 2 * P])
        p_xh = two("p_xh", [P, 2, 2 * P], F32R)
        p_xl = two("p_xl", [P, 2, 2 * P], F32R)
        qk_all = sb("qk_all", [P, U, 4, 2 * P])
        q0_raw = [pos_row_i[0:HD, 2 * P * i:2 * P * (i + 1)].bitcast(F32) for i in range(2)]
        v_all = sb("v_all", [P, U * 2 * E, HD + 1])
        p_rl = two("p_rl", [P, 2, G1])
        p_rw = two("p_rw", [P, 2, E, G1])
        g_lg = sb("g_lg", [P, L * E])
        g_lb = sb("g_lb", [P, L * E])
        g_nm = sb("g_nm", [P, L])
        g_df = sb("g_df", [P, L * E])
        g_ex = sb("g_ex", [P, L * E])
        g_sm = sb("g_sm", [P, L])
        g_rs = sb("g_rs", [P, L])
        g_g = sb("g_g", [P, L * E])
        g_mn = sb("g_mn", [P, L, 2])
        g_kp = sb("g_kp", [P, L, E])
        g_ks = sb("g_ks", [P, L])
        g_eg = sb("g_eg", [P, L * E])
        g_ek = sb("g_ek", [P, L * E])
        g_es = sb("g_es", [P, L])
        g_er = sb("g_er", [P, L])
        g_w = sb("g_w", [P, L * E])
        qs = [x[:] for x in p_xn]
        q2s = [pos_row_i[0:HD, 2 * P * (2 + i):2 * P * (3 + i)].bitcast(F32) for i in range(2)]
        p_nm = two("p_nm", [P, E, 2])
        p_ex = [x[:, 0:E].rearrange("p e a n -> p (e a) n") for x in et]
        p_pt = [x[:, E:2 * E].rearrange("p e a n -> p (e a) n") for x in et]
        p_ri = two("p_ri", [P, 2 * E])
        p_fc = two("p_fc", [P, 2 * E])
        p_y = two("p_y", [P, 2, 2 * P])
        p_yt = [x[:].rearrange("p h x -> p (h x)").bitcast(F32)[:, 0:4 * P].rearrange("p (c n) -> p c n", c=2) for x in qks]
        p_o = [x[:].rearrange("p (a n) -> p a n", a=2) for x in qkf]

        q_early = sem("p_rows_loaded_early")
        q_late = sem("p_rows_loaded_late")
        q_st = sem("p_stats")
        q_rs = sem("p_rstd")
        q_xn = sem("p_xn_done")
        q_xT = sem("p_x_transposed")
        q_hi = sem("p_x_hi")
        q_lo = sem("p_x_lo")
        q_qk = sem("p_qk_done")
        q_vg = sem("p_vg_done")
        q_qe = sem("p_qk_copied")
        q_cv = sem("p_conv")
        q_rl = sem("p_relu")
        q_vc = sem("p_v_copied")
        q_gp = sem("p_gate_products")
        q_lg = sem("p_gate_logits")
        q_gd = sem("gate_dve")
        q_ga = sem("gate_exps")
        q_qs = sem("p_queries_copied")
        q_sc = sem("p_scores")
        q_nm = sem("p_max")
        q_ex = sem("p_exp")
        q_pT = sem("p_p_transposed")
        q_pa = sem("p_pt_copied_act")
        q_pd = sem("p_pt_copied_dve")
        q_pv = sem("p_pv")
        q_fc = sem("p_factor")
        q_y = sem("p_y_done")
        q_yT = sem("p_y_transposed")
        q_yt = sem("p_yt_copied")
        q_pr = sem("p_proj")
        q_o = sem("p_out_made")
        s_out = [sem(f"out_stored_{i}") for i in range(2)]

        pX = [psA, psB]
        pQ = [psT, psS]
        pV = [psC, psD]
        pS = [psB[:, 0:2 * P], psS[:, 0, 0:2 * P], psS[:, 1, 0:2 * P]]
        pP = [psC, psD]
        pO = psT[:, 0, 0:2 * E * (HD + 1)].rearrange("p (i d) -> p i d", d=HD + 1)
        pR = psT[:, 1, 0:2 * C]
        pY = psA

        block = ctx.enter_context(nc.Block())

        def wait(eng, s, value):
            if not isinstance(value, int) or value > 0:
                eng.wait_ge(s, value)

        def steps(eng, stages, n, last, enter=None):
            lo = last + 2
            hi = lo + (n - lo) // 2 * 2

            def one(s):
                stages(s, s % 2, lambda off: 0 <= s - off < n)

            for s in range(lo):
                one(s)
            if enter:
                enter()
            with eng.Fori(lo, hi - 1, 2) as s:
                for k in range(2):
                    stages(s + k, (lo + k) % 2, lambda off: True)
            for s in range(hi, n + last):
                one(s)

        trb = psB[:, 256:512].bitcast(F16)
        mtb = psB[:, 0:64].bitcast(F16)
        pvw = psD[:, 256:256 + (H + WIDE - 1) * DA].rearrange("p (h d) -> p h d", d=DA)
        pvo = pvw[:, 0:H, :]

        @block.sync
        def _(sp):
            sp.dma_start(ids_w[:], word_ids).then_inc(s_ids, 16)
            sp.dma_start(pos_row_i[:], pos_ids.partition_broadcast(P)).then_inc(s_tabs, 16)
            sp.dma_start(type_tab[:].rearrange("p a c -> p (a c)"),
                         type_emb.rearrange("a c -> (a c)").partition_broadcast(P)).then_inc(s_tabs, 16)
            sp.dma_start(wi_f[:, 0, :], w_in[0:P, :]).then_inc(s_win, 16)
            sp.wait_ge(s_zero, 1)
            sp.dma_start(wi_f[0:CB, 1, :], w_in[P:C, :]).then_inc(s_win, 16)
            sp.dma_start(wi_f[CB:CB + 1, 1, :], b_in.unsqueeze(0)).then_inc(s_win, 16)
            sp.wait_ge(s_zero, 3)
            sp.dma_start(wo_f[:, 0, :], w_out[0:P, :]).then_inc(s_wop, 16)
            sp.dma_start(wo_f[0:CB, 1, :], w_out[P:C, :]).then_inc(s_wop, 16)
            sp.dma_start(wo_f[CB:CB + 1, 1, :], b_out.unsqueeze(0)).then_inc(s_wop, 16)
            hs16 = head_scale.rearrange("h a b -> h (a b)")
            sp.dma_start(hs_col[:, 0:1], hs16[0:P // D, :].unsqueeze(1).broadcast_to([P // D, D, 1])).then_inc(s_wop, 16)
            sp.dma_start(hs_col[0:CB, 1:2], hs16[P // D:H, :].unsqueeze(1).broadcast_to([H - P // D, D, 1])).then_inc(s_wop, 16)
            sp.dma_start(wp_f[:, 0, :], w_p[0:P, :]).then_inc(s_wop, 16)
            sp.dma_start(wp_f[0:CB, 1, :], w_p[P:C, :]).then_inc(s_wop, 16)
            sp.dma_start(wp_f[CB:CB + 1, 1, :], b_p.unsqueeze(0)).then_inc(s_wop, 16)
            for dst, src in ((slice(0, 2 * C), w_qk), (slice(3 * C, NW2), w_g1)):
                sp.dma_start(w2_f[:, 0, dst], src[0:P, :]).then_inc(s_w2, 16)
                sp.dma_start(w2_f[0:CB, 1, dst], src[P:C, :]).then_inc(s_w2, 16)
            for e in range(E):
                dst = slice(2 * C + e * HD, 2 * C + (e + 1) * HD)
                sp.dma_start(w2_f[:, 0, dst], w_v[e, 0:P, :]).then_inc(s_w2, 16)
                sp.dma_start(w2_f[0:CB, 1, dst], w_v[e, P:C, :]).then_inc(s_w2, 16)
            sp.dma_start(w2_f[CB:CB + 1, 1, 0:2 * C], b_qk.unsqueeze(0)).then_inc(s_w2, 16)
            sp.dma_start(w2_f[CB:CB + 1, 1, 2 * C:3 * C], b_v.rearrange("e d -> (e d)").unsqueeze(0)).then_inc(s_w2, 16)
            sp.dma_start(w2_f[CB:CB + 1, 1, 3 * C:NW2], b_g1.unsqueeze(0)).then_inc(s_w2, 16)
            sp.dma_start(conv_c[:, 0:3], conv_w.rearrange("c a k -> c (a k)")).then_inc(s_w2, 16)
            sp.dma_start(conv_c[:, 3:4], conv_b.unsqueeze(1)).then_inc(s_w2, 16)
            sp.dma_start(wg2_b[:].rearrange("p e g -> p (e g)"), w_g2.rearrange("e g -> (e g)").partition_broadcast(P)).then_inc(s_w2, 16)
            sp.dma_start(bg2_b[:], b_g2.partition_broadcast(P)).then_inc(s_w2, 16)

            def store_h1(t, b):
                wait(sp, s_h1, t + 1)
                sp.dma_start(h_scratch[bass.ts(t, P), :], h1t[b][:]).then_inc(s_st1[b], 16)

            def stages(s, b, on):
                if on(6):
                    store_h1(s - 6, b)

            src = h_scratch.rearrange("(n l) c -> n l c", l=L)

            def load_rows(t0, t1, signal):
                for b in range(2):
                    sp.wait_ge(s_st1[b], 16 * ((t1 + 1 - b) // 2))
                rows = slice(NPOS * t0, NPOS * t1)
                sp.dma_start(hb[rows, :, :], src[rows, :, :]).then_inc(signal, 16)

            steps(sp, stages, T - 2, LAST)
            load_rows(0, T - 2, q_early)
            for t in range(T - 2, T):
                store_h1(t, t % 2)
            for t in range(T - 2, T):
                load_rows(t, t + 1, q_late)

            def store_out(u, b):
                wait(sp, q_o, u + 1)
                sp.dma_start(out[bass.ds(2 * u, 2), :, :].rearrange("a n c -> n a c"), p_o[b]).then_inc(s_out[b], 16)

            def stages2(s, b, on):
                if on(2):
                    store_out(s - 2, b)

            steps(sp, stages2, U, 2)
            for b in range(2):
                sp.wait_ge(s_out[b], 16 * (U // 2))

        @block.gpsimd
        def _(pool):
            pool.iota(iota_p[:], pattern=[[0, 1]], base=0, channel_multiplier=1,
                      allow_small_or_imprecise_dtypes=True).then_inc(s_pc, 1)
            pool.memset(ident[:], 0.0).then_inc(s_pc, 1)
            pool.wait_ge(s_pc, 2)
            pool.affine_select(out=ident[:], in_=ident[:], compare_op=ALU.not_equal, fill=1.0, base=0,
                               pattern=[[-1, P]], channel_multiplier=1).then_inc(s_pc, 1)
            pool.wait_ge(s_ids, 16)

            def gather(t):
                pool.indirect_dma_start(
                    word[:, t, :], None, word_emb,
                    bass.IndirectOffsetOnAxis(ids_w[:, t:t + 1].bitcast(U32), 0)).then_inc(s_word[min(t, LO)], 16)

            for t in range(2):
                gather(t)
            pool.memset(own_pos[:], 1.0).then_inc(s_pc, 1)
            pool.wait_ge(s_pc, 4)
            pool.affine_select(out=own_pos[:], in_=own_pos[:], compare_op=ALU.is_ge, fill=0.0, base=0,
                               pattern=[[-L, NPOS]], channel_multiplier=1).then_inc(s_pc, 1)
            pool.wait_ge(s_pc, 5)
            pool.affine_select(out=own_pos[:], in_=own_pos[:], compare_op=ALU.is_ge, fill=0.0, base=L - 1,
                               pattern=[[L, NPOS]], channel_multiplier=-1).then_inc(s_own, 1)
            for t in range(2, 8):
                gather(t)

            LATER_WORDS = ((8,), (9, 10), (), (11, 12), (13,), (14,), (15,), ())

            def mask_rows(p):
                pool.wait_ge(s_zero, 6)
                r0 = 64 * p + J
                pool.affine_select(out=mm_own[:, p, :], in_=mm_own[:, p, :], compare_op=ALU.is_ge, fill=0.0,
                                   base=L * r0, pattern=[[1, P]], channel_multiplier=-L).then_inc(s_mm, 1)
                wait(pool, s_mm, 4 * p)
                pool.affine_select(out=mm_sel[:], in_=mm_sel[:], compare_op=ALU.not_equal, fill=1.0,
                                   base=-64 * p, pattern=[[-1, J], [0, P]], channel_multiplier=1).then_inc(s_mm, 1)
                pool.wait_ge(s_mm, 4 * p + 1)
                pool.affine_select(out=mm_own[:, p, :], in_=mm_own[:, p, :], compare_op=ALU.is_ge, fill=0.0,
                                   base=L - 1 - L * r0, pattern=[[-1, P]], channel_multiplier=L).then_inc(s_mm, 1)
                pool.wait_ge(s_mm, 4 * p + 3)
                pool.affine_select(out=mm_own[:, p, :], in_=mm_own[:, p, :], compare_op=ALU.not_equal, fill=MASK_K,
                                   base=-(r0 + NPOS), pattern=[[0, P]], channel_multiplier=1).then_inc(s_mm, 1)

            def causal_mask():
                pool.affine_select(out=causal[:], in_=causal[:], compare_op=ALU.is_ge, fill=CAUSAL_OFF, base=0,
                                   pattern=[[0, 2], [-1, P]], channel_multiplier=1).then_inc(s_cz, 1)

            def rstd(ve, rs, mv, eps, s_own, t):
                pool.tensor_tensor(ve[:], mv[:, 1:2], eps, ALU.add).then_inc(s_own, 1)
                wait(pool, s_own, 2 * t + 1)
                pool.tensor_tensor(rs[:], ve[:], minus_half[:, 0:1], ALU.pow).then_inc(s_own, 1)

            def rnorm(t, b):
                wait(pool, s_ss, 2 * t + 2)
                pool.tensor_tensor(rno[b][:], ssc[b][:], minus_half[:], ALU.pow).then_inc(s_rn, 1)
                wait(pool, s_rn, 2 * t + 1)
                wait(pool, s_unit, t - 1)
                if isinstance(t, int) and t == 0:
                    pool.wait_ge(s_qsc, 3)
                pool.tensor_tensor(rnk[b][:], rno[b][:], qk_scale[:], ALU.mult).then_inc(s_rn, 1)

            def unit_lo(t, b):
                wait(pool, s_uh, 2 * t + 2)
                u = unit[b][:].rearrange("p (h d) -> p h d", d=D)
                pool.tensor_tensor(qks[b][:, 0:H, D:2 * D], u[:, 0:H, :], qks[b][:, 0:H, 0:D], ALU.subtract).then_inc(s_ul, 1)
                pool.tensor_tensor(qks[b][:, H:2 * H, 2 * D:3 * D], u[:, H:2 * H, :], qks[b][:, H:2 * H, 0:D], ALU.subtract).then_inc(s_ul, 1)

            pool.wait_ge(s_zero, 4)

            def stages(s, b, on):
                if on(1):
                    wait(pool, s_nd, 2 * s)
                    rstd(ve2[1 - b], rs2[1 - b], mv2[1 - b], eps[:, 0:1], s_ln2, s - 1)
                filling = isinstance(s, int) and s < LAST - 1
                if not filling and on(2):
                    rnorm(s - 2, b)
                if on(0):
                    wait(pool, s_e1, 4 * s + 4)
                    rstd(ve1[b], rs1[b], mv1[b], eps[:, 2:3], s_ln1, s)
                if filling and on(2):
                    rnorm(s - 2, b)
                if on(3):
                    unit_lo(s - 3, 1 - b)
                if isinstance(s, int) and s < LO:
                    if s == 0:
                        mask_rows(0)
                        causal_mask()
                    if s == 1:
                        mask_rows(1)
                    for t in LATER_WORDS[s]:
                        gather(t)

            steps(pool, stages, T, LAST)

            def gate(u, b):
                wait(pool, q_rl, u + 1)
                wait(pool, q_lg, u - 1)
                pool.tensor_tensor(p_rw[b][:], p_rl[b][:].unsqueeze(2).broadcast_to([P, 2, E, G1]),
                                   wg2_b[:].unsqueeze(1).broadcast_to([P, 2, E, G1]), ALU.mult).then_inc(q_gp, 1)

            def rstd2(u, b):
                wait(pool, q_st, 4 * u + 4)
                pool.tensor_tensor(p_ve[b][:], p_mv[b][:, :, 1:2].rearrange("p a o -> p (a o)"), eps[:, 0:2], ALU.add).then_inc(q_rs, 1)
                wait(pool, q_rs, 2 * u + 1)
                pool.tensor_tensor(p_rs[b][:], p_ve[b][:], minus_half[:, 0:2], ALU.pow).then_inc(q_rs, 1)

            def p_queries(u, b):
                if isinstance(u, int) and u == 0:
                    pool.wait_ge(q_xT, U)
                wait(pool, q_sc, 3 * (u - 1))
                wait(pool, q_qe, 6 * u + 5)
                wait(pool, q_cv, 2 * u + 2)
                at = bass.ds(u, 1)
                pool.tensor_copy(qs[b], qk_all[:, at, 0:2, :].rearrange("p o x n -> p (o x) n")).then_inc(q_qs, 1)
                pool.tensor_copy(q2s[b], qk_all[0:HD, at, 2, :].rearrange("p o n -> p (o n)")).then_inc(q_qs, 1)

            pool.wait_ge(s_w2, 16 * 17)

            def stages2(s, b, on):
                if on(0):
                    rstd2(s, b)
                if isinstance(s, int) and s > U:
                    p_queries(s - U - 1, (s - U - 1) % 2)
                if on(2):
                    gate(s - 2, b)

            steps(pool, stages2, U, 3)

            def stages3(s, b, on):
                if not isinstance(s, int) or s > 1:
                    p_queries(s, b)

            steps(pool, stages3, U, 0)

        @block.scalar
        def _(act):
            act.dma_start(pos_tab[:], pos_emb).then_inc(s_tabs, 16)
            act.dma_start(ids_t[:], type_ids).then_inc(s_tabs, 16)
            act.dma_start(gamma_b[:], gamma.partition_broadcast(P)).then_inc(s_misc, 16)
            act.dma_start(beta_b[:], beta.partition_broadcast(P)).then_inc(s_misc, 16)
            act.dma_start(lscale[:], logit_scale.rearrange("h a b -> (h a b)").partition_broadcast(P)).then_inc(s_misc, 16)
            act.wait_ge(s_qsc, 1)
            act.activation(qk_scale[:, 0:H], lscale_min[:], ACT.Exp).then_inc(s_qsc, 1)
            act.wait_ge(s_win, 48)
            act.activation(wi_hi[:], wi_f[:], ACT.Copy).then_inc(s_wh, 1)

            def late_setup():
                act.wait_ge(s_w2, 16 * 17)
                act.activation(w2_hi[:], w2_f[:], ACT.Copy).then_inc(s_w2h, 1)

            def x_hi(t, b):
                wait(act, s_xT, t + 1)
                wait(act, s_qkv, t - 1)
                act.activation(xt_hi[b][:].rearrange("p a n -> p (a n)"), psA[:, 2 * P:4 * P], ACT.Copy).then_inc(s_hi, 1)

            def copy_qk(t, b):
                wait(act, s_qk, t + 1)
                wait(act, s_unit, t - 1)
                act.activation(qkf[b][:], psC[:, 0:2 * C], ACT.Copy).then_inc(s_qc, 1)

            def squares(t, b):
                wait(act, s_qkv, t + 1)
                wait(act, s_va, t - 1)
                act.activation(vnew[b][:], psD[:, 0:C], ACT.Copy).then_inc(s_v, 1)
                wait(act, s_qc, t + 1)
                wait(act, s_ss, 2 * (t - 1) - 1)
                act.activation(sq[b][:], qkf[b][:], ACT.Square).then_inc(s_sq, 1)

            def unit_hi(t, b, of_k):
                wait(act, s_unit, t + 1)
                wait(act, s_tr, 3 * (t - 1))
                u = unit[b][:].rearrange("p (h d) -> p h d", d=D)
                if isinstance(t, int) and t == 0:
                    act.wait_ge(s_qm, 4 * 4)
                if of_k:
                    to = qks[b][:, H:2 * H, 0:2 * D].rearrange("p h (a x) -> p h a x", x=D)
                else:
                    to = qks[b][:, 0:H, :].rearrange("p h (a x) -> p h a x", x=2 * D)[:, :, :, 0:D]
                act.activation(to, u[:, of_k * H:(of_k + 1) * H, :].unsqueeze(2).broadcast_to([P, H, 2, D]), ACT.Copy).then_inc(s_uh, 1)

            def copy_qkt(t, b, g):
                wait(act, s_tr, 3 * t + g + 1)
                wait(act, s_st, 3 * (t - 2) + g + 1)
                act.activation(qkt[b][:, g, :, :].rearrange("p a n -> p (a n)"), trb, ACT.Copy).then_inc(s_qkt, 1)

            def copy_max(t, b):
                wait(act, s_mT, t + 1)
                wait(act, s_st, 3 * (t - 1))
                act.activation(nmt[b][:], mtb, ACT.Copy).then_inc(s_nmt, 1)

            def exps(t, b, g):
                wait(act, s_st, 3 * t + g + 1)
                wait(act, s_pv, 3 * (t - 2) + g + 1)
                act.activation(et[b][:, 2 * g:2 * g + 2, :, :].rearrange("q j p c -> q p j c"),
                               psT[:, :, 0:2 * P].rearrange("q p (j c) -> q p j c", j=2),
                               ACT.Exp, scale=1.0 / KEY_SCALE).then_inc(s_ex, 1)

            def copy_ot(t, b):
                wait(act, s_oT, t + 1)
                wait(act, s_pr, t - 1)
                act.activation(ot[b][:].rearrange("p a n -> p (a n)"), psA[:, 2 * P:4 * P], ACT.Copy).then_inc(s_ot, 1)

            def stages(s, b, on):
                for g in range(NG):
                    if on(5):
                        exps(s - 5, 1 - b, g)
                    if g == 0 and on(2):
                        squares(s - 2, b)
                    if g == 2 and on(1):
                        x_hi(s - 1, 1 - b)
                    if on(4):
                        copy_qkt(s - 4, b, g)
                    if g > 0 and on(3):
                        unit_hi(s - 3, 1 - b, g - 1)
                if on(1):
                    copy_qk(s - 1, 1 - b)
                if on(4):
                    copy_max(s - 4, b)
                if on(5):
                    copy_ot(s - 5, 1 - b)
                if isinstance(s, int) and s == LAST:
                    late_setup()

            steps(act, stages, T, LAST)

            def p_hi(u, b):
                wait(act, q_xT, u + 1)
                wait(act, q_vg, u - 1)
                act.activation(p_xh[b][:].rearrange("p a n -> p (a n)"), pX[b][:], ACT.Copy).then_inc(q_hi, 1)

            def p_qkcopy(u, b):
                wait(act, q_qk, u + 1)
                to = qk_all[:, bass.ds(u, 1), :, :].rearrange("p o x n -> p (o x) n")
                f = float(HD) ** -0.5
                wait(act, q_cv, 2 * (u - 1))
                act.activation(q0_raw[b], pQ[b][0:HD, 0, 0:2 * P], ACT.Copy).then_inc(q_qe, 1)
                act.activation(to[0:HD, 0, :], pQ[b][0:HD, 0, 0:2 * P], ACT.Identity, bias=conv_c[:, 3:4], scale=conv_c[:, 1:2]).then_inc(q_qe, 1)
                act.activation(to[HD:P, 0, :], pQ[b][HD:P, 0, 0:2 * P], ACT.Copy).then_inc(q_qe, 1)
                act.activation(to[:, 1, :], pQ[b][:, 0, 2 * P:4 * P], ACT.Copy, scale=f).then_inc(q_qe, 1)
                act.activation(to[0:HD, 2, :], pQ[b][0:HD, 1, 0:2 * P], ACT.Copy).then_inc(q_qe, 1)
                act.activation(to[0:HD, 3, :], pQ[b][HD:P, 1, 0:2 * P], ACT.Copy, scale=f).then_inc(q_qe, 1)

            def p_vgcopy(u, b):
                wait(act, q_vg, u + 1)
                wait(act, q_gp, u - 1)
                vg = pV[b][:, 0:2 * (C + G1)].rearrange("p (a n) -> p a n", a=2)
                act.activation(p_rl[b][:], vg[:, :, C:C + G1], ACT.Relu).then_inc(q_rl, 1)
                for a in range(2):
                    act.activation(v_all[:, bass.ds((2 * u + a) * E, E), 0:HD], vg[:, a, 0:C].rearrange("p (e d) -> p e d", e=E), ACT.Copy).then_inc(q_vc, 1)

            def stages2(s, b, on):
                if on(1):
                    p_hi(s - 1, 1 - b)
                if on(2):
                    p_qkcopy(s - 2, b)
                    p_vgcopy(s - 2, b)

            act.wait_ge(s_w2, 16 * 17)
            steps(act, stages2, U, 3)

            def gate_exp():
                act.wait_ge(q_gd, 3)
                act.activation(g_ex[:], g_df[:], ACT.Exp).then_inc(q_ga, 1)

            def gate_exp_again():
                act.wait_ge(q_gd, 6)
                act.activation(g_eg[:], g_g[:], ACT.Exp).then_inc(q_ga, 1)

            def p_exp(u, b, e):
                wait(act, q_nm, 3 * u + e + 1)
                wait(act, q_pT, 2 * (u - 1))
                act.activation(p_ex[b][:, 2 * e, :], pS[e][:, 0:P], ACT.Exp, bias=p_nm[b][:, e, 0:1])
                act.activation(p_ex[b][:, 2 * e + 1, :], pS[e][:, P:2 * P], ACT.Exp, bias=p_nm[b][:, e, 1:2]).then_inc(q_ex, 1)

            def p_ptcopy(u, b):
                wait(act, q_pT, 2 * u + 1)
                wait(act, q_pv, u - 1)
                act.activation(p_pt[b][:, 0:3, :].rearrange("p a n -> p (a n)"), pP[0][:, 0:3 * P], ACT.Copy).then_inc(q_pa, 1)

            def p_ytcopy(u, b):
                wait(act, q_yT, u + 1)
                wait(act, q_pr, u - 1)
                act.activation(p_yt[b].rearrange("p a n -> p (a n)"), pY[:], ACT.Copy).then_inc(q_yt, 1)

            def stages3(s, b, on):
                if isinstance(s, int) and s == 0:
                    gate_exp()
                if on(0):
                    p_exp(s, b, 0)
                if on(2):
                    p_ytcopy(s - 2, b)
                if on(0):
                    p_exp(s, b, 1)
                if on(1):
                    p_ptcopy(s - 1, 1 - b)
                if on(0):
                    p_exp(s, b, 2)
                if isinstance(s, int) and s == 0:
                    gate_exp_again()

            steps(act, stages3, U, 2)

        @block.vector
        def _(dve):
            dve.memset(wi_f[:, 1, :], 0.0).then_inc(s_zero, 1)
            dve.memset(w2_f[:, 1, :], 0.0).then_inc(s_zero, 1)
            dve.memset(wo_f[:, 1, :], 0.0)
            dve.memset(wp_f[:, 1, :], 0.0)
            dve.memset(hs_col[:], 1.0).then_inc(s_zero, 1)
            dve.memset(eps[:, 0:2], 1e-5)
            dve.memset(eps[:, 2:3], 1e-12)
            dve.memset(minus_half[:], -0.5).then_inc(s_zero, 1)
            dve.memset(keep_in[:], 1.0).then_inc(s_id, 1)
            dve.wait_ge(s_pc, 3)
            dve.tensor_copy(ident_h[:], ident[:]).then_inc(s_id, 1)
            dve.tensor_copy(ident_b[:], ident[:]).then_inc(s_id, 1)
            for b in range(2):
                dve.memset(qks[b][:].rearrange("p h x -> p (h x)").bitcast(U32), 0)
                dve.memset(nmx[b][:].bitcast(U32), 0)
            dve.memset(mm_own[:], MASK_K).then_inc(s_zero, 1)
            dve.memset(mm_sel[:], 0.0).then_inc(s_zero, 1)
            dve.memset(causal[:], 0.0).then_inc(s_zero, 1)
            for b in range(2):
                for tile in (xn[b], oa[b]):
                    dve.memset(tile[:, C:C + 1], 1.0)
                    dve.memset(tile[:, C + 1:2 * P], 0.0)
                for tile in (p_xn[b], p_y[b]):
                    dve.memset(tile[:, :, C:C + 1], 1.0)
                    dve.memset(tile[:, :, C + 1:2 * P], 0.0)
                dve.memset(vaug[b][:, 0:H, D:DA], 1.0)
                dve.memset(vaug[b][:, H:H + WIDE - 1, :], 0.0)
                dve.memset(v_all[:, b * L * E // 2:(b + 1) * L * E // 2, HD:HD + 1], 1.0).then_inc(s_one, 1)
            dve.wait_ge(s_own, 1)
            dve.wait_ge(s_zero, 7)

            def mask_columns():
                for b in range(2):
                    for h0_, f in ((0, MASK_Q), (H, MASK_K)):
                        dve.tensor_scalar(qks[b][:, h0_:h0_ + H, 3 * D:3 * D + NPOS],
                                          own_pos[:].unsqueeze(1).broadcast_to([P, H, NPOS]), f, None, ALU.mult).then_inc(s_qm, 1)
                    dve.memset(qks[b][:, 0:H, 3 * D + NPOS:3 * D + NPOS + 1], -MASK_Q).then_inc(s_qm, 1)
                    dve.memset(qks[b][:, H:2 * H, 3 * D + NPOS:3 * D + NPOS + 1], MASK_K).then_inc(s_qm, 1)
                    for p in range(2):
                        o = 64 * p + J
                        dve.tensor_scalar(nmx[b][:, o:o + NPOS], own_pos[:], MASK_Q, None, ALU.mult).then_inc(s_qm, 1)
                        dve.memset(nmx[b][:, o + NPOS:o + NPOS + 1], -MASK_Q).then_inc(s_qm, 1)

            mask_columns()
            dve.wait_ge(s_tabs, 64)
            dve.tensor_tensor(type_diff[:], type_tab[:, 1, :], type_tab[:, 0, :], ALU.subtract).then_inc(s_tb, 1)
            dve.tensor_tensor(pos_tab0[:], pos_tab[:], type_tab[:, 0, :], ALU.add).then_inc(s_tb, 1)
            dve.tensor_copy(type_f[:], ids_t[:]).then_inc(s_tb, 1)
            dve.wait_ge(s_tb, 2)
            dve.tensor_copy(pos_parts[:, 0, :], pos_tab0[:]).then_inc(s_pp, 1)
            dve.wait_ge(s_pp, 1)
            dve.tensor_tensor(pos_rest[:, 0, :], pos_tab0[:], pos_parts[:, 0, :], ALU.subtract).then_inc(s_pp, 1)
            dve.wait_ge(s_pp, 2)
            dve.tensor_copy(pos_parts[:, 1, :], pos_rest[:, 0, :]).then_inc(s_pp, 1)
            dve.wait_ge(s_pp, 3)
            dve.tensor_tensor(pos_parts[:, 2, :], pos_rest[:, 0, :], pos_parts[:, 1, :], ALU.subtract).then_inc(s_pp, 1)

            def early_setup():
                dve.wait_ge(s_misc, 16 * 3)
                dve.tensor_scalar(lscale_min[:], lscale[:], LOG_SCALE_MAX, None, ALU.min).then_inc(s_qsc, 1)
                dve.memset(qk_scale[:, H:2 * H], KEY_SCALE).then_inc(s_qsc, 1)
                dve.wait_ge(s_wh, 1)
                dve.tensor_tensor(wi_lo[:], wi_f[:], wi_hi[:].bitcast(F32), ALU.subtract).then_inc(s_wl, 1)

            def mask_sums():
                dve.wait_ge(s_mm, 8)
                dve.tensor_tensor(mm_sum[:], mm_own[:, 0, :], mm_own[:, 1, :], ALU.add).then_inc(s_mm, 1)
                dve.wait_ge(s_mm, 9)
                dve.tensor_tensor(mm_lhs[:], mm_sel[:], mm_sum[:].unsqueeze(1).broadcast_to([P, J, P]), ALU.add).then_inc(s_mm, 1)

            def late_setup():
                dve.wait_ge(s_wop, 16 * 8)
                for c in range(2):
                    dve.tensor_scalar(wo_s[:, c, :], wo_f[:, c, :], hs_col[:, c:c + 1], None, ALU.mult).then_inc(s_ws, 1)

            def w2_setup():
                dve.wait_ge(s_w2h, 1)
                dve.tensor_tensor(w2_lo[:], w2_f[:], w2_hi[:].bitcast(F32), ALU.subtract).then_inc(s_w2l, 1)

            def build_onehot(t, b):
                wait(dve, s_pos, t - 1)
                dve.tensor_scalar(onehot[b][:], pos_row_i[:, bass.ts(t, P)], iota_p[:, 0:1], None, ALU.is_equal).then_inc(s_oh, 1)

            def embed(t, b):
                if isinstance(t, int) and t < LO:
                    dve.wait_ge(s_word[t], 16)
                if not isinstance(t, int) or t >= 1:
                    wait(dve, s_nd, 2 * (t - 1) + 1)
                dve.scalar_tensor_tensor(emb_a[b][:], type_diff[:], type_f[:, bass.ds(t, 1)],
                                         word[:, bass.ds(t, 1), :].rearrange("p a c -> p (a c)"), ALU.mult, ALU.add).then_inc(s_e1, 1)
                if not isinstance(t, int) or t >= 1:
                    stats2_end(t - 1, 1 - b)

            def embed_rows(t, b):
                wait(dve, s_e1, 4 * t + 1)
                wait(dve, s_pos, t + 1)
                dve.tensor_tensor(emb_b[b][:], emb_a[b][:], psA[:, 0:C], ALU.add).then_inc(s_e1, 1)
                wait(dve, s_e1, 4 * t + 2)
                dve.bn_stats(st1[b][:], emb_b[b][:]).then_inc(s_e1, 1)

            def embed_end(t, b):
                if isinstance(t, int):
                    wait(dve, s_e1, 4 * t + 3)
                dve.bn_aggr(mv1[b][:], st1[b][:]).then_inc(s_e1, 1)

            def centre(t, b):
                wait(dve, s_e1, 4 * t + 4)
                dve.scalar_tensor_tensor(nrg[b][:], emb_b[b][:], mv1[b][:, 0:1], gamma_b[:], ALU.subtract, ALU.mult).then_inc(s_aff, 1)

            def normalise(t, b):
                wait(dve, s_ln1, 2 * t + 2)
                wait(dve, s_aff, 2 * t + 1)
                dve.scalar_tensor_tensor(h0[:, bass.ds(t, 1), :].rearrange("p a c -> p (a c)"), nrg[b][:], rs1[b][:, 0:1], beta_b[:],
                                         ALU.mult, ALU.add).then_inc(s_aff, 1)

            def stats2_waits(t):
                wait(dve, s_aff, 2 * t + 2)
                wait(dve, s_ln2, 2 * t - 2)

            def stats2(t, b):
                if isinstance(t, int):
                    stats2_waits(t)
                dve.bn_stats(st2[b][:], h0[:, bass.ds(t, 1), :].rearrange("p a c -> p (a c)")).then_inc(s_nd, 1)

            def stats2_end(t, b):
                if isinstance(t, int):
                    wait(dve, s_nd, 2 * t + 1)
                dve.bn_aggr(mv2[b][:], st2[b][:]).then_inc(s_nd, 1)

            def normalise2(t, b, more=None):
                if more:
                    more()
                wait(dve, s_ln2, 2 * t + 2)
                wait(dve, s_xT, t - 1)
                dve.tensor_scalar(xn[b][:, 0:C], h0[:, bass.ds(t, 1), :].rearrange("p a c -> p (a c)"), mv2[b][:, 0:1], rs2[b][:, 0:1],
                                  ALU.subtract, ALU.mult).then_inc(s_xn, 1)

            def x_lo(t, b):
                wait(dve, s_hi, t + 1)
                dve.tensor_tensor(xt_lo[b][:].rearrange("p a n -> p (a n)"), psA[:, 2 * P:4 * P],
                                  xt_hi[b][:].bitcast(F32).rearrange("p a n -> p (a n)"), ALU.subtract).then_inc(s_lo, 1)

            def square_sums(t, b):
                wait(dve, s_sq, t + 1)
                dve.tensor_reduce(ssq[b][:], sq[b][:].rearrange("p (h d) -> p h d", d=D), AX.X, ALU.add).then_inc(s_ss, 1)
                wait(dve, s_ss, 2 * t + 1)
                dve.tensor_scalar(ssc[b][:], ssq[b][:], 1e-24, None, ALU.max).then_inc(s_ss, 1)

            def units(t, b):
                wait(dve, s_rn, 2 * t + 2)
                wait(dve, s_ul, 2 * (t - 1))
                dve.tensor_tensor(unit[b][:].rearrange("p (h d) -> p h d", d=D), qkf[b][:].rearrange("p (h d) -> p h d", d=D),
                                  rnk[b][:].unsqueeze(2).broadcast_to([P, 2 * H, D]), ALU.mult).then_inc(s_unit, 1)

            def augment_v(t, b):
                wait(dve, s_v, t + 1)
                wait(dve, s_pv, 3 * (t - 1))
                dve.tensor_copy(vaug[b][:, 0:H, 0:D], vnew[b][:].rearrange("p (h d) -> p h d", d=D)).then_inc(s_va, 1)

            def maxima(t, b, g):
                wait(dve, s_sc, 3 * t + g + 1)
                wait(dve, s_mT, t - 1)
                dst = nmx[b][:].rearrange("q (p x) -> q p x", p=2)[:, :, 2 * g:2 * g + 2]
                dve.tensor_reduce(dst, psS[:, :, 0:2 * P].rearrange("q p (j c) -> q p j c", j=2), AX.X, ALU.max,
                                  negate=True).then_inc(s_mx, 1)

            def attn_out(t, b):
                wait(dve, s_pv, 3 * t + 3)
                dve.reciprocal(rsum[b][:].unsqueeze(2), pvo[:, :, D:DA]).then_inc(s_rc, 1)
                wait(dve, s_rc, t + 1)
                wait(dve, s_oT, t - 1)
                dve.tensor_tensor(oa[b][:, 0:C].rearrange("p (h d) -> p h d", d=D), pvo[:, :, 0:D],
                                  rsum[b][:].unsqueeze(2).broadcast_to([P, H, D]), ALU.mult).then_inc(s_oa, 1)

            def residual(t, b):
                wait(dve, s_pr, t + 1)
                if not isinstance(t, int) or t >= 2:
                    wait(dve, s_st1[b], (t - b) * 8)
                dve.tensor_tensor(h1t[b][:], psA[:, 0:C], h0[:, bass.ds(t, 1), :].rearrange("p a c -> p (a c)"), ALU.add).then_inc(s_h1, 1)

            dve.wait_ge(s_pc, 1)
            dve.wait_ge(s_misc, 16 * 3)

            def stages(s, b, on):
                if on(0):
                    if on(1):
                        stats2_waits(s - 1)
                    build_onehot(s, b)
                if on(1):
                    stats2(s - 1, 1 - b)
                if on(0):
                    embed(s, b)
                elif on(1):
                    stats2_end(s - 1, 1 - b)
                if on(2):
                    square_sums(s - 2, b)
                if on(6):
                    residual(s - 6, b)
                if on(3):
                    units(s - 3, 1 - b)
                if on(4):
                    maxima(s - 4, b, 0)
                if on(0):
                    embed_rows(s, b)
                if on(1):
                    normalise2(s - 1, 1 - b, (lambda: wait(dve, s_e1, 4 * s + 3)) if on(0) else None)
                filling = isinstance(s, int) and s < LAST - 1
                if on(0):
                    embed_end(s, b)
                    if filling:
                        centre(s, b)
                        normalise(s, b)
                if on(4):
                    maxima(s - 4, b, 1)
                if on(1):
                    x_lo(s - 1, 1 - b)
                if on(5):
                    attn_out(s - 5, 1 - b)
                if on(4):
                    maxima(s - 4, b, 2)
                if on(3):
                    augment_v(s - 3, 1 - b)
                if on(0) and not filling:
                    centre(s, b)
                    normalise(s, b)
                if isinstance(s, int):
                    if s == 0:
                        early_setup()
                    if s == 3:
                        mask_sums()
                        late_setup()
                    if s == T + 1:
                        w2_setup()

            steps(dve, stages, T, LAST, lambda: dve.wait_ge(s_word[LO], 16 * (T - LO)))

            def p_stats(u, b):
                for a in range(2):
                    dve.bn_stats(p_st[b][:, a, :], hb[:, bass.ds(2 * u + a, 1), :].rearrange("p a c -> p (a c)")).then_inc(q_st, 1)

            def p_stats_end(u, b):
                for a in range(2):
                    if isinstance(u, int):
                        wait(dve, q_st, 4 * u + 1 + a)
                    dve.bn_aggr(p_mv[b][:, a, :], p_st[b][:, a, :]).then_inc(q_st, 1)

            def p_norm(u, b):
                wait(dve, q_rs, 2 * u + 2)
                wait(dve, q_xT, u - 1)
                for a in range(2):
                    dve.tensor_scalar(p_xn[b][:, a, 0:C], hb[:, bass.ds(2 * u + a, 1), :].rearrange("p a c -> p (a c)"), p_mv[b][:, a, 0:1],
                                      p_rs[b][:, a:a + 1], ALU.subtract, ALU.mult).then_inc(q_xn, 1)

            def p_lo(u, b):
                wait(dve, q_hi, u + 1)
                dve.tensor_tensor(p_xl[b][:].rearrange("p a n -> p (a n)"), pX[b][:],
                                  p_xh[b][:].bitcast(F32).rearrange("p a n -> p (a n)"), ALU.subtract).then_inc(q_lo, 1)

            def p_conv(u, b):
                q0 = q0_raw[b].rearrange("p (a n) -> p a n", a=2)
                c = qk_all[0:HD, bass.ds(u, 1), 0, :].rearrange("p o (a n) -> p (o a) n", a=2)
                wait(dve, q_qe, 6 * u + 2)
                dve.scalar_tensor_tensor(c[:, :, 1:P], q0[:, :, 0:P - 1], conv_c[:, 0:1], c[:, :, 1:P], ALU.mult, ALU.add).then_inc(q_cv, 1)
                wait(dve, q_cv, 2 * u + 1)
                dve.scalar_tensor_tensor(c[:, :, 0:P - 1], q0[:, :, 1:P], conv_c[:, 2:3], c[:, :, 0:P - 1], ALU.mult, ALU.add).then_inc(q_cv, 1)

            def p_logits(u, b):
                wait(dve, q_gp, u + 1)
                dve.tensor_reduce(g_lg[:, bass.ds(2 * E * u, 2 * E)], p_rw[b][:].rearrange("p a e g -> p (a e) g"), AX.X, ALU.add).then_inc(q_lg, 1)

            def stages2(s, b, on):
                if on(0):
                    p_stats(s, b)
                if on(3):
                    if on(0):
                        wait(dve, q_st, 4 * s + 2)
                    p_logits(s - 3, 1 - b)
                if on(0):
                    p_stats_end(s, b)
                if on(1):
                    p_lo(s - 1, 1 - b)
                if on(0):
                    p_norm(s, b)
                if on(2):
                    p_conv(s - 2, b)

            dve.wait_ge(q_early, 16)
            dve.wait_ge(q_late, 32)
            steps(dve, stages2, U, 3)

            def three(x):
                return x.rearrange("p (a e) -> p a e", e=E)

            def bc(x):
                return x.unsqueeze(2).broadcast_to([P, L, E])

            def gate_softmax():
                dve.wait_ge(q_lg, U)
                dve.tensor_tensor(three(g_lb[:]), three(g_lg[:]), bg2_b[:].unsqueeze(1).broadcast_to([P, L, E]), ALU.add).then_inc(q_gd, 1)
                dve.wait_ge(q_gd, 1)
                dve.tensor_reduce(g_nm[:], three(g_lb[:]), AX.X, ALU.max, negate=True).then_inc(q_gd, 1)
                dve.wait_ge(q_gd, 2)
                dve.tensor_tensor(three(g_df[:]), three(g_lb[:]), bc(g_nm[:]), ALU.add).then_inc(q_gd, 1)

            def gate_probs():
                dve.wait_ge(q_ga, 1)
                dve.tensor_reduce(g_sm[:], three(g_ex[:]), AX.X, ALU.add).then_inc(q_gd, 1)
                dve.wait_ge(q_gd, 4)
                dve.reciprocal(g_rs[:], g_sm[:]).then_inc(q_gd, 1)
                dve.wait_ge(q_gd, 5)
                dve.tensor_tensor(three(g_g[:]), three(g_ex[:]), bc(g_rs[:]), ALU.mult).then_inc(q_gd, 1)

            def gate_keep():
                g3 = three(g_g[:])
                dve.wait_ge(q_gd, 6)
                dve.tensor_tensor(g_mn[:], g3[:, :, 1:3], g3[:, :, 0:2], ALU.min).then_inc(q_gd, 1)
                dve.wait_ge(q_gd, 7)
                dve.tensor_tensor(g_kp[:, :, 0:1], g3[:, :, 0:1], g_mn[:, :, 1:2], ALU.is_ge).then_inc(q_gd, 1)
                dve.tensor_tensor(g_kp[:, :, 2:3], g3[:, :, 2:3], g_mn[:, :, 0:1], ALU.is_gt).then_inc(q_gd, 1)
                dve.wait_ge(q_gd, 9)
                dve.tensor_tensor(g_ks[:].unsqueeze(2), g_kp[:, :, 0:1], g_kp[:, :, 2:3], ALU.add).then_inc(q_gd, 1)
                dve.wait_ge(q_gd, 10)
                dve.tensor_scalar(g_kp[:, :, 1:2], g_ks[:].unsqueeze(2), -1.0, 2.0, ALU.mult, ALU.add).then_inc(q_gd, 1)

            def gate_weights():
                dve.wait_ge(q_gd, 11)
                dve.wait_ge(q_ga, 2)
                dve.tensor_tensor(three(g_ek[:]), three(g_eg[:]), g_kp[:], ALU.mult).then_inc(q_gd, 1)
                dve.wait_ge(q_gd, 12)
                dve.tensor_reduce(g_es[:], three(g_ek[:]), AX.X, ALU.add).then_inc(q_gd, 1)
                dve.wait_ge(q_gd, 13)
                dve.reciprocal(g_er[:], g_es[:]).then_inc(q_gd, 1)
                dve.wait_ge(q_gd, 14)
                dve.tensor_tensor(three(g_w[:]), three(g_ek[:]), bc(g_er[:]), ALU.mult).then_inc(q_gd, 1)

            def p_max(u, b, e):
                wait(dve, q_sc, 3 * u + e + 1)
                wait(dve, q_ex, 3 * (u - 1))
                dve.tensor_reduce(p_nm[b][:, e, :], pS[e].rearrange("p (a n) -> p a n", n=P), AX.X, ALU.max, negate=True).then_inc(q_nm, 1)

            def p_ptcopy(u, b):
                wait(dve, q_pT, 2 * u + 2)
                wait(dve, q_pv, u - 1)
                dve.tensor_copy(p_pt[b][:, 3:6, :].rearrange("p a n -> p (a n)"), pP[1][:, 0:3 * P]).then_inc(q_pd, 1)

            def p_outs(u, b):
                wait(dve, q_pv, u + 1)
                dve.reciprocal(p_ri[b][:].unsqueeze(2), pO[:, :, HD:HD + 1]).then_inc(q_fc, 1)
                wait(dve, q_fc, 2 * u + 1)
                if isinstance(u, int) and u == 0:
                    dve.wait_ge(q_gd, 15)
                dve.tensor_tensor(p_fc[b][:], p_ri[b][:], g_w[:, bass.ds(2 * E * u, 2 * E)], ALU.mult).then_inc(q_fc, 1)
                wait(dve, q_fc, 2 * u + 2)
                wait(dve, q_yT, u - 1)
                dve.tensor_tensor(p_y[b][:, :, 0:C].rearrange("p a (e d) -> p a e d", e=E),
                                  pO[:, :, 0:HD].rearrange("p (a e) d -> p a e d", a=2),
                                  p_fc[b][:].rearrange("p (a e) -> p a e", a=2).unsqueeze(3).broadcast_to([P, 2, E, HD]), ALU.mult).then_inc(q_y, 1)

            def p_residual(u, b):
                wait(dve, q_pr, u + 1)
                if not isinstance(u, int) or u >= 2:
                    wait(dve, s_out[b], (u - b) * 8)
                dve.tensor_tensor(p_o[b], pR.rearrange("p (a n) -> p a n", a=2), hb[:, bass.ds(2 * u, 2), :], ALU.add).then_inc(q_o, 1)

            def stages3(s, b, on):
                if on(0):
                    p_max(s, b, 0)
                if isinstance(s, int) and s == 0:
                    gate_probs()
                if on(0):
                    p_max(s, b, 1)
                if isinstance(s, int) and s == 0:
                    gate_keep()
                if on(1):
                    p_ptcopy(s - 1, 1 - b)
                if on(0):
                    p_max(s, b, 2)
                if on(2):
                    p_residual(s - 2, b)
                if isinstance(s, int) and s == 0:
                    gate_weights()
                if on(1):
                    p_outs(s - 1, 1 - b)

            gate_softmax()
            steps(dve, stages3, U, 2)

        @block.tensor
        def _(pe):
            WARM_END = {4: 10}

            def keep_warm(bank, n, width=P):
                for _ in range(n):
                    pe.matmul(bank[:, 0:width], ident_h[:], keep_in[:, 0:width], start=True, stop=True)

            pe.wait_ge(s_pc, 3)
            pe.wait_ge(s_id, 3)
            keep_warm(psT[:, 0, :], 60)
            pe.wait_ge(s_pp, 4)

            def pos_rows(t, b):
                wait(pe, s_oh, t + 1)
                wait(pe, s_h1, t - 5)
                for k in range(3):
                    m = pe.matmul(psA[:, 0:C], onehot[b][:], pos_parts[:, k, :], start=(k == 0), stop=(k == 2))
                m.then_inc(s_pos, 1)

            def x_transpose(t, b):
                wait(pe, s_xn, t + 1)
                wait(pe, s_e1, 4 * (t + 1) + 2 if not isinstance(t, int) else 4 * min(t + 1, T - 1) + 2)
                wait(pe, s_h1, t - 4)
                for c in range(2):
                    m = pe.transpose(psA[:, (c + 2) * P:(c + 3) * P], xn[b][:, c * P:(c + 1) * P], ident[:])
                m.then_inc(s_xT, 1)

            def qkv_parts(b):
                parts = [(xt_hi[b], wi_hi), (xt_hi[b], wi_lo), (xt_lo[b], wi_hi)]
                return [(x[:, c, :], w[:, c, :], k + c == 0, k == 2 and c == 1) for k, (x, w) in enumerate(parts) for c in range(2)]

            def qk_product(t, b):
                wait(pe, s_lo, t + 1)
                wait(pe, s_qc, t)
                if isinstance(t, int) and t == 0:
                    pe.wait_ge(s_wl, 1)
                    pe.wait_ge(s_one, 2)
                for x, w, first, last in qkv_parts(b):
                    m = pe.matmul(psC[:, 0:2 * C], x, w[:, 0:2 * C], start=first, stop=last)
                m.then_inc(s_qk, 1)

            def v_product(t, b):
                wait(pe, s_v, t)
                wait(pe, s_oa, t - 3)
                for x, w, first, last in qkv_parts(b):
                    m = pe.matmul(psD[:, 0:C], x, w[:, 2 * C:3 * C], start=first, stop=last)
                m.then_inc(s_qkv, 1)

            def transposes(t, b, g):
                wait(pe, s_ul, 2 * t + 2)
                wait(pe, s_qkt, 3 * t + g)
                if g == 0:
                    wait(pe, s_nmt, t)
                for i in range(4):
                    h0_ = (i // 2) * H + 4 * g + 2 * (i % 2)
                    m = pe.transpose(trb[:, i * P:(i + 1) * P], qks[b][:, h0_:h0_ + 2, :].rearrange("p h x -> p (h x)"), ident_h[:])
                m.then_inc(s_tr, 1)

            def scores(t, b, g):
                wait(pe, s_qkt, 3 * t + g + 1)
                wait(pe, s_mx, 3 * t + g)
                for j in range(2):
                    for p in range(2):
                        r = slice(64 * p, 64 * p + 64)
                        m = pe.matmul(psS[:, p, j * P:(j + 1) * P], qkt[b][r, g, j, :], qkt[b][r, g, 2 + j, :], start=True, stop=True)
                m.then_inc(s_sc, 1)

            def max_transpose(t, b):
                wait(pe, s_mx, 3 * t + 3)
                pe.transpose(mtb, nmx[b][:], ident_h[:]).then_inc(s_mT, 1)

            def scores_t(t, b, g):
                wait(pe, s_nmt, t + 1)
                wait(pe, s_ex, 3 * t + g)
                if isinstance(t, int) and t + g == 0:
                    pe.wait_ge(s_mm, 10)
                for j in range(2):
                    for p in range(2):
                        r = slice(64 * p, 64 * p + 64)
                        rs = slice(64 * p, 64 * p + 3 * D)
                        o = psT[:, p, j * P:(j + 1) * P]
                        pe.matmul(o, mm_lhs[r, 2 * g + j, :], nmt[b][r, :], start=True, stop=False)
                        m = pe.matmul(o, qkt[b][rs, g, 2 + j, :], qkt[b][rs, g, j, :], start=False, stop=True)
                m.then_inc(s_st, 1)

            def weighted(t, b, g):
                wait(pe, s_ex, 3 * t + g + 1)
                if g == 0:
                    wait(pe, s_v, t + 4 if not isinstance(t, int) else min(t + 4, T))
                    wait(pe, s_va, t + 1)
                for j in range(2):
                    for p in range(2):
                        h = 4 * g + 2 * j + p
                        m = pe.matmul(pvw[:, h:h + WIDE, :], et[b][:, 2 * g + j, p, :], vaug[b][:, h:h + WIDE, :], start=True, stop=True)
                m.then_inc(s_pv, 1)

            def out_transpose(t, b):
                wait(pe, s_oa, t + 1)
                wait(pe, s_lo, t + 5 if not isinstance(t, int) else min(t + 5, T))
                wait(pe, s_h1, t)
                for c in range(2):
                    m = pe.transpose(psA[:, (c + 2) * P:(c + 3) * P], oa[b][:, c * P:(c + 1) * P], ident[:])
                m.then_inc(s_oT, 1)

            def project(t, b):
                wait(pe, s_ot, t + 1)
                if isinstance(t, int) and t == 0:
                    pe.wait_ge(s_ws, 2)
                for c in range(2):
                    m = pe.matmul(psA[:, 0:C], ot[b][:, c, :], wo_s[:, c, :], start=(c == 0), stop=(c == 1))
                m.then_inc(s_pr, 1)

            def stages(s, b, on):
                if on(5):
                    scores_t(s - 5, 1 - b, 0)
                if on(4):
                    transposes(s - 4, b, 0)
                if on(6):
                    project(s - 6, b)
                if on(5):
                    scores_t(s - 5, 1 - b, 1)
                    weighted(s - 5, 1 - b, 0)
                if on(4):
                    scores(s - 4, b, 0)
                    transposes(s - 4, b, 1)
                if on(0):
                    pos_rows(s, b)
                if on(5):
                    scores_t(s - 5, 1 - b, 2)
                    weighted(s - 5, 1 - b, 1)
                if on(4):
                    scores(s - 4, b, 1)
                    transposes(s - 4, b, 2)
                if isinstance(s, int) and 0 < s < 5:
                    keep_warm(psT[:, 0, :], 14)
                if on(1):
                    x_transpose(s - 1, 1 - b)
                if on(5):
                    weighted(s - 5, 1 - b, 2)
                if isinstance(s, int) and 0 < s < 5:
                    keep_warm(psT[:, 0, :], 14)
                if on(1):
                    qk_product(s - 1, 1 - b)
                elif isinstance(s, int) and s > T:
                    wait(pe, s_qc, T)
                    keep_warm(psC, 12)
                if on(4):
                    scores(s - 4, b, 2)
                if on(1):
                    v_product(s - 1, 1 - b)
                if on(4):
                    max_transpose(s - 4, b)
                if isinstance(s, int) and s in WARM_END:
                    wait(pe, s_qc, s)
                    keep_warm(psC, WARM_END[s])
                if isinstance(s, int) and s > T:
                    keep_warm(psC, 6)
                if on(5):
                    out_transpose(s - 5, 1 - b)

            steps(pe, stages, T, LAST)

            keep_warm(psC, 30, 4 * P)

            def p_xT(u, b):
                wait(pe, q_xn, 2 * u + 2)
                if isinstance(u, int) and u == 0:
                    pe.wait_ge(s_h1, T)
                    pe.wait_ge(s_w2l, 1)
                    pe.wait_ge(s_cz, 1)
                wait(pe, q_lo, u - 1)
                for c in range(2):
                    for a in range(2):
                        o = 256 * c + P * a
                        m = pe.transpose(pX[b][:, o:o + P], p_xn[b][:, a, c * P:(c + 1) * P], ident[:])
                m.then_inc(q_xT, 1)

            def p_qkv(u, b):
                wait(pe, q_lo, u + 1)
                wait(pe, q_qe, 6 * (u - 1))
                wait(pe, q_vc, 2 * (u - 1))
                parts = [(p_xh[b], w2_hi), (p_xh[b], w2_lo), (p_xl[b], w2_hi)]
                n = len(parts) * 2
                for i in range(3):
                    o = pQ[b][:, i // 2, 256 * (i % 2):256 * (i % 2) + 256]
                    for k in range(n):
                        x, w = parts[k // 2]
                        m = pe.matmul(o, w[:, k % 2, i * P:(i + 1) * P], x[:, k % 2, :], start=(k == 0), stop=(k == n - 1))
                m.then_inc(q_qk, 1)
                for a in range(2):
                    o = pV[b][:, a * (C + G1):(a + 1) * (C + G1)]
                    for k in range(n):
                        x, w = parts[k // 2]
                        m = pe.matmul(o, x[:, k % 2, a * P:(a + 1) * P], w[:, k % 2, 2 * C:NW2], start=(k == 0), stop=(k == n - 1))
                m.then_inc(q_vg, 1)

            def stages2(s, b, on):
                if on(1):
                    p_xT(s - 1, 1 - b)
                if isinstance(s, int) and s == 1:
                    keep_warm(psC, 9, 4 * P)
                if on(2):
                    p_qkv(s - 2, b)

            steps(pe, stages2, U, 3)

            def p_scores(u, b, e):
                wait(pe, q_ex, 3 * (u - 1) + e + 1 if not isinstance(u, int) or u else 0)
                pe.matmul(pS[e], ident_b[:], causal[:].rearrange("p a n -> p (a n)"), start=True, stop=True, skip_group_check=True)
                qk = qk_all[:, bass.ds(u, 1), :, :].rearrange("p o x n -> p (o x) n")
                wait(pe, q_qs, 2 * u + (2 if e == 2 else 1))
                for a in range(2):
                    col = slice(a * P, (a + 1) * P)
                    lhs = (qs[b][0:HD, 0, col], qs[b][HD:P, 0, col], q2s[b][:, col])[e]
                    rhs = (qs[b][0:HD, 1, col], qs[b][HD:P, 1, col], qk[0:HD, 3, col])[e]
                    m = pe.matmul(pS[e][:, col], lhs, rhs, start=False, stop=True, skip_group_check=True)
                m.then_inc(q_sc, 1)

            def p_pT(u, b):
                for i in range(2 * E):
                    if i % 2 == 0:
                        wait(pe, q_ex, 3 * u + i // 2 + 1)
                    if i == 0:
                        wait(pe, q_pa, u)
                        wait(pe, q_pd, u)
                    m = pe.transpose(pP[i // 3][:, (i % 3) * P:(i % 3 + 1) * P], p_ex[b][:, i, :], ident[:])
                    if i % 3 == 2:
                        m.then_inc(q_pT, 1)

            def p_pv(u, b):
                wait(pe, q_pa, u + 1)
                wait(pe, q_pd, u + 1)
                wait(pe, q_y, u)
                for i in range(2 * E):
                    k = (i % 2) * E + i // 2
                    m = pe.matmul(pO[:, k, :], p_pt[b][:, i, :], v_all[:, bass.ds(2 * E * u + k, 1), :].rearrange("p o d -> p (o d)"), start=True, stop=True)
                m.then_inc(q_pv, 1)

            def p_yT(u, b):
                wait(pe, q_y, u + 1)
                wait(pe, q_yt, u)
                for c in range(2):
                    for a in range(2):
                        o = 256 * c + P * a
                        m = pe.transpose(pY[:, o:o + P], p_y[b][:, a, c * P:(c + 1) * P], ident[:])
                m.then_inc(q_yT, 1)

            def p_project(u, b):
                wait(pe, q_yt, u + 1)
                wait(pe, q_o, u)
                for a in range(2):
                    for c in range(2):
                        m = pe.matmul(pR[:, a * C:(a + 1) * C], p_yt[b][:, c, a * P:(a + 1) * P], wp_f[:, c, :], start=(c == 0), stop=(c == 1))
                m.then_inc(q_pr, 1)

            def stages3(s, b, on):
                if on(0):
                    p_scores(s, b, 0)
                    p_scores(s, b, 1)
                if isinstance(s, int) and s < 2:
                    keep_warm(psA, 14)
                if on(2):
                    p_yT(s - 2, b)
                if on(1):
                    p_pT(s - 1, 1 - b)
                if on(0):
                    p_scores(s, b, 2)
                if isinstance(s, int) and s == 0:
                    keep_warm(psA, 14)
                if isinstance(s, int) and s == 1:
                    keep_warm(psA, 14)
                if on(2):
                    p_project(s - 2, b)
                if on(1):
                    p_pv(s - 1, 1 - b)

            pe.wait_ge(q_lo, U)
            keep_warm(psA, 20)
            pe.wait_ge(q_cv, 2 * U)
            pe.wait_ge(q_qe, 6 * U)
            pe.wait_ge(q_vc, 2 * U)
            steps(pe, stages3, U, 2)


_INS = ['word_ids', 'type_ids', 'pos_ids', 'word_emb', 'pos_emb', 'type_emb', 'gamma', 'beta',
        'w_in', 'b_in', 'logit_scale', 'head_scale', 'w_out', 'b_out', 'w_qk', 'b_qk', 'w_v', 'b_v',
        'conv_w', 'conv_b', 'w_g1', 'b_g1', 'w_g2', 'b_g2', 'w_p', 'b_p']


def kernel(**inputs):
    import numpy as _np
    import concourse.bacc as _bacc
    from concourse import mybir as _mybir
    from concourse.bass_utils import run_bass_kernel_spmd as _run

    a = {k: _np.asarray(v) for k, v in inputs.items()}
    seqs, positions = a['x'].shape
    near = 128 // seqs

    def by_tile(ids):
        return ids.reshape(seqs, positions // near, near).transpose(1, 2, 0)

    laid = {
        'word_ids': by_tile(a['x']).reshape(-1, 128).T,
        'type_ids': by_tile(a['mask_BS_i1_0']).reshape(-1, 128).T,
        'pos_ids': by_tile(a['pos_BS']).reshape(-1),
        'word_emb': a['L0_tok_word_emb'], 'pos_emb': a['L0_tok_pos_emb'], 'type_emb': a['L0_tok_type_emb'],
        'gamma': a['L0_tok_gamma'], 'beta': a['L0_tok_beta'],
        'w_in': a['L0_attn_in_proj_weight'].T, 'b_in': a['L0_attn_in_proj_bias'],
        'logit_scale': a['L0_attn_logit_scale'], 'head_scale': a['L0_attn_head_scale'],
        'w_out': a['L0_attn_out_w'].T, 'b_out': a['L0_attn_out_b'],
    }
    hd = a['L0_ffn_Wqk'].shape[1] // 6
    order = _np.concatenate([_np.arange(hd) + hd * e for e in (0, 1, 3, 4, 2, 5)])
    laid['w_qk'] = a['L0_ffn_Wqk'][:, order]
    laid['b_qk'] = a['L0_ffn_bqk'][order]
    laid['w_g2'] = a['L0_ffn_Wg2'].T
    for name, key in (('w_v', 'Wv'), ('b_v', 'bv'), ('conv_w', 'conv_w'), ('conv_b', 'conv_b'), ('w_g1', 'Wg1'),
                      ('b_g1', 'bg1'), ('b_g2', 'bg2'), ('w_p', 'Wp'), ('b_p', 'bp')):
        laid[name] = a['L0_ffn_' + key]

    nc = _bacc.Bacc("TRN2", target_bir_lowering=False, num_devices=1)
    arrays, args = {}, []
    for name in _INS:
        x = _np.ascontiguousarray(laid[name])
        arrays[f"in_{name}"] = x
        args.append(nc.dram_tensor(f"in_{name}", x.shape, _mybir.dt.from_np(x.dtype), kind="ExternalInput").ap())
    width = a['L0_tok_word_emb'].shape[1]
    args.append(nc.dram_tensor("h_scratch", (seqs * positions, width), _mybir.dt.float32, kind="Internal").ap())
    args.append(nc.dram_tensor("out_0", (seqs, positions, width), _mybir.dt.float32, kind="ExternalOutput").ap())
    block_kernel(nc, *args)
    r = _run(nc, [arrays], core_ids=[0])
    return r.results[0]["out_0"]
```
